# Optimizing a Trainium2 kernel written in Bass

```python
import numpy as np
import jax
import jax.numpy as jnp

def _softmax(x, axis=-1):
    return jax.nn.softmax(x, axis=axis)

def _gelu(x):
    return jax.nn.gelu(x, approximate=True)

def _silu(x):
    return jax.nn.silu(x)

def _sigmoid(x):
    return jax.nn.sigmoid(x)

def _layernorm(x, axis=-1, eps=1e-05):
    m = jnp.mean(x, axis=axis, keepdims=True)
    v = jnp.var(x, axis=axis, keepdims=True)
    return (x - m) / jnp.sqrt(v + eps)

def _scatter_add(tgt, idx, src, axis=0):
    return tgt.at[idx].add(src)

def _segment_sum(src, seg, n):
    return jax.ops.segment_sum(src, seg, n)
kernel_name = 'mk_macaron_d2_jaxref_r8_0e0314'

def setup_inputs(seed: int=0):
    np.random.seed(seed)
    _w = jnp.asarray

    def _L0_attn_setup():
        import jax, jax.numpy as jnp
        import numpy as np
        B, T, D = (8, 256, 128)

        def rmsnorm(x, gamma):
            n = jnp.maximum(jnp.linalg.norm(x, axis=-1, keepdims=True), 1e-12)
            return x / n * D ** 0.5 * (gamma + 1.0)

        def lru_cell_pointwise(x_in, hidden, Wi, Wif, Whf, bhf):
            ni = jnp.tanh(x_in @ Wi.T)
            g = jax.nn.sigmoid(hidden @ Whf.T + bhf + x_in @ Wif.T)
            return hidden + g * (jnp.tanh(ni) - hidden)

        def lru_layer(x, Wi, Wif, Whf, bhf, h0):
            ni = jnp.tanh(jnp.einsum('btd,hd->bth', x, Wi))
            fi = jnp.einsum('btd,hd->bth', x, Wif)
            h_init = jnp.broadcast_to(h0, (x.shape[0], h0.shape[0]))

            def step(h, inp):
                ni_t, fi_t = inp
                g = jax.nn.sigmoid(h @ Whf.T + bhf + fi_t)
                h_next = h + g * (jnp.tanh(ni_t) - h)
                return (h_next, h_next)
            _, hs = jax.lax.scan(step, h_init, (ni.transpose(1, 0, 2), fi.transpose(1, 0, 2)))
            return hs.transpose(1, 0, 2)
        key = jax.random.key(seed)
        ks = jax.random.split(key, 8)
        s = 1.0 / np.sqrt(D)
        return {'x': jax.random.normal(ks[0], (B, T, D), jnp.float32), 'gamma': jnp.zeros((D,), jnp.float32), 'gWi': jax.random.normal(ks[1], (D, D), jnp.float32) * s, 'gWif': jax.random.normal(ks[2], (D, D), jnp.float32) * s, 'gWhf': jax.random.normal(ks[3], (D, D), jnp.float32) * s, 'gbhf': jnp.zeros((D,), jnp.float32), 'lWi': jax.random.normal(ks[4], (2, D, D), jnp.float32) * s, 'lWif': jax.random.normal(ks[5], (2, D, D), jnp.float32) * s, 'lWhf': jax.random.normal(ks[6], (2, D, D), jnp.float32) * s, 'lbhf': jnp.zeros((2, D), jnp.float32), 'l_init_hidden': jnp.zeros((2, D), jnp.float32)}
    _L0_attn_in = _L0_attn_setup()

    def _L0_ffn_setup():
        import jax, jax.numpy as jnp
        import numpy as np
        import math
        E = 16
        TOP_K = 2
        D = 128
        F = 512
        SH = 256
        key = jax.random.key(seed)
        ks = jax.random.split(key, 10)
        s = lambda k, shape, fan: jax.random.normal(k, shape, jnp.float32) / np.sqrt(fan)
        return {'x': jax.random.normal(ks[0], (32, 32, D), jnp.float32), 'gate_w': s(ks[1], (E, D), D), 'up_w': s(ks[2], (E, F, D), D), 'up_b': s(ks[3], (E, F), D), 'gw': s(ks[4], (E, F, D), D), 'gb': s(ks[5], (E, F), D), 'down_w': s(ks[6], (E, D, F), F), 'down_b': s(ks[7], (E, D), F), 'sh_gate_w': s(ks[8], (SH, D), D), 'sh_up_w': s(ks[9], (SH, D), D), 'sh_down_w': s(jax.random.fold_in(key, 11), (D, SH), SH)}
    _L0_ffn_in = _L0_ffn_setup()

    def _L1_attn_setup():
        import jax, jax.numpy as jnp
        import numpy as np
        import math
        B, T, D, H = (4, 256, 128, 16)
        HD = D // H
        ROPE_BASE = 10000.0

        def apply_rope(x):
            t, hd = (x.shape[2], x.shape[3])
            half = hd // 2
            theta = 1.0 / ROPE_BASE ** (jnp.arange(0, hd, 2, dtype=jnp.float32) / hd)
            pos = jnp.arange(1, t + 1, dtype=jnp.float32)
            ang = pos[:, None] * theta[None, :]
            ang = jnp.concatenate([ang, ang], axis=-1)
            sin, cos = (jnp.sin(ang), jnp.cos(ang))
            rot = jnp.concatenate([-x[..., half:], x[..., :half]], axis=-1)
            return x * cos[None, None, :, :] + rot * sin[None, None, :, :]
        key = jax.random.key(seed)
        ks = jax.random.split(key, 9)
        s = 1.0 / math.sqrt(D)
        return {'x': jax.random.normal(ks[0], (B, T, D), dtype=jnp.float32), 'Wq': jax.random.normal(ks[1], (D, D), dtype=jnp.float32) * s, 'bq': jax.random.normal(ks[2], (D,), dtype=jnp.float32) * 0.01, 'Wk': jax.random.normal(ks[3], (D, D), dtype=jnp.float32) * s, 'bk': jax.random.normal(ks[4], (D,), dtype=jnp.float32) * 0.01, 'Wv': jax.random.normal(ks[5], (D, D), dtype=jnp.float32) * s, 'bv': jax.random.normal(ks[6], (D,), dtype=jnp.float32) * 0.01, 'Wo': jax.random.normal(ks[7], (D, D), dtype=jnp.float32) * s, 'bo': jax.random.normal(ks[8], (D,), dtype=jnp.float32) * 0.01}
    _L1_attn_in = _L1_attn_setup()

    def _L1_ffn_setup():
        import jax, jax.numpy as jnp
        import numpy as np
        H = 128
        I = 256
        E = 8
        B, S = (2, 128)

        def _swiglu(x, wg, wu, wd):
            return jax.nn.silu(x @ wg) * (x @ wu) @ wd
        key = jax.random.key(seed)
        ks = jax.random.split(key, 8)
        sc_h = 1.0 / np.sqrt(H)
        sc_i = 1.0 / np.sqrt(I)
        return {'hidden_states': jax.random.normal(ks[0], (B, S, H), jnp.float32), 'gate_w': jax.random.normal(ks[1], (H, E), jnp.float32) * sc_h, 'sh_gate': jax.random.normal(ks[2], (H, I), jnp.float32) * sc_h, 'sh_up': jax.random.normal(ks[3], (H, I), jnp.float32) * sc_h, 'sh_down': jax.random.normal(ks[4], (I, H), jnp.float32) * sc_i, 'rt_gate': jax.random.normal(ks[5], (E, H, I), jnp.float32) * sc_h, 'rt_up': jax.random.normal(ks[6], (E, H, I), jnp.float32) * sc_h, 'rt_down': jax.random.normal(ks[7], (E, I, H), jnp.float32) * sc_i}
    _L1_ffn_in = _L1_ffn_setup()
    _d = {'L0_attn_x': _L0_attn_in['x'], 'L0_attn_gamma': _L0_attn_in['gamma'], 'L0_attn_gWi': _L0_attn_in['gWi'], 'L0_attn_gWif': _L0_attn_in['gWif'], 'L0_attn_gWhf': _L0_attn_in['gWhf'], 'L0_attn_gbhf': _L0_attn_in['gbhf'], 'L0_attn_lWi': _L0_attn_in['lWi'], 'L0_attn_lWif': _L0_attn_in['lWif'], 'L0_attn_lWhf': _L0_attn_in['lWhf'], 'L0_attn_lbhf': _L0_attn_in['lbhf'], 'L0_attn_l_init_hidden': _L0_attn_in['l_init_hidden'], 'L0_ffn_gate_w': _L0_ffn_in['gate_w'], 'L0_ffn_up_w': _L0_ffn_in['up_w'], 'L0_ffn_up_b': _L0_ffn_in['up_b'], 'L0_ffn_gw': _L0_ffn_in['gw'], 'L0_ffn_gb': _L0_ffn_in['gb'], 'L0_ffn_down_w': _L0_ffn_in['down_w'], 'L0_ffn_down_b': _L0_ffn_in['down_b'], 'L0_ffn_sh_gate_w': _L0_ffn_in['sh_gate_w'], 'L0_ffn_sh_up_w': _L0_ffn_in['sh_up_w'], 'L0_ffn_sh_down_w': _L0_ffn_in['sh_down_w'], 'L1_attn_Wq': _L1_attn_in['Wq'], 'L1_attn_bq': _L1_attn_in['bq'], 'L1_attn_Wk': _L1_attn_in['Wk'], 'L1_attn_bk': _L1_attn_in['bk'], 'L1_attn_Wv': _L1_attn_in['Wv'], 'L1_attn_bv': _L1_attn_in['bv'], 'L1_attn_Wo': _L1_attn_in['Wo'], 'L1_attn_bo': _L1_attn_in['bo'], 'L1_ffn_gate_w': _L1_ffn_in['gate_w'], 'L1_ffn_sh_gate': _L1_ffn_in['sh_gate'], 'L1_ffn_sh_up': _L1_ffn_in['sh_up'], 'L1_ffn_sh_down': _L1_ffn_in['sh_down'], 'L1_ffn_rt_gate': _L1_ffn_in['rt_gate'], 'L1_ffn_rt_up': _L1_ffn_in['rt_up'], 'L1_ffn_rt_down': _L1_ffn_in['rt_down']}
    _x0 = _d['L0_attn_x']
    _d['L0_attn_x'] = jax.random.normal(jax.random.fold_in(jax.random.key(seed), 1), (4, 512, 128), dtype=_x0.dtype)
    del _x0
    return _d

def reference(L0_attn_x, L0_attn_gamma, L0_attn_gWi, L0_attn_gWif, L0_attn_gWhf, L0_attn_gbhf, L0_attn_lWi, L0_attn_lWif, L0_attn_lWhf, L0_attn_lbhf, L0_attn_l_init_hidden, L0_ffn_gate_w, L0_ffn_up_w, L0_ffn_up_b, L0_ffn_gw, L0_ffn_gb, L0_ffn_down_w, L0_ffn_down_b, L0_ffn_sh_gate_w, L0_ffn_sh_up_w, L0_ffn_sh_down_w, L1_attn_Wq, L1_attn_bq, L1_attn_Wk, L1_attn_bk, L1_attn_Wv, L1_attn_bv, L1_attn_Wo, L1_attn_bo, L1_ffn_gate_w, L1_ffn_sh_gate, L1_ffn_sh_up, L1_ffn_sh_down, L1_ffn_rt_gate, L1_ffn_rt_up, L1_ffn_rt_down):

    def _L0_attn_ref(x, gamma, gWi, gWif, gWhf, gbhf, lWi, lWif, lWhf, lbhf, l_init_hidden):
        import jax, jax.numpy as jnp
        import numpy as np
        B, T, D = (8, 256, 128)

        def rmsnorm(x, gamma):
            n = jnp.maximum(jnp.linalg.norm(x, axis=-1, keepdims=True), 1e-12)
            return x / n * D ** 0.5 * (gamma + 1.0)

        def lru_cell_pointwise(x_in, hidden, Wi, Wif, Whf, bhf):
            ni = jnp.tanh(x_in @ Wi.T)
            g = jax.nn.sigmoid(hidden @ Whf.T + bhf + x_in @ Wif.T)
            return hidden + g * (jnp.tanh(ni) - hidden)

        def lru_layer(x, Wi, Wif, Whf, bhf, h0):
            ni = jnp.tanh(jnp.einsum('btd,hd->bth', x, Wi))
            fi = jnp.einsum('btd,hd->bth', x, Wif)
            h_init = jnp.broadcast_to(h0, (x.shape[0], h0.shape[0]))

            def step(h, inp):
                ni_t, fi_t = inp
                g = jax.nn.sigmoid(h @ Whf.T + bhf + fi_t)
                h_next = h + g * (jnp.tanh(ni_t) - h)
                return (h_next, h_next)
            _, hs = jax.lax.scan(step, h_init, (ni.transpose(1, 0, 2), fi.transpose(1, 0, 2)))
            return hs.transpose(1, 0, 2)
        xn = rmsnorm(x, gamma)
        h = xn
        for i in range(2):
            h = lru_layer(h, lWi[i], lWif[i], lWhf[i], lbhf[i], l_init_hidden[i])
        y = lru_cell_pointwise(h, xn, gWi, gWif, gWhf, gbhf)
        return y + x

    def _L0_ffn_ref(x, gate_w, up_w, up_b, gw, gb, down_w, down_b, sh_gate_w, sh_up_w, sh_down_w):
        import jax, jax.numpy as jnp
        import numpy as np
        import math
        E = 16
        TOP_K = 2
        D = 128
        F = 512
        SH = 256
        B, S, Dm = x.shape
        h = x.reshape(-1, Dm)
        T = h.shape[0]
        scores = jax.nn.sigmoid(h @ gate_w.T)
        cap = math.ceil(T / E * TOP_K)
        topk_score, topk_ids = jax.lax.top_k(scores.T, cap)
        xin = h[topk_ids]
        up = jnp.einsum('ecd,efd->ecf', xin, up_w) + up_b[:, None, :]
        g = jnp.einsum('ecd,efd->ecf', xin, gw) + gb[:, None, :]
        eo = jax.nn.silu(g) * up
        eo = jnp.einsum('ecf,edf->ecd', eo, down_w) + down_b[:, None, :]
        flat = (eo * topk_score[..., None]).reshape(-1, Dm)
        out = jnp.zeros_like(h).at[topk_ids.reshape(-1)].add(flat)
        out = out.reshape(B, S, Dm)
        shared = jax.nn.silu(jnp.einsum('bsd,fd->bsf', x, sh_gate_w)) * jnp.einsum('bsd,fd->bsf', x, sh_up_w)
        shared = jnp.einsum('bsf,df->bsd', shared, sh_down_w)
        return out + shared

    def _L1_attn_ref(x, Wq, bq, Wk, bk, Wv, bv, Wo, bo):
        import jax, jax.numpy as jnp
        import numpy as np
        import math
        B, T, D, H = (4, 256, 128, 16)
        HD = D // H
        ROPE_BASE = 10000.0

        def apply_rope(x):
            t, hd = (x.shape[2], x.shape[3])
            half = hd // 2
            theta = 1.0 / ROPE_BASE ** (jnp.arange(0, hd, 2, dtype=jnp.float32) / hd)
            pos = jnp.arange(1, t + 1, dtype=jnp.float32)
            ang = pos[:, None] * theta[None, :]
            ang = jnp.concatenate([ang, ang], axis=-1)
            sin, cos = (jnp.sin(ang), jnp.cos(ang))
            rot = jnp.concatenate([-x[..., half:], x[..., :half]], axis=-1)
            return x * cos[None, None, :, :] + rot * sin[None, None, :, :]
        b, t, d = x.shape
        h, hd = (H, HD)
        q = x @ Wq.T + bq
        k = x @ Wk.T + bk
        v = x @ Wv.T + bv
        split = lambda z: z.reshape(b, t, h, hd).transpose(0, 2, 1, 3)
        q, k, v = (split(q), split(k), split(v))
        q = apply_rope(q)
        k = apply_rope(k)
        scale = math.sqrt(hd)
        att = jnp.einsum('bhqd,bhkd->bhqk', q, k) / scale
        mask = jnp.tril(jnp.ones((t, t), dtype=bool))
        att = jnp.where(mask[None, None, :, :], att, -jnp.inf)
        att = jax.nn.softmax(att, axis=-1)
        y = jnp.einsum('bhqk,bhkd->bhqd', att, v)
        y = y.transpose(0, 2, 1, 3).reshape(b, t, d)
        y = y @ Wo.T + bo
        return y

    def _L1_ffn_ref(hidden_states, gate_w, sh_gate, sh_up, sh_down, rt_gate, rt_up, rt_down):
        import jax, jax.numpy as jnp
        import numpy as np
        H = 128
        I = 256
        E = 8
        B, S = (2, 128)

        def _swiglu(x, wg, wu, wd):
            return jax.nn.silu(x @ wg) * (x @ wu) @ wd
        b, s, h = hidden_states.shape
        x = hidden_states.reshape(-1, h)
        logits = x @ gate_w
        top_val = jnp.max(logits, axis=-1, keepdims=True)
        top_id = jnp.argmax(logits, axis=-1)
        score = jax.nn.sigmoid(top_val)
        xs = x * score
        g = jnp.einsum('th,ehi->eti', xs, rt_gate)
        u = jnp.einsum('th,ehi->eti', xs, rt_up)
        act = jax.nn.silu(g) * u
        y = jnp.einsum('eti,eih->eth', act, rt_down)
        onehot = jax.nn.one_hot(top_id, E, dtype=x.dtype)
        routed = jnp.einsum('eth,te->th', y, onehot)
        shared = _swiglu(x, sh_gate, sh_up, sh_down)
        return (shared + routed).reshape(b, s, h)
    x = L0_attn_x
    x = x + 0.5 * _L0_ffn_ref(_layernorm(x, axis=-1), L0_ffn_gate_w, L0_ffn_up_w, L0_ffn_up_b, L0_ffn_gw, L0_ffn_gb, L0_ffn_down_w, L0_ffn_down_b, L0_ffn_sh_gate_w, L0_ffn_sh_up_w, L0_ffn_sh_down_w)
    x = x + _L0_attn_ref(_layernorm(x, axis=-1), L0_attn_gamma, L0_attn_gWi, L0_attn_gWif, L0_attn_gWhf, L0_attn_gbhf, L0_attn_lWi, L0_attn_lWif, L0_attn_lWhf, L0_attn_lbhf, L0_attn_l_init_hidden)
    x = x + 0.5 * _L0_ffn_ref(_layernorm(x, axis=-1), L0_ffn_gate_w, L0_ffn_up_w, L0_ffn_up_b, L0_ffn_gw, L0_ffn_gb, L0_ffn_down_w, L0_ffn_down_b, L0_ffn_sh_gate_w, L0_ffn_sh_up_w, L0_ffn_sh_down_w)
    x = x + 0.5 * _L1_ffn_ref(_layernorm(x, axis=-1), L1_ffn_gate_w, L1_ffn_sh_gate, L1_ffn_sh_up, L1_ffn_sh_down, L1_ffn_rt_gate, L1_ffn_rt_up, L1_ffn_rt_down)
    x = x + _L1_attn_ref(_layernorm(x, axis=-1), L1_attn_Wq, L1_attn_bq, L1_attn_Wk, L1_attn_bk, L1_attn_Wv, L1_attn_bv, L1_attn_Wo, L1_attn_bo)
    x = x + 0.5 * _L1_ffn_ref(_layernorm(x, axis=-1), L1_ffn_gate_w, L1_ffn_sh_gate, L1_ffn_sh_up, L1_ffn_sh_down, L1_ffn_rt_gate, L1_ffn_rt_up, L1_ffn_rt_down)
    return x

_drawn_inputs = setup_inputs


def setup_inputs(seed=0):
    import zlib

    import numpy as np

    out = dict(_drawn_inputs(seed))
    spreads = {'L0_attn_gamma': (0.0, 0.1),
     'L0_attn_gbhf': (0.0, 0.415),
     'L0_attn_lbhf': (0.0, 0.8),
     'L0_attn_l_init_hidden': (0.0, 2.0)}
    factors = {'L0_attn_lWhf': 3.36,
     'L1_attn_bq': 64.0,
     'L1_attn_bk': 64.0,
     'L1_attn_bv': 8.0,
     'L1_attn_bo': 8.0}
    for name, (base, spread) in spreads.items():
        noise = np.random.default_rng([zlib.crc32(name.encode()), seed]).standard_normal(out[name].shape)
        drawn = base * np.exp(spread * noise) if base else spread * noise
        out[name] = jnp.asarray(drawn.astype(out[name].dtype))
    for name, factor in factors.items():
        out[name] = (out[name] * factor).astype(out[name].dtype)
    return out
```

```python
from contextlib import ExitStack, contextmanager

import numpy as np

import concourse.bass as bass
from concourse import mybir

ALU = mybir.AluOpType
ACT = mybir.ActivationFunctionType
AX = mybir.AxisListType
F32 = mybir.dt.float32
F16 = mybir.dt.float16
U32 = mybir.dt.uint32

P = 128
D = 128
B, T = 4, 512
N = B * T
NT = N // P
LN_EPS = 1e-5

E0, F0, SH0 = 16, 512, 256
CAP = N // E0 * 2
SEG = P // E0
SEGLEN = N // SEG
F0T = F0 // P
HROW = D + E0
SCORE_BITS = 30


class Serial:

    def __init__(self, engine, sem):
        self.engine, self.sem, self.done = engine, sem, 0

    def step(self, instruction):
        instruction.then_inc(self.sem, 1)
        self.done += 1
        self.engine.wait_ge(self.sem, self.done)

    def mark(self, instruction):
        instruction.then_inc(self.sem, 1)
        self.done += 1

    def settle(self):
        self.engine.wait_ge(self.sem, self.done)


def pass_waits(core, pool):
    pool.sem_inc(core.waits_passed, 1)


class Core:

    def __init__(self, nc, dram):
        self.nc, self.dram, self.keep = nc, dram, ExitStack()
        self.made = 0
        self.to_clear = []

    def sbuf(self, name, shape, dtype=F32, ctx=None):
        self.made += 1
        return (ctx or self.keep).enter_context(self.nc.sbuf_tensor(f"{name}_{self.made}", shape, dtype))

    def psum(self, name, shape, ctx, dtype=F32):
        self.made += 1
        return ctx.enter_context(self.nc.psum_tensor(f"{name}_{self.made}", shape, dtype))

    def sem(self, name, ctx=None):
        self.made += 1
        sem = (ctx or self.keep).enter_context(self.nc.semaphore(f"{name}_{self.made}"))
        if ctx is not None:
            self.to_clear.append(sem.num)
        return sem

    @contextmanager
    def stage(self):
        outer, self.to_clear = self.to_clear, []
        with ExitStack() as ctx:
            yield ctx
            numbers = sorted(self.to_clear)
            runs = []
            for n in numbers:
                if runs and runs[-1].stop == n:
                    runs[-1] = range(runs[-1].start, n + 1)
                else:
                    runs.append(range(n, n + 1))
            if runs:
                with self.nc.Block() as block:

                    @block.gpsimd
                    def _(pool):
                        for run in runs:
                            pool.sem_clear(run)

        self.to_clear = outer


def setup(core):
    nc, dram = core.nc, core.dram
    core.x = core.sbuf("x", [P, NT, D])
    core.h = core.sbuf("h", [P, NT, D])
    core.ht = core.sbuf("ht", [P, N])
    core.ident = core.sbuf("ident", [P, P])
    core.ident16 = core.sbuf("ident16", [P, P], F16)
    core.eps = core.sbuf("eps", [P, 1])
    core.x_loaded = core.sem("x_loaded")
    core.tables_loaded = core.sem("tables_loaded")
    core.gate_loaded = core.sem("gate_loaded")
    core.waits_passed = core.sem("waits_passed")

    small = {}

    def table(name, shape, dtype=F32):
        small[name] = core.sbuf(name, shape, dtype)

    table("same_block", [P, P], F16)
    table("earlier_segment", [P, P], F16)
    table("earlier_token", [P, P], F16)
    table("ones16", [P, P], F16)
    table("slot_numbers", [P, CAP], F16)
    table("token_ids", [P, NT], F16)
    table("bit_masks", [P, SCORE_BITS], U32)
    table("bit_values", [P, SCORE_BITS])
    table("ones_row", [1, P])
    table("l0_sh_gate", [P, SH0])
    table("l0_sh_up", [P, SH0])
    table("l0_sh_down", [P, SH0 // P, D])
    table("l0_gate_bias", [P, E0 * F0T])
    table("l0_up_bias", [P, E0 * F0T])
    table("l0_down_bias", [1, E0 * D])
    for name in ("lru_wi", "lru_wif", "lru_whf"):
        table(name, [P, 2, P])
    for name in ("cell_wi", "cell_wif", "cell_whf"):
        table(name, [P, P])
    table("lru_bhf", [1, 2 * P])
    table("cell_bhf", [P, 1])
    table("lru_gamma", [P, 1])
    table("lru_init", [P, 2 * B])
    table("l1_gate", [P, E1])
    table("l1_sh_gate", [P, F1])
    table("l1_sh_up", [P, F1])
    table("l1_sh_down", [P, F1T, D])
    table("expert_ranks", [P, NT, E1])
    table("same_expert", [P, E1 * NT])
    table("ones8", [P, E1])
    table("tile_numbers", [P, ETILES, E1])
    table("partition", [P, 1])
    for name in ("att_q", "att_q_partner", "att_k", "att_k_partner", "att_v", "att_o"):
        table(name, [P, P])
    table("att_bias", [P, 4])
    table("att_bv", [1, D])
    table("att_bo", [1, D])
    table("rope_cos", [P, T])
    table("rope_sin", [P, T])
    table("ident_bf16", [P, P], BF16)
    table("causal", [P, P], BF16)
    for kind in ("q", "k"):
        for part in ("hi", "lo"):
            table(f"spread_{kind}_{part}", [P, GROUPS * P], F16)
    core.tables = small
    core.gate_spread = core.sbuf("gate_spread", [P, SEG, P])

    with core.stage() as ctx:
        gate = core.sbuf("gate", [P, E0], ctx=ctx)
        zeros = core.sbuf("zeros", [P, ETILES * D], ctx=ctx)
        cleared = core.sem("cleared")
        zeroed = core.sem("zeroed", ctx)
        spread = core.sem("spread", ctx)
        x_tiled = dram["x"].rearrange("(t p) d -> p t d", p=P)
        with nc.Block() as block:

            @block.sync
            def _(sp):
                sp.dma_start(core.x[:], x_tiled).then_inc(core.x_loaded, 16)
                sp.dma_start(gate[:], dram["l0_gate"]).then_inc(core.gate_loaded, 16)
                sp.dma_start(core.ident[:], dram["ident"]).then_inc(core.tables_loaded, 16)
                sp.dma_start(core.ident16[:], dram["ident16"]).then_inc(core.tables_loaded, 16)
                for name, tensor in small.items():
                    sp.dma_start(tensor[:], dram[name]).then_inc(core.tables_loaded, 16)
                sp.wait_ge(core.x_loaded, 16)
                sp.wait_ge(core.tables_loaded, 16 * (len(small) + 2))

            @block.gpsimd
            def _(pool):
                nc.gpsimd.memset(core.gate_spread[:], 0.0).then_inc(zeroed, 1)
                nc.gpsimd.memset(zeros[:], 0.0).then_inc(zeroed, 1)
                pool.wait_ge(zeroed, 2)
                pool.dma_start(dram["sorted"].rearrange("(p t) d -> p (t d)", p=P), zeros[:]).then_inc(cleared, 16)
                pool.wait_ge(cleared, 16)

            @block.vector
            def _(dve):
                dve.wait_ge(zeroed, 2)
                dve.wait_ge(core.gate_loaded, 16)
                for s in range(SEG):
                    nc.vector.tensor_copy(core.gate_spread[:, s, s:P:SEG], gate[:]).then_inc(spread, 1)


def layer_norm(core):
    nc, x, h, ht = core.nc, core.x, core.h, core.ht
    with core.stage() as ctx:
        stats = core.sbuf("stats", [P, NT, 6], ctx=ctx)
        mean_var = core.sbuf("mean_var", [P, NT, 2], ctx=ctx)
        var = core.sbuf("var", [P, NT], ctx=ctx)
        std = core.sbuf("std", [P, NT], ctx=ctx)
        rstd = core.sbuf("rstd", [P, NT], ctx=ctx)
        turned = core.psum("turned", [P, 4, 512], ctx)
        dve_chain = core.sem("ln_chain", ctx)
        var_ready = core.sem("var_ready", ctx)
        std_ready = core.sem("std_ready", ctx)
        h_ready = core.sem("h_ready", ctx)
        turned_ready = core.sem("turned_ready", ctx)
        with nc.Block() as block:

            @block.vector
            def _(dve):
                chain = Serial(dve, dve_chain)
                for t in range(NT):
                    chain.mark(nc.vector.bn_stats(stats[:, t, :], x[:, t, :]))
                chain.settle()
                for t in range(NT):
                    chain.mark(nc.vector.bn_aggr(mean_var[:, t, :], stats[:, t, :]))
                chain.settle()
                nc.vector.tensor_scalar(var[:], mean_var[:, :, 1], LN_EPS, None, ALU.add).then_inc(var_ready, 1)
                dve.wait_ge(std_ready, 1)
                chain.step(nc.vector.reciprocal(rstd[:], std[:]))
                for t in range(NT):
                    nc.vector.tensor_scalar(h[:, t, :], x[:, t, :], mean_var[:, t, 0:1], rstd[:, t:t + 1],
                                            ALU.subtract, ALU.mult).then_inc(h_ready, 1)

            @block.tensor
            def _(pe):
                for t in range(NT):
                    pe.wait_ge(h_ready, t + 1)
                    pe.transpose(turned[:, t // 4, t % 4 * P:(t % 4 + 1) * P], h[:, t, :],
                                 core.ident[:]).then_inc(turned_ready, 1)

            @block.scalar
            def _(act):
                act.wait_ge(var_ready, 1)
                nc.scalar.activation(std[:], var[:], ACT.Sqrt).then_inc(std_ready, 1)
                for g in range(4):
                    act.wait_ge(turned_ready, 4 * g + 4)
                    nc.scalar.activation(ht[:, 512 * g:512 * (g + 1)], turned[:, g, :], ACT.Copy)


def route_and_shared0(core, select):
    nc, dram, tb = core.nc, core.dram, core.tables
    K = SH0 // P
    BLK = 4
    with core.stage() as ctx:
        score = core.sbuf("score", [P, SEGLEN], ctx=ctx)
        over = core.sbuf("over", [P, SEGLEN], ctx=ctx)
        equal = core.sbuf("equal", [P, SEGLEN], ctx=ctx)
        count_eq = core.sbuf("count_eq", [P, SEGLEN], ctx=ctx)
        fits = core.sbuf("fits", [P, SEGLEN], ctx=ctx)
        taken_eq = core.sbuf("taken_eq", [P, SEGLEN], ctx=ctx)
        taken = core.sbuf("taken", [P, SEGLEN], ctx=ctx)
        count_taken = core.sbuf("count_taken", [P, SEGLEN], ctx=ctx)
        slot = core.sbuf("slot", [P, SEGLEN], ctx=ctx)
        ones = core.sbuf("ones", [P, SEGLEN], ctx=ctx)
        cand = core.sbuf("cand", [P, 2], U32, ctx=ctx)
        least = core.sbuf("least", [P, 2], U32, ctx=ctx)
        kept_bit = core.sbuf("kept_bit", [P, 1], U32, ctx=ctx)
        part_count = core.sbuf("part_count", [P, 1], F16, ctx=ctx)
        part_sum = core.sbuf("part_sum", [P, 2], F16, ctx=ctx)
        need = core.sbuf("need", [P, 1], ctx=ctx)
        offset = core.sbuf("offset", [P, 2], ctx=ctx)
        half_score = core.sbuf("half_score", [P, NT, E0], ctx=ctx)
        silu = core.sbuf("silu", [P, 2, 512], ctx=ctx)
        act = core.sbuf("act", [P, 2, K, 512], ctx=ctx)
        x_next = core.sbuf("x_next", [P, NT, D], ctx=ctx)

        ps_score = core.psum("ps_score", [P, 512], ctx)
        ps_count = core.psum("ps_count", [P, 512], ctx)
        ps_turn = core.psum("ps_turn", [P, 4, P], ctx)
        ps_gu = core.psum("ps_gu", [P, 2, 2, 512], ctx)
        ps_down = core.psum("ps_down", [P, 4, P], ctx)

        scores_summed = core.sem("scores_summed", ctx)
        score_ready = core.sem("score_ready", ctx)
        chain_sem = core.sem("route_chain", ctx)
        counted = core.sem("counted", ctx)
        totalled = core.sem("totalled", ctx)
        turned = core.sem("turned", ctx)
        table_ready = core.sem("table_ready", ctx)
        gate_done = core.sem("gate_done", ctx)
        up_done = core.sem("up_done", ctx)
        silu_done = core.sem("silu_done", ctx)
        act_done = core.sem("act_done", ctx)
        down_done = core.sem("down_done", ctx)
        next_ready = core.sem("next_ready", ctx)
        stored = core.sem("stored", ctx)

        rounds = []
        for blk in range(BLK):
            for k in range(K):
                rounds += [("gate", blk, k), ("up", blk, k)]
                if k == 0 and blk:
                    rounds.append(("down", blk - 1, 0))
        rounds.append(("down", BLK - 1, 0))
        assert len(rounds) <= SCORE_BITS

        with nc.Block() as block:

            @block.tensor
            def _(pe):
                for s in range(SEG):
                    mm = pe.matmul(ps_score[:, 0:SEGLEN], core.gate_spread[:, s, :],
                                   core.ht[:, s * SEGLEN:(s + 1) * SEGLEN], start=(s == 0), stop=(s == SEG - 1))
                mm.then_inc(scores_summed, 1)

                def shared(what, blk, k):
                    n = blk * K + k
                    if what == "gate":
                        if n >= 2:
                            pe.wait_ge(act_done, n - 1)
                        pe.matmul(ps_gu[:, n % 2, 0, :], tb["l0_sh_gate"][:, k * P:(k + 1) * P],
                                  core.ht[:, blk * 512:(blk + 1) * 512], start=True, stop=True).then_inc(gate_done, 1)
                    elif what == "up":
                        pe.matmul(ps_gu[:, n % 2, 1, :], tb["l0_sh_up"][:, k * P:(k + 1) * P],
                                  core.ht[:, blk * 512:(blk + 1) * 512], start=True, stop=True).then_inc(up_done, 1)
                    else:
                        pe.wait_ge(act_done, K * (blk + 1))
                        if blk:
                            pe.wait_ge(next_ready, blk)
                        for t in range(4):
                            for j in range(K):
                                mm = pe.matmul(ps_down[:, t, :], act[:, blk % 2, j, t * P:(t + 1) * P],
                                               tb["l0_sh_down"][:, j, :], start=(j == 0), stop=(j == K - 1))
                        mm.then_inc(down_done, 1)

                for r in range(SCORE_BITS):
                    pe.wait_ge(counted, r + 1)
                    pe.matmul(ps_count[:, 0:1], tb["same_block"][:], part_count[:], start=True,
                              stop=True).then_inc(totalled, 1)
                    if r < len(rounds):
                        shared(*rounds[r])
                pe.wait_ge(counted, SCORE_BITS + 1)
                pe.matmul(ps_count[:, 0:1], tb["same_block"][:], part_count[:], start=True,
                          stop=True).then_inc(totalled, 1)
                for j in range(2):
                    pe.wait_ge(counted, SCORE_BITS + 2 + j)
                    pe.matmul(ps_count[:, 1 + j:2 + j], tb["earlier_segment"][:], part_sum[:, j:j + 1],
                              start=True, stop=True).then_inc(totalled, 1)
                for j in range(2):
                    pe.transpose(ps_turn[:, 2 + j, :], score[:, j * P:(j + 1) * P], core.ident[:])
                pe.wait_ge(counted, SCORE_BITS + 4)
                for j in range(2):
                    mm = pe.transpose(ps_turn[:, j, :], slot[:, j * P:(j + 1) * P], core.ident[:])
                mm.then_inc(turned, 1)

            @block.scalar
            def _(act_e):
                nc.scalar.preload_act_table_set("sigmoid_and_others")
                act_e.wait_ge(scores_summed, 1)
                nc.scalar.activation(score[:], ps_score[:, 0:SEGLEN], ACT.Sigmoid).then_inc(score_ready, 1)
                nc.scalar.preload_act_table_set("silu_and_others")
                for n in range(BLK * K):
                    act_e.wait_ge(gate_done, n + 1)
                    if n >= 2:
                        act_e.wait_ge(act_done, n - 1)
                    nc.scalar.activation(silu[:, n % 2, :], ps_gu[:, n % 2, 0, :], ACT.Silu).then_inc(silu_done, 1)

            @block.vector
            def _(dve):
                chain = Serial(dve, chain_sem)
                chain.mark(nc.vector.memset(ones[:], 1.0))
                chain.mark(nc.vector.memset(least[:], 0))
                chain.mark(nc.vector.tensor_copy(cand[:, 0:1], tb["bit_masks"][:, 0:1]))
                chain.settle()
                dve.wait_ge(score_ready, 1)

                def shared(what, blk, k):
                    n = blk * K + k
                    if what == "up":
                        dve.wait_ge(silu_done, n + 1)
                        dve.wait_ge(up_done, n + 1)
                        if blk >= 2:
                            dve.wait_ge(down_done, blk - 1)
                        nc.vector.tensor_tensor(act[:, blk % 2, k, :], silu[:, n % 2, :], ps_gu[:, n % 2, 1, :],
                                                ALU.mult).then_inc(act_done, 1)
                    elif what == "down":
                        dve.wait_ge(down_done, blk + 1)
                        nc.vector.scalar_tensor_tensor(
                            out=x_next[:, 4 * blk:4 * blk + 4, :], in0=ps_down[:], scalar=0.5,
                            in1=core.x[:, 4 * blk:4 * blk + 4, :], op0=ALU.mult, op1=ALU.add).then_inc(next_ready, 1)

                for r in range(SCORE_BITS):
                    now, nxt = r % 2, (r + 1) % 2
                    nc.vector.tensor_scalar(over[:], score[:], cand[:, now:now + 1].bitcast(F32), None, ALU.is_ge,
                                            ALU.add, accum_out=part_count[:]).then_inc(counted, 1)
                    if 1 <= r <= len(rounds):
                        shared(*rounds[r - 1])
                    dve.wait_ge(totalled, r + 1)
                    chain.step(nc.vector.tensor_scalar(kept_bit[:], ps_count[:, 0:1], float(CAP),
                                                       tb["bit_values"][:, r:r + 1], ALU.is_ge, ALU.mult))
                    if r + 1 < SCORE_BITS:
                        chain.mark(nc.vector.scalar_tensor_tensor(
                            out=cand[:, nxt:nxt + 1], in0=kept_bit[:], scalar=tb["bit_masks"][:, r + 1:r + 2],
                            in1=least[:, now:now + 1], op0=ALU.bitwise_or, op1=ALU.bitwise_or))
                    chain.step(nc.vector.tensor_tensor(least[:, nxt:nxt + 1], least[:, now:now + 1], kept_bit[:],
                                                       ALU.bitwise_or))
                bound = least[:, SCORE_BITS % 2:SCORE_BITS % 2 + 1].bitcast(F32)

                nc.vector.tensor_scalar(over[:], score[:], bound, None, ALU.is_gt, ALU.add,
                                        accum_out=part_count[:]).then_inc(counted, 1)
                chain.step(nc.vector.tensor_scalar(equal[:], score[:], bound, None, ALU.is_equal))
                chain.step(nc.vector.tensor_tensor_scan(count_eq[:], ones[:], equal[:], 0.0, ALU.mult, ALU.add))
                nc.vector.tensor_copy(part_sum[:, 0:1], count_eq[:, SEGLEN - 1:SEGLEN]).then_inc(counted, 1)
                dve.wait_ge(totalled, SCORE_BITS + 2)
                chain.mark(nc.vector.tensor_scalar(need[:], ps_count[:, 0:1], -1.0, float(CAP), ALU.mult, ALU.add))
                chain.mark(nc.vector.tensor_copy(offset[:, 0:1], ps_count[:, 1:2]))
                chain.settle()
                chain.step(nc.vector.tensor_scalar(fits[:], count_eq[:], offset[:, 0:1], need[:], ALU.add, ALU.is_le))
                chain.step(nc.vector.tensor_tensor(taken_eq[:], equal[:], fits[:], ALU.mult))
                dve.wait_ge(counted, SCORE_BITS + 1)
                chain.step(nc.vector.tensor_tensor(taken[:], taken_eq[:], over[:], ALU.add))
                chain.step(nc.vector.tensor_tensor_scan(count_taken[:], ones[:], taken[:], 0.0, ALU.mult, ALU.add))
                nc.vector.tensor_copy(part_sum[:, 1:2], count_taken[:, SEGLEN - 1:SEGLEN]).then_inc(counted, 1)
                dve.wait_ge(totalled, SCORE_BITS + 3)
                chain.step(nc.vector.tensor_copy(offset[:, 1:2], ps_count[:, 2:3]))
                nc.vector.scalar_tensor_tensor(out=slot[:], in0=count_taken[:], scalar=offset[:, 1:2], in1=taken[:],
                                               op0=ALU.add, op1=ALU.mult).then_inc(counted, 1)
                dve.wait_ge(turned, 1)
                nc.vector.tensor_copy(select[:], ps_turn[:, 0:2, :]).then_inc(chain_sem, 1)
                for j in range(2):
                    nc.vector.tensor_scalar(
                        half_score[:, j:NT:2, :].rearrange("p s e -> p e s"),
                        ps_turn[:, 2 + j, :].rearrange("p (e s) -> p e s", s=SEG),
                        0.5, None, ALU.mult).then_inc(table_ready, 1)

            @block.sync
            def _(sp):
                rows = dram["rows"].rearrange("(t p) r -> p t r", p=P)
                sp.dma_start(rows[:, :, 0:D], core.h[:]).then_inc(stored, 16)
                sp.wait_ge(next_ready, BLK)
                sp.dma_start(dram["sum"].rearrange("(t p) d -> p t d", p=P), x_next[:]).then_inc(stored, 16)
                sp.wait_ge(table_ready, 2)
                sp.dma_start(rows[:, :, D:HROW], half_score[:]).then_inc(stored, 16)
                sp.wait_ge(stored, 48)


def experts0(core, select):
    nc, dram, tb = core.nc, core.dram, core.tables
    CH = CAP // P
    with core.stage() as ctx:
        onehot = core.sbuf("onehot", [P, 2, NT, CAP], F16, ctx=ctx)
        ids = core.sbuf("ids", [P, 2, CH], U32, ctx=ctx)
        rows = core.sbuf("rows", [P, 2, CH, HROW], ctx=ctx)
        xt = core.sbuf("xt", [P, 2, CAP], ctx=ctx)
        w_up = core.sbuf("w_up", [P, 2, F0], ctx=ctx)
        w_gate = core.sbuf("w_gate", [P, 2, F0], ctx=ctx)
        w_down = core.sbuf("w_down", [P, 2, F0T, D], ctx=ctx)
        silu = core.sbuf("silu", [P, 2, CAP], ctx=ctx)
        hidden = core.sbuf("hidden", [P, 2, F0T, CAP], ctx=ctx)
        result = core.sbuf("result", [P, 2, CH, D], ctx=ctx)
        ps_ids = core.psum("ps_ids", [P, 512], ctx)
        ps_xt = core.psum("ps_xt", [P, 512], ctx)
        ps_gu = core.psum("ps_gu", [P, 2, 2, 512], ctx)
        ps_down = core.psum("ps_down", [P, 2, 4, P], ctx)

        onehot_ready = core.sem("onehot_ready", ctx)
        ids_summed = core.sem("ids_summed", ctx)
        ids_ready = core.sem("ids_ready", ctx)
        gathered = [core.sem("gathered"), core.sem("gathered")]
        scattered = [core.sem("scattered"), core.sem("scattered")]
        weights_loaded = [core.sem("weights_loaded", ctx), core.sem("weights_loaded", ctx)]
        xt_turned = core.sem("xt_turned", ctx)
        xt_ready = core.sem("xt_ready", ctx)
        gate_done = core.sem("gate_done", ctx)
        up_done = core.sem("up_done", ctx)
        silu_done = core.sem("silu_done", ctx)
        hidden_done = core.sem("hidden_done", ctx)
        down_done = core.sem("down_done", ctx)
        result_done = core.sem("result_done", ctx)
        x_loaded = core.sem("x_loaded", ctx)

        def later(i):
            return not isinstance(i, int) or i > 0

        def each_expert(engine, body):
            for k in range(2):
                body(k, 0, k, True)
            with engine.Fori(1, E0 // 2 - 1) as pair:
                for k in range(2):
                    body(2 * pair + k, pair, k, True)
            last = E0 // 2 - 1
            for k in range(2):
                body(2 * last + k, last, k, k == 0)

        with nc.Block() as block:

            @block.sync
            def _(sp):
                def load(e, k):
                    one = slice(e, e + 1) if isinstance(e, int) else bass.ds(e, 1)
                    for dst, name in ((w_up[:, k, :], "l0_up"), (w_gate[:, k, :], "l0_gate_proj"),
                                      (w_down[:, k].rearrange("p f d -> p (f d)"), "l0_down")):
                        sp.dma_start(dst, dram[name][one].rearrange("o p f -> (o p) f")
                                     ).then_inc(weights_loaded[k], 16)

                for k in range(2):
                    load(k, k)
                with sp.Fori(1, E0 // 2) as pair:
                    for k in range(2):
                        sp.wait_ge(down_done, 2 * pair + k - 1)
                        load(2 * pair + k, k)
                for k in range(2):
                    sp.wait_ge(scattered[k], 32 * (E0 // 2))
                sp.dma_start(core.x[:], dram["sum"].rearrange("(t p) d -> p t d", p=P)).then_inc(x_loaded, 16)
                sp.wait_ge(x_loaded, 16)

            @block.vector
            def _(dve):
                def onehots(e, k):
                    dve.wait_ge(ids_summed, e + 1)
                    for t in range(NT):
                        col = t % 2 * P + t // 2
                        at = e * SEG + col
                        one = slice(at, at + 1) if isinstance(at, int) else bass.ds(at, 1)
                        last = nc.vector.tensor_scalar(onehot[:, k, t, :], tb["slot_numbers"][:],
                                                       select_flat[:, one], None, ALU.is_equal)
                    last.then_inc(onehot_ready, 1)

                def take_ids(e, pair, k):
                    dve.wait_ge(ids_summed, e + 3)
                    if later(pair):
                        dve.wait_ge(scattered[k], 32 * pair)
                    nc.vector.tensor_copy(ids[:, k, :], ps_ids[:, 0:CH]).then_inc(ids_ready, 1)

                select_flat = select[:].rearrange("p j c -> p (j c)")
                dve.sem_inc(hidden_done, 2)
                onehots(0, 0)
                take_ids(0, 0, 0)

                def expert(e, pair, k, has_next):
                    if has_next:
                        onehots(e + 1, 1 - k)
                    for f in range(F0T):
                        at = e * F0T + f
                        one = slice(at, at + 1) if isinstance(at, int) else bass.ds(at, 1)
                        dve.wait_ge(silu_done, e * F0T + f + 1)
                        dve.wait_ge(up_done, e * F0T + f + 1)
                        nc.vector.scalar_tensor_tensor(
                            out=hidden[:, k, f, :], in0=ps_gu[:, f % 2, 1, 0:CAP], scalar=tb["l0_up_bias"][:, one],
                            in1=silu[:, f % 2, :], op0=ALU.add, op1=ALU.mult).then_inc(hidden_done, 1)
                        if f == 0 and has_next:
                            take_ids(e + 1, pair + k, 1 - k)

                each_expert(dve, expert)

            @block.tensor
            def _(pe):
                def sum_ids(e, k):
                    pe.wait_ge(onehot_ready, e + 1)
                    if later(e):
                        pe.wait_ge(ids_ready, e)
                    for c in range(CH):
                        for t in range(NT):
                            mm = pe.matmul(ps_ids[:, c:c + 1], onehot[:, k, t, c * P:(c + 1) * P],
                                           tb["token_ids"][:, t:t + 1], start=(t == 0), stop=(t == NT - 1))
                    mm.then_inc(ids_summed, 1)

                pe.sem_inc(ids_summed, 2)
                sum_ids(0, 0)

                def expert(e, pair, k, has_next):
                    if has_next:
                        sum_ids(e + 1, 1 - k)
                    pe.wait_ge(gathered[k], 32 * (pair + 1))
                    if later(e):
                        pe.wait_ge(xt_ready, e)
                    for c in range(CH):
                        mm = pe.transpose(ps_xt[:, c * P:(c + 1) * P], rows[:, k, c, 0:D], core.ident[:])
                    mm.then_inc(xt_turned, 1)
                    pe.wait_ge(xt_ready, e + 1)
                    pe.wait_ge(weights_loaded[k], 48 * (pair + 1))
                    for f in range(F0T):
                        pe.wait_ge(hidden_done, e * F0T + f + 1)
                        pe.matmul(ps_gu[:, f % 2, 0, 0:CAP], w_gate[:, k, f * P:(f + 1) * P], xt[:, k, :],
                                  start=True, stop=True).then_inc(gate_done, 1)
                        pe.matmul(ps_gu[:, f % 2, 1, 0:CAP], w_up[:, k, f * P:(f + 1) * P], xt[:, k, :],
                                  start=True, stop=True).then_inc(up_done, 1)
                    pe.wait_ge(result_done, e + 1)
                    pe.wait_ge(hidden_done, (e + 1) * F0T + 2)
                    at = e * D
                    bias = slice(at, at + D) if isinstance(at, int) else bass.ds(at, D)
                    for c in range(CH):
                        pe.matmul(ps_down[:, k, c, :], tb["ones_row"][:], tb["l0_down_bias"][:, bias],
                                  start=True, stop=False)
                        for f in range(F0T):
                            mm = pe.matmul(ps_down[:, k, c, :], hidden[:, k, f, c * P:(c + 1) * P],
                                           w_down[:, k, f, :], start=False, stop=(f == F0T - 1))
                    mm.then_inc(down_done, 1)

                each_expert(pe, expert)

            @block.scalar
            def _(act):
                nc.scalar.preload_act_table_set("silu_and_others")
                act.sem_inc(result_done, 2)

                def expert(e, pair, k, has_next):
                    act.wait_ge(xt_turned, e + 1)
                    nc.scalar.activation(xt[:, k, :], ps_xt[:, 0:CAP], ACT.Copy).then_inc(xt_ready, 1)
                    for f in range(F0T):
                        at = e * F0T + f
                        one = slice(at, at + 1) if isinstance(at, int) else bass.ds(at, 1)
                        act.wait_ge(gate_done, e * F0T + f + 1)
                        act.wait_ge(hidden_done, e * F0T + f + 1)
                        nc.scalar.activation(silu[:, f % 2, :], ps_gu[:, f % 2, 0, 0:CAP], ACT.Silu,
                                             bias=tb["l0_gate_bias"][:, one]).then_inc(silu_done, 1)
                    act.wait_ge(down_done, e + 1)
                    if later(pair):
                        act.wait_ge(scattered[k], 32 * pair)
                    at = e + D
                    one = slice(at, at + 1) if isinstance(at, int) else bass.ds(at, 1)
                    for c in range(CH):
                        last = nc.scalar.activation(result[:, k, c, :], ps_down[:, k, c, :], ACT.Copy,
                                                    scale=rows[:, k, c, one])
                    last.then_inc(result_done, 1)

                each_expert(act, expert)

            @block.gpsimd
            def _(pool):
                def gather(e, k):
                    pool.wait_ge(ids_ready, e + 1)
                    pool.wait_ge(result_done, e + 1)
                    pass_waits(core, pool)
                    for c in range(CH):
                        pool.indirect_dma_start(rows[:, k, c, :], None, dram["rows"],
                                                bass.IndirectOffsetOnAxis(ap=ids[:, k, c:c + 1], axis=0)
                                                ).then_inc(gathered[k], 16)

                gather(0, 0)

                def expert(e, pair, k, has_next):
                    if has_next:
                        gather(e + 1, 1 - k)
                    pool.wait_ge(result_done, e + 3)
                    if later(e):
                        pool.wait_ge(scattered[1 - k], 32 * (pair + k))
                    pass_waits(core, pool)
                    for c in range(CH):
                        pool.indirect_dma_start(dram["sum"], bass.IndirectOffsetOnAxis(ap=ids[:, k, c:c + 1], axis=0),
                                                result[:, k, c, :], None, compute_op=ALU.add
                                                ).then_inc(scattered[k], 16)

                each_expert(pool, expert)


def moe0(core):
    with core.stage() as ctx:
        select = core.sbuf("select", [P, 2, P], ctx=ctx)
        layer_norm(core)
        route_and_shared0(core, select)
        experts0(core, select)


C = 16
CHUNKS = T // C
W = C * B
LAYERS = 2
L2 = LAYERS * B
LAG = 2


def rms_norm(core, xnt):
    nc, h, tb = core.nc, core.h, core.tables
    with core.stage() as ctx:
        xn = core.sbuf("xn", [P, NT, D], ctx=ctx)
        square = core.sbuf("square", [P, NT, D], ctx=ctx)
        norm2 = core.sbuf("norm2", [P, NT], ctx=ctx)
        norm = core.sbuf("norm", [P, NT], ctx=ctx)
        bounded = core.sbuf("bounded", [P, NT], ctx=ctx)
        inverse = core.sbuf("inverse", [P, NT], ctx=ctx)
        factor = core.sbuf("factor", [P, NT], ctx=ctx)
        gamma1 = core.sbuf("gamma1", [P, 1], ctx=ctx)
        ps_turn = core.psum("ps_turn", [P, 4, 512], ctx)
        squared = core.sem("squared", ctx)
        summed = core.sem("summed", ctx)
        norm_ready = core.sem("norm_ready", ctx)
        dve_chain = core.sem("rms_chain", ctx)
        gamma_ready = core.sem("gamma_ready", ctx)
        xn_ready = core.sem("xn_ready", ctx)
        turned = core.sem("turned", ctx)
        with nc.Block() as block:

            @block.gpsimd
            def _(pool):
                nc.gpsimd.tensor_tensor(square[:], h[:], h[:], ALU.mult).then_inc(squared, 1)

            @block.scalar
            def _(act):
                act.wait_ge(summed, 1)
                nc.scalar.activation(norm[:], norm2[:], ACT.Sqrt).then_inc(norm_ready, 1)
                act.wait_ge(gamma_ready, 1)
                for g in range(4):
                    act.wait_ge(turned, 4 * g + 4)
                    nc.scalar.activation(xnt[:, g, :], ps_turn[:, g, :], ACT.Copy, scale=gamma1[:])

            @block.vector
            def _(dve):
                chain = Serial(dve, dve_chain)
                nc.vector.tensor_scalar(gamma1[:], tb["lru_gamma"][:], 1.0, None, ALU.add).then_inc(gamma_ready, 1)
                dve.wait_ge(squared, 1)
                nc.vector.tensor_reduce(norm2[:], square[:], AX.X, ALU.add).then_inc(summed, 1)
                dve.wait_ge(norm_ready, 1)
                chain.step(nc.vector.tensor_scalar(bounded[:], norm[:], 1e-12, None, ALU.max))
                chain.step(nc.vector.reciprocal(inverse[:], bounded[:]))
                chain.step(nc.vector.tensor_scalar(factor[:], inverse[:], float(np.sqrt(np.float32(D))), None, ALU.mult))
                for t in range(NT):
                    nc.vector.tensor_scalar(xn[:, t, :], h[:, t, :], factor[:, t:t + 1], None,
                                            ALU.mult).then_inc(xn_ready, 1)

            @block.tensor
            def _(pe):
                for t in range(NT):
                    pe.wait_ge(xn_ready, t + 1)
                    pe.transpose(ps_turn[:, t // 4, t % 4 * P:(t % 4 + 1) * P], xn[:, t, :],
                                 core.ident[:]).then_inc(turned, 1)


def recurrence(core, xnt, zt):
    nc, tb = core.nc, core.tables
    with core.stage() as ctx:
        whf_hi = core.sbuf("whf_hi", [P, LAYERS, P], F16, ctx=ctx)
        whf_lo = core.sbuf("whf_lo", [P, LAYERS, P], F16, ctx=ctx)
        gate = core.sbuf("gate", [P, L2], ctx=ctx)
        u = core.sbuf("u", [P, L2], ctx=ctx)
        u_hi = core.sbuf("u_hi", [P, L2], F16, ctx=ctx)
        u_lo = core.sbuf("u_lo", [P, L2], F16, ctx=ctx)
        gap = core.sbuf("gap", [P, L2], ctx=ctx)
        h_hi = core.sbuf("h_hi", [P, 2, L2], F16, ctx=ctx)
        h_lo = core.sbuf("h_lo", [P, 2, L2], F16, ctx=ctx)
        states = core.sbuf("states", [P, 2, C, L2], ctx=ctx)
        towards = core.sbuf("towards", [P, 2, C, L2], ctx=ctx)
        tanh_once = core.sbuf("tanh_once", [P, LAYERS, C, B], ctx=ctx)
        cell_once = core.sbuf("cell_once", [P, C, B], ctx=ctx)
        cell_n = core.sbuf("cell_n", [P, C, B], ctx=ctx)
        cell_g = core.sbuf("cell_g", [P, C, B], ctx=ctx)
        cell_gap = core.sbuf("cell_gap", [P, C, B], ctx=ctx)
        cell_u = core.sbuf("cell_u", [P, C, B], ctx=ctx)
        ps_gate = core.psum("ps_gate", [P, 2, 2, 512], ctx)
        ps_n = core.psum("ps_n", [P, LAYERS, 512], ctx)
        ps_cell_n = core.psum("ps_cell_n", [P, 512], ctx)
        ps_cell_g = core.psum("ps_cell_g", [P, 512], ctx)

        begun = core.sem("begun", ctx)
        split_chain = core.sem("split_chain", ctx)
        input_ready = core.sem("input_ready", ctx)
        gate_done = core.sem("gate_done", ctx)
        u_hi_done = core.sem("u_hi_done", ctx)
        u_done = core.sem("u_done", ctx)
        u_lo_done = core.sem("u_lo_done", ctx)
        state_done = core.sem("state_done", ctx)
        gap_done = core.sem("gap_done", ctx)
        h_hi_done = core.sem("h_hi_done", ctx)
        h_lo_done = core.sem("h_lo_done", ctx)
        n_done = [core.sem("n_done", ctx) for _ in range(LAYERS)]
        n_read = [core.sem("n_read", ctx) for _ in range(LAYERS)]
        towards_ready = [core.sem("towards_ready", ctx) for _ in range(LAYERS)]
        cell_n_done = core.sem("cell_n_done", ctx)
        cell_g_done = core.sem("cell_g_done", ctx)
        cell_n_read = core.sem("cell_n_read", ctx)
        cell_inputs = core.sem("cell_inputs", ctx)
        cell_chain = core.sem("cell_chain", ctx)

        def each_chunk(engine, body):
            def peeled(c):
                runs = [l for l in range(LAYERS) if 0 <= c - l * LAG < CHUNKS]
                nexts = [l for l in range(LAYERS) if 0 <= c + 1 - l * LAG < CHUNKS]
                body(c, c % 2, runs, nexts, c >= LAG + 1)

            both = list(range(LAYERS))
            for c in range(4):
                peeled(c)
            with engine.Fori(2, CHUNKS // 2 - 1) as pair:
                for k in range(2):
                    body(2 * pair + k, k, both, both, True)
            for c in range(CHUNKS - 2, CHUNKS + LAG):
                peeled(c)

        def columns(layers):
            return slice(layers[0] * B, (layers[-1] + 1) * B)

        with nc.Block() as block:

            @block.tensor
            def _(pe):
                def project_n(l, m, k, weights, rhs, out, done, read):
                    if not (isinstance(m, int) and m == 0):
                        pe.wait_ge(read, m)
                    pe.matmul(out[:, 0:W], weights, rhs, start=True, stop=True).then_inc(done, 1)

                def source(l, c, k):
                    if l == 0:
                        at = (c + 1) * C
                        at = slice(at, at + C) if isinstance(at, int) else bass.ds(at, C)
                        return xnt[:, :, at].rearrange("p b t -> p t b")
                    return states[:, 1 - k, :, 0:B]

                def source_half(l, c, k, half):
                    if l == 0:
                        at = (c + 1) * C + half
                        at = slice(at, at + C - 1, 2) if isinstance(at, int) else bass.ds(at, C // 2, step=2)
                        return xnt[:, :, at].rearrange("p b t -> p t b")
                    return states[:, 1 - k, half:C:2, 0:B]

                def gate_columns(k, half, l):
                    return ps_gate[:, k, half, 0:C // 2 * L2].rearrange("p (t c) -> p t c", c=L2)[:, :, l * B:(l + 1) * B]

                def project_gate(c, k, half, l, what, first):
                    out = gate_columns(1 - k, half, l)
                    if what == "input":
                        pe.matmul(out, tb["lru_wif"][:, l, :], source_half(l, c, k, half),
                                  start=first, stop=False, skip_group_check=True)
                    else:
                        pe.matmul(out, tb["lru_bhf"][:, l * P:(l + 1) * P], tb["ones_row"][:, 0:W // 2],
                                  start=False, stop=False, skip_group_check=True)

                def fillers(c, k, nexts, cell):
                    work = []
                    for l in nexts:
                        m = c + 1 - l * LAG
                        work.append(lambda l=l, m=m: project_n(l, m, k, tb["lru_wi"][:, l, :], source(l, c, k),
                                                               ps_n[:, l], n_done[l], n_read[l]))
                    if cell:
                        m = c - LAG - 1
                        x_at = m * C
                        x_at = slice(x_at, x_at + C) if isinstance(x_at, int) else bass.ds(x_at, C)
                        seen = states[:, 1 - k, :, B:L2]

                        def cell_gate_first():
                            if not (isinstance(m, int) and m == 0):
                                pe.wait_ge(cell_inputs, m)
                            pe.matmul(ps_cell_g[:, 0:W], tb["cell_wif"][:], seen, start=True, stop=False)

                        def cell_gate_second():
                            pe.matmul(ps_cell_g[:, 0:W], tb["cell_whf"][:], xnt[:, :, x_at].rearrange("p b t -> p t b"),
                                      start=False, stop=True).then_inc(cell_g_done, 1)

                        work.append(lambda: project_n(None, m, k, tb["cell_wi"][:], seen, ps_cell_n,
                                                      cell_n_done, cell_n_read))
                        work += [cell_gate_first, cell_gate_second]
                    for half in range(2):
                        for l in nexts:
                            for what in ("input", "bias"):
                                work.append(lambda half=half, l=l, what=what: project_gate(
                                    c, k, half, l, what, l == nexts[0] and what == "input"))
                    assert len(work) < C
                    return work

                def before_products(k, s, layers):
                    for l in layers:
                        out = ps_gate[:, k, s % 2, s // 2 * L2 + l * B:s // 2 * L2 + (l + 1) * B]
                        part = slice(l * B, (l + 1) * B)
                        pe.matmul(out, whf_hi[:, l, :], h_hi[:, s % 2, part], start=False, stop=False, skip_group_check=True)
                        pe.matmul(out, whf_lo[:, l, :], h_hi[:, s % 2, part], start=False, stop=False, skip_group_check=True)
                        pe.matmul(out, whf_hi[:, l, :], h_lo[:, s % 2, part], start=False, stop=False, skip_group_check=True)

                def iteration(c, k, runs, nexts, cell):
                    work = fillers(c, k, nexts, cell)
                    for s in range(C):
                        at = c * C + s
                        start_of_all = isinstance(at, int) and at == 0
                        out = [ps_gate[:, k, s % 2, s // 2 * L2 + l * B:s // 2 * L2 + (l + 1) * B] for l in range(LAYERS)]
                        if not start_of_all:
                            pe.wait_ge(u_hi_done, at)
                        for l in runs:
                            part = slice(l * B, (l + 1) * B)
                            pe.matmul(out[l], whf_hi[:, l, :], u_hi[:, part], start=False, stop=False, skip_group_check=True)
                            pe.matmul(out[l], whf_lo[:, l, :], u_hi[:, part], start=False, stop=False, skip_group_check=True)
                        if not start_of_all:
                            pe.wait_ge(u_lo_done, at)
                        for l in runs:
                            part = slice(l * B, (l + 1) * B)
                            mm = pe.matmul(out[l], whf_hi[:, l, :], u_lo[:, part], start=False, stop=True, skip_group_check=True)
                        mm.then_inc(input_ready, 1)
                        if s + 1 < C:
                            if not start_of_all:
                                pe.wait_ge(h_lo_done, at)
                            before_products(k, s + 1, runs)
                            if s < len(work):
                                work[s]()
                        elif nexts:
                            pe.wait_ge(h_lo_done, at)
                            before_products(1 - k, 0, nexts)

                pe.wait_ge(begun, 1)
                project_n(0, 0, 0, tb["lru_wi"][:, 0, :], source(0, -1, 1), ps_n[:, 0], n_done[0], n_read[0])
                for half in range(2):
                    for what in ("input", "bias"):
                        project_gate(-1, 1, half, 0, what, what == "input")
                before_products(0, 0, [0])
                each_chunk(pe, iteration)
                pe.wait_ge(state_done, (CHUNKS + LAG) * C)
                for filler in fillers(CHUNKS + LAG, 0, [], True):
                    filler()

            @block.scalar
            def _(act):
                nc.scalar.preload_act_table_set("sigmoid_and_others")

                def double_tanh(l, m, k_to):
                    def first():
                        act.wait_ge(n_done[l], m + 1)
                        nc.scalar.activation(tanh_once[:, l], ps_n[:, l, 0:W].rearrange("p (t b) -> p t b", b=B),
                                             ACT.Tanh).then_inc(n_read[l], 1)

                    def second():
                        act.wait_ge(n_read[l], m + 1)
                        nc.scalar.activation(towards[:, k_to, :, l * B:(l + 1) * B], tanh_once[:, l],
                                             ACT.Tanh).then_inc(towards_ready[l], 1)
                    return [first, second]

                def cell_work(m):
                    def first():
                        act.wait_ge(cell_n_done, m + 1)
                        if not (isinstance(m, int) and m == 0):
                            act.wait_ge(cell_chain, 3 * m)
                        nc.scalar.activation(cell_once[:], ps_cell_n[:, 0:W].rearrange("p (t b) -> p t b", b=B),
                                             ACT.Tanh).then_inc(cell_n_read, 1)

                    def second():
                        act.wait_ge(cell_n_read, m + 1)
                        nc.scalar.activation(cell_n[:], cell_once[:], ACT.Tanh)

                    def third():
                        act.wait_ge(cell_g_done, m + 1)
                        nc.scalar.activation(cell_g[:], ps_cell_g[:, 0:W].rearrange("p (t b) -> p t b", b=B),
                                             ACT.Sigmoid, bias=tb["cell_bhf"][:]).then_inc(cell_inputs, 1)
                    return [first, second, third]

                def iteration(c, k, runs, nexts, cell):
                    work = [None, None]
                    for l in nexts:
                        work += double_tanh(l, c + 1 - l * LAG, 1 - k)
                    if cell:
                        work += cell_work(c - LAG - 1)
                    sl = columns(runs)
                    for s in range(C):
                        act.wait_ge(input_ready, c * C + s + 1)
                        nc.scalar.activation(gate[:, sl], ps_gate[:, k, s % 2, s // 2 * L2 + sl.start:s // 2 * L2 + sl.stop],
                                             ACT.Sigmoid).then_inc(gate_done, 1)
                        if s < len(work) and work[s]:
                            work[s]()

                for step in double_tanh(0, 0, 0):
                    step()
                each_chunk(act, iteration)
                for step in cell_work(CHUNKS - 1):
                    step()

            @block.vector
            def _(dve):
                chain = Serial(dve, split_chain)
                chain.step(nc.vector.tensor_copy(whf_hi[:], tb["lru_whf"][:]))
                chain.mark(nc.vector.tensor_tensor(whf_lo[:], tb["lru_whf"][:], whf_hi[:], ALU.subtract))
                chain.mark(nc.vector.memset(u_hi[:], 0.0))
                chain.mark(nc.vector.memset(u_lo[:], 0.0))
                chain.mark(nc.vector.tensor_copy(states[:, 1, C - 1, :], tb["lru_init"][:]))
                for k in range(2):
                    chain.mark(nc.vector.tensor_copy(h_hi[:, k, :], tb["lru_init"][:]))
                chain.settle()
                for k in range(2):
                    chain.mark(nc.vector.tensor_tensor(h_lo[:, k, :], tb["lru_init"][:], h_hi[:, k, :], ALU.subtract))
                nc.vector.memset(u[:], 0.0).then_inc(begun, 1)
                dve.wait_ge(begun, 1)
                chain.settle()
                dve.wait_ge(towards_ready[0], 1)
                chain.step(nc.vector.tensor_tensor(gap[:, 0:B], towards[:, 0, 0, 0:B], states[:, 1, C - 1, 0:B],
                                                   ALU.subtract))

                def iteration(c, k, runs, nexts, cell):
                    sl = columns(runs)
                    for s in range(C):
                        at = c * C + s
                        before = states[:, k, s - 1, sl] if s else states[:, 1 - k, C - 1, sl]
                        now = states[:, k, s, sl]
                        dve.wait_ge(gate_done, at + 1)
                        nc.vector.tensor_tensor(u_hi[:, sl], gate[:, sl], gap[:, sl], ALU.mult).then_inc(u_hi_done, 1)
                        nc.vector.tensor_tensor(u[:, sl], gate[:, sl], gap[:, sl], ALU.mult).then_inc(u_done, 1)
                        dve.wait_ge(u_done, at + 1)
                        nc.vector.tensor_tensor(u_lo[:, sl], u[:, sl], u_hi[:, sl], ALU.subtract).then_inc(u_lo_done, 1)
                        nc.vector.tensor_tensor(now, before, u[:, sl], ALU.add).then_inc(state_done, 1)
                        dve.wait_ge(state_done, at + 1)
                        if s + 1 < C:
                            nc.vector.tensor_tensor(gap[:, sl], towards[:, k, s + 1, sl], now,
                                                    ALU.subtract).then_inc(gap_done, 1)
                        elif nexts:
                            for l in nexts:
                                dve.wait_ge(towards_ready[l], c + 2 - l * LAG)
                            nx = columns(nexts)
                            nc.vector.tensor_tensor(gap[:, nx], towards[:, 1 - k, 0, nx], states[:, k, s, nx],
                                                    ALU.subtract).then_inc(gap_done, 1)
                        else:
                            nc.vector.memset(gap[:, sl], 0.0).then_inc(gap_done, 1)
                        nc.vector.tensor_copy(h_hi[:, s % 2, sl], now).then_inc(h_hi_done, 1)
                        dve.wait_ge(h_hi_done, at + 1)
                        nc.vector.tensor_tensor(h_lo[:, s % 2, sl], now, h_hi[:, s % 2, sl],
                                                ALU.subtract).then_inc(h_lo_done, 1)
                        dve.wait_ge(gap_done, at + 1)

                each_chunk(dve, iteration)

            @block.gpsimd
            def _(pool):
                nc.gpsimd.tensor_tensor(core.x[:], core.x[:], core.h[:], ALU.add)

                def cell(m):
                    at = m * C
                    at = slice(at, at + C) if isinstance(at, int) else bass.ds(at, C)
                    xn_now = xnt[:, :, at].rearrange("p b t -> p t b")
                    pool.wait_ge(cell_inputs, m + 1)
                    nc.gpsimd.tensor_tensor(cell_gap[:], cell_n[:], xn_now, ALU.subtract).then_inc(cell_chain, 1)
                    pool.wait_ge(cell_chain, 3 * m + 1)
                    nc.gpsimd.tensor_tensor(cell_u[:], cell_g[:], cell_gap[:], ALU.mult).then_inc(cell_chain, 1)
                    pool.wait_ge(cell_chain, 3 * m + 2)
                    nc.gpsimd.tensor_tensor(zt[:, :, at].rearrange("p b t -> p t b"), cell_u[:], xn_now,
                                            ALU.add).then_inc(cell_chain, 1)
                    pool.wait_ge(cell_chain, 3 * m + 3)

                with pool.Fori(0, CHUNKS) as m:
                    cell(m)


def turn_and_add(core, zt):
    nc = core.nc
    with core.stage() as ctx:
        ps_turn = core.psum("ps_turn", [P, 4, 4, P], ctx)
        turned = core.sem("turned", ctx)
        with nc.Block() as block:

            @block.tensor
            def _(pe):
                for t in range(NT):
                    pe.transpose(ps_turn[:, t // 4, t % 4, :], zt[:, t // 4, t % 4 * P:(t % 4 + 1) * P],
                                 core.ident[:]).then_inc(turned, 1)

            @block.vector
            def _(dve):
                for g in range(4):
                    dve.wait_ge(turned, 4 * g + 4)
                    nc.vector.tensor_tensor(core.x[:, 4 * g:4 * g + 4, :], ps_turn[:, g], core.x[:, 4 * g:4 * g + 4, :],
                                            ALU.add)


def lru(core):
    with core.stage() as ctx:
        xnt = core.sbuf("xnt", [P, B, T], ctx=ctx)
        zt = core.sbuf("zt", [P, B, T], ctx=ctx)
        layer_norm(core)
        rms_norm(core, xnt)
        recurrence(core, xnt, zt)
        turn_and_add(core, zt)


E1, F1 = 8, 256
F1T = F1 // P
ETILES = NT + E1
WROW = 3 * F1


def moe1(core):
    nc, dram, tb = core.nc, core.dram, core.tables
    layer_norm(core)
    x, h, ht = core.x, core.h, core.ht
    K = F1T
    BLK = 4
    TE = NT * E1
    with ExitStack() as stage:
        position = core.sbuf("position", [P, NT], U32, ctx=stage)
        weight_rows = core.sbuf("weight_rows", [P, ETILES], U32, ctx=stage)
        with core.stage() as ctx:
            top = core.sbuf("top", [P, NT], ctx=ctx)
            score = core.sbuf("score", [P, NT], ctx=ctx)
            best = core.sbuf("best", [P, NT, E1], ctx=ctx)
            rank = core.sbuf("rank", [P, NT, E1], ctx=ctx)
            top_rank = core.sbuf("top_rank", [P, NT], ctx=ctx)
            chosen = core.sbuf("chosen", [P, NT, E1], F16, ctx=ctx)
            totals = core.sbuf("totals", [P, E1, NT], ctx=ctx)
            upto = core.sbuf("upto", [P, E1, NT], ctx=ctx)
            before = core.sbuf("before", [P, E1, NT], ctx=ctx)
            tiles_int = core.sbuf("tiles_int", [P, 2, E1], U32, ctx=ctx)
            tiles = core.sbuf("tiles", [P, E1], ctx=ctx)
            ends = core.sbuf("ends", [P, E1], ctx=ctx)
            starts = core.sbuf("starts", [P, E1], ctx=ctx)
            base = core.sbuf("base", [P, E1, NT], ctx=ctx)
            spots = core.sbuf("spots", [P, NT, E1], ctx=ctx)
            own_spot = core.sbuf("own_spot", [P, NT, E1], ctx=ctx)
            ended = core.sbuf("ended", [P, ETILES, E1], ctx=ctx)
            owner = core.sbuf("owner", [P, ETILES], ctx=ctx)
            owner_base = core.sbuf("owner_base", [P, ETILES], ctx=ctx)
            scaled = core.sbuf("scaled", [P, NT, D], ctx=ctx)
            silu = core.sbuf("silu", [P, 2, 512], ctx=ctx)
            act = core.sbuf("act", [P, 2, K, 512], ctx=ctx)
            ps_gu = core.psum("ps_gu", [P, 2, 2, 512], ctx)
            ps_down = core.psum("ps_down", [P, 4, P], ctx)
            ps_logit = core.psum("ps_logit", [P, 512], ctx)
            ps_rank = core.psum("ps_rank", [P, 2, TE], ctx)

            logits_done = core.sem("logits_done", ctx)
            chain_sem = core.sem("chain", ctx)
            top_ready = core.sem("top_ready", ctx)
            score_ready = core.sem("score_ready", ctx)
            chosen_ready = core.sem("chosen_ready", ctx)
            ranked = core.sem("ranked", ctx)
            scaled_ready = core.sem("scaled_ready", ctx)
            position_ready = core.sem("position_ready", ctx)
            sorted_out = core.sem("sorted_out")
            gate_done = core.sem("gate_done", ctx)
            up_done = core.sem("up_done", ctx)
            silu_done = core.sem("silu_done", ctx)
            act_done = core.sem("act_done", ctx)
            down_done = core.sem("down_done", ctx)
            x_updated = core.sem("x_updated", ctx)
            with nc.Block() as block:

                @block.tensor
                def _(pe):
                    for t in range(NT):
                        mm = pe.matmul(ps_logit[:, t * E1:(t + 1) * E1], ht[:, t * P:(t + 1) * P], tb["l1_gate"][:],
                                       start=True, stop=True)
                    mm.then_inc(logits_done, 1)

                    def products(n):
                        blk, k = n // K, n % K
                        if n >= 2:
                            pe.wait_ge(act_done, n - 1)
                        for i, (name, done) in enumerate((("l1_sh_gate", gate_done), ("l1_sh_up", up_done))):
                            pe.matmul(ps_gu[:, n % 2, i, :], tb[name][:, k * P:(k + 1) * P],
                                      ht[:, blk * 512:(blk + 1) * 512], start=True, stop=True).then_inc(done, 1)

                    products(0)
                    pe.wait_ge(chosen_ready, 1)
                    flat = chosen[:].rearrange("p t e -> p (t e)")
                    pe.matmul(ps_rank[:, 0, :], tb["earlier_token"][:], flat, start=True, stop=True)
                    pe.matmul(ps_rank[:, 1, :], tb["ones16"][:], flat, start=True, stop=True).then_inc(ranked, 1)
                    for n in range(1, BLK * K + 1):
                        if n < BLK * K:
                            products(n)
                        if n % K == 0:
                            blk = n // K - 1
                            pe.wait_ge(act_done, K * (blk + 1))
                            if blk:
                                pe.wait_ge(x_updated, blk)
                            for t in range(4):
                                for j in range(K):
                                    mm = pe.matmul(ps_down[:, t, :], act[:, blk % 2, j, t * P:(t + 1) * P],
                                                   tb["l1_sh_down"][:, j, :], start=(j == 0), stop=(j == K - 1))
                            mm.then_inc(down_done, 1)

                @block.scalar
                def _(act_e):
                    nc.scalar.preload_act_table_set("sigmoid_and_others")
                    act_e.wait_ge(top_ready, 1)
                    nc.scalar.activation(score[:], top[:], ACT.Sigmoid).then_inc(score_ready, 1)
                    nc.scalar.preload_act_table_set("silu_and_others")
                    for n in range(BLK * K):
                        act_e.wait_ge(gate_done, n + 1)
                        if n >= 2:
                            act_e.wait_ge(act_done, n - 1)
                        nc.scalar.activation(silu[:, n % 2, :], ps_gu[:, n % 2, 0, :], ACT.Silu).then_inc(silu_done, 1)

                @block.vector
                def _(dve):
                    chain = Serial(dve, chain_sem)
                    logits = ps_logit[:, 0:TE].rearrange("p (t e) -> p t e", e=E1)

                    def over_experts(a):
                        return a.rearrange("p (t o) -> p t o", o=1).to_broadcast([P, NT, E1])

                    dve.wait_ge(logits_done, 1)
                    nc.vector.tensor_reduce(top[:], logits, AX.X, ALU.max).then_inc(top_ready, 1)
                    dve.wait_ge(top_ready, 1)
                    chain.step(nc.vector.tensor_tensor(best[:], logits, over_experts(top[:]), ALU.is_equal))
                    chain.step(nc.vector.tensor_tensor(rank[:], best[:], tb["expert_ranks"][:], ALU.mult))
                    chain.step(nc.vector.tensor_reduce(top_rank[:], rank[:], AX.X, ALU.max))
                    nc.vector.tensor_tensor(chosen[:], rank[:], over_experts(top_rank[:]),
                                            ALU.is_equal).then_inc(chosen_ready, 1)
                    dve.wait_ge(ranked, 1)
                    by_expert = ps_rank[:, 1, :].rearrange("p (t e) -> p e t", e=E1)
                    chain.step(nc.vector.tensor_copy(totals[:], by_expert))
                    chain.step(nc.vector.tensor_tensor_scan(
                        upto[:].rearrange("p e t -> p (e t)"), tb["same_expert"][:],
                        totals[:].rearrange("p e t -> p (e t)"), 0.0, ALU.mult, ALU.add))
                    chain.mark(nc.vector.tensor_tensor(before[:], upto[:], totals[:], ALU.subtract))
                    chain.step(nc.vector.tensor_scalar(tiles_int[:, 0, :], upto[:, :, NT - 1], float(P - 1), None, ALU.add))
                    chain.step(nc.vector.tensor_scalar(tiles_int[:, 1, :], tiles_int[:, 0, :], 7, None,
                                                       ALU.logical_shift_right))
                    chain.step(nc.vector.tensor_copy(tiles[:], tiles_int[:, 1, :]))
                    chain.step(nc.vector.tensor_tensor_scan(ends[:], tb["ones8"][:], tiles[:], 0.0, ALU.mult, ALU.add))
                    chain.step(nc.vector.tensor_tensor(starts[:], ends[:], tiles[:], ALU.subtract))
                    chain.step(nc.vector.scalar_tensor_tensor(
                        out=base[:], in0=starts[:].rearrange("p (e o) -> p e o", o=1).to_broadcast([P, E1, NT]),
                        scalar=float(P), in1=before[:], op0=ALU.mult, op1=ALU.add))
                    chain.step(nc.vector.tensor_tensor(spots[:], ps_rank[:, 0, :].rearrange("p (t e) -> p t e", e=E1),
                                                       base[:].rearrange("p e t -> p t e"), ALU.add))
                    dve.wait_ge(chosen_ready, 1)
                    chain.step(nc.vector.tensor_tensor(own_spot[:], spots[:], chosen[:], ALU.mult))
                    chain.mark(nc.vector.tensor_reduce(top_rank[:], own_spot[:], AX.X, ALU.add))
                    chain.step(nc.vector.tensor_tensor(
                        ended[:], ends[:].rearrange("p (o e) -> p o e", o=1).to_broadcast([P, ETILES, E1]),
                        tb["tile_numbers"][:], ALU.is_le))
                    nc.vector.tensor_copy(position[:], top_rank[:]).then_inc(position_ready, 1)
                    chain.step(nc.vector.tensor_reduce(owner[:], ended[:], AX.X, ALU.add))
                    chain.step(nc.vector.tensor_scalar(owner_base[:], owner[:], float(E1 - 1), float(P), ALU.min, ALU.mult))
                    nc.vector.tensor_scalar(weight_rows[:], owner_base[:], tb["partition"][:], None, ALU.add)
                    dve.wait_ge(score_ready, 1)
                    for t in range(NT):
                        nc.vector.tensor_scalar(scaled[:, t, :], h[:, t, :], score[:, t:t + 1], None,
                                                ALU.mult).then_inc(scaled_ready, 1)

                    for n in range(BLK * K):
                        blk, k = n // K, n % K
                        dve.wait_ge(silu_done, n + 1)
                        dve.wait_ge(up_done, n + 1)
                        if blk >= 2:
                            dve.wait_ge(down_done, blk - 1)
                        nc.vector.tensor_tensor(act[:, blk % 2, k, :], silu[:, n % 2, :], ps_gu[:, n % 2, 1, :],
                                                ALU.mult).then_inc(act_done, 1)
                        if k == K - 1:
                            dve.wait_ge(down_done, blk + 1)
                            nc.vector.scalar_tensor_tensor(
                                out=x[:, 4 * blk:4 * blk + 4, :], in0=ps_down[:], scalar=0.5,
                                in1=x[:, 4 * blk:4 * blk + 4, :], op0=ALU.mult, op1=ALU.add).then_inc(x_updated, 1)

                @block.gpsimd
                def _(pool):
                    pool.wait_ge(position_ready, 1)
                    for t in range(NT):
                        pool.wait_ge(scaled_ready, t + 1)
                        pool.indirect_dma_start(dram["sorted"], bass.IndirectOffsetOnAxis(ap=position[:, t:t + 1], axis=0),
                                                scaled[:, t, :], None).then_inc(sorted_out, 16)
                    pool.wait_ge(sorted_out, 16 * NT)

        with core.stage() as ctx:
            rows = core.sbuf("rows", [P, 2, D], ctx=ctx)
            w = core.sbuf("w", [P, 2, WROW], ctx=ctx)
            w_index = core.sbuf("w_index", [P, 2], U32, ctx=ctx)
            xt = core.sbuf("xt", [P, 2, P], ctx=ctx)
            silu = core.sbuf("silu", [P, 2, F1T, P], ctx=ctx)
            hidden = core.sbuf("hidden", [P, 2, F1T, P], ctx=ctx)
            y = core.sbuf("y", [P, 2, D], ctx=ctx)
            ps_xt = core.psum("ps_xt", [P, 2, 512], ctx)
            ps_gu = core.psum("ps_gu", [P, 2, 2, 512], ctx)
            ps_y = core.psum("ps_y", [P, 2, 512], ctx)
            rows_loaded = [core.sem("rows_loaded", ctx), core.sem("rows_loaded", ctx)]
            w_loaded = [core.sem("w_loaded"), core.sem("w_loaded")]
            y_stored = [core.sem("y_stored", ctx), core.sem("y_stored", ctx)]
            index_ready = core.sem("index_ready", ctx)
            xt_turned = core.sem("xt_turned", ctx)
            xt_ready = core.sem("xt_ready", ctx)
            gate_done = core.sem("gate_done", ctx)
            up_done = core.sem("up_done", ctx)
            silu_done = core.sem("silu_done", ctx)
            hidden_done = core.sem("hidden_done", ctx)
            down_done = core.sem("down_done", ctx)
            y_ready = core.sem("y_ready", ctx)

            def each_tile(engine, body, first=0):
                for k in range(2):
                    body(k, 0, k)
                with engine.Fori(1, ETILES // 2) as pair:
                    for k in range(2):
                        body(2 * pair + k, pair, k)

            def later(j, n):
                return not isinstance(j, int) or j >= n

            with nc.Block() as block:

                @block.sync
                def _(sp):
                    def tile(j, pair, k):
                        at = slice(j * P, (j + 1) * P) if isinstance(j, int) else bass.ds(j * P, P)
                        if later(j, 2):
                            sp.wait_ge(xt_turned, j - 1)
                        sp.dma_start(rows[:, k, :], dram["sorted"][at, :]).then_inc(rows_loaded[k], 16)

                    each_tile(sp, tile)
                    for k in range(2):
                        sp.wait_ge(y_stored[k], 16 * (ETILES // 2))

                @block.gpsimd
                def _(pool):
                    def tile(j, pair, k):
                        pool.wait_ge(index_ready, j + 1)
                        if later(j, 2):
                            pool.wait_ge(down_done, j - 1)
                        pass_waits(core, pool)
                        pool.indirect_dma_start(w[:, k, :], None, dram["l1_experts"],
                                                bass.IndirectOffsetOnAxis(ap=w_index[:, k:k + 1], axis=0)
                                                ).then_inc(w_loaded[k], 16)

                    each_tile(pool, tile)

                @block.vector
                def _(dve):
                    def index(j, pair, k):
                        one = slice(j, j + 1) if isinstance(j, int) else bass.ds(j, 1)
                        if later(j, 2):
                            dve.wait_ge(w_loaded[k], 16 * pair)
                        nc.vector.tensor_copy(w_index[:, k:k + 1], weight_rows[:, one]).then_inc(index_ready, 1)

                    def tile(j, pair, k):
                        dve.wait_ge(xt_turned, j + 1)
                        if later(j, 2):
                            dve.wait_ge(up_done, j - 1)
                        nc.vector.tensor_copy(xt[:, k, :], ps_xt[:, k, 0:P]).then_inc(xt_ready, 1)
                        if later(j, 2):
                            index(j, pair, k)
                        dve.wait_ge(silu_done, j + 1)
                        dve.wait_ge(up_done, j + 1)
                        if later(j, 2):
                            dve.wait_ge(down_done, j - 1)
                        nc.vector.tensor_tensor(hidden[:, k], silu[:, k],
                                                ps_gu[:, k, 1, 0:F1].rearrange("p (f t) -> p f t", f=F1T),
                                                ALU.mult).then_inc(hidden_done, 1)

                    for k in range(2):
                        index(k, 0, k)
                    each_tile(dve, tile)

                @block.tensor
                def _(pe):
                    def turn(j, pair, k):
                        pe.wait_ge(rows_loaded[k], 16 * (pair + 1))
                        if later(j, 2):
                            pe.wait_ge(xt_ready, j - 1)
                        pe.transpose(ps_xt[:, k, 0:P], rows[:, k, :], core.ident[:]).then_inc(xt_turned, 1)

                    def down(j, k):
                        pe.wait_ge(hidden_done, j + 1)
                        if later(j, 2):
                            pe.wait_ge(y_ready, j - 1)
                        for f in range(F1T):
                            mm = pe.matmul(ps_y[:, k, 0:D], hidden[:, k, f, :],
                                           w[:, k, 2 * F1 + f * P:2 * F1 + (f + 1) * P],
                                           start=(f == 0), stop=(f == F1T - 1))
                        mm.then_inc(down_done, 1)

                    def tile(j, pair, k):
                        turn(j, pair, k)
                        if later(j, 1):
                            down(j - 1, 1 - k)
                        pe.wait_ge(xt_ready, j + 1)
                        pe.wait_ge(w_loaded[k], 16 * (pair + 1))
                        if later(j, 2):
                            pe.wait_ge(hidden_done, j - 1)
                        for i, done in enumerate((gate_done, up_done)):
                            for f in range(F1T):
                                mm = pe.matmul(ps_gu[:, k, i, f * P:(f + 1) * P],
                                               w[:, k, i * F1 + f * P:i * F1 + (f + 1) * P], xt[:, k, :],
                                               start=True, stop=True)
                            mm.then_inc(done, 1)

                    each_tile(pe, tile)
                    down(ETILES - 1, 1)

                @block.scalar
                def _(act):
                    nc.scalar.preload_act_table_set("silu_and_others")

                    def give(j, pair, k):
                        at = slice(j * P, (j + 1) * P) if isinstance(j, int) else bass.ds(j * P, P)
                        act.wait_ge(down_done, j + 1)
                        if later(j, 2):
                            act.wait_ge(y_stored[k], 16 * pair)
                        nc.scalar.activation(y[:, k, :], ps_y[:, k, 0:D], ACT.Copy, scale=0.5).then_inc(y_ready, 1)
                        act.wait_ge(y_ready, j + 1)
                        act.dma_start(dram["expert_out"][at, :], y[:, k, :]).then_inc(y_stored[k], 16)

                    def tile(j, pair, k):
                        act.wait_ge(gate_done, j + 1)
                        if later(j, 2):
                            act.wait_ge(hidden_done, j - 1)
                        nc.scalar.activation(silu[:, k], ps_gu[:, k, 0, 0:F1].rearrange("p (f t) -> p f t", f=F1T),
                                             ACT.Silu).then_inc(silu_done, 1)
                        if later(j, 1):
                            give(j - 1, pair - (1 - k), 1 - k)

                    each_tile(act, tile)
                    give(ETILES - 1, ETILES // 2 - 1, 1)

        with core.stage() as ctx:
            back = core.sbuf("back", [P, NT, D], ctx=ctx)
            fetched = [core.sem("fetched") for _ in range(4)]
            with nc.Block() as block:

                @block.gpsimd
                def _(pool):
                    for t in range(NT):
                        pool.indirect_dma_start(back[:, t, :], None, dram["expert_out"],
                                                bass.IndirectOffsetOnAxis(ap=position[:, t:t + 1], axis=0)
                                                ).then_inc(fetched[t // 4], 16)

                @block.vector
                def _(dve):
                    for g in range(4):
                        dve.wait_ge(fetched[g], 64)
                        part = slice(4 * g, 4 * g + 4)
                        nc.vector.tensor_tensor(x[:, part, :], x[:, part, :], back[:, part, :], ALU.add)


HEADS, HD = 16, 8
GROUPS = 4
QT = T // P
BF16 = mybir.dt.bfloat16
ATT_SCALE = float(HD) ** -0.5
UNITS = [[(0, 3, 0)], [(0, 0, 0), (0, 2, P)], [(1, 3, 0)], [(1, 0, 0), (1, 2, P)], [(0, 1, 0), (1, 1, 2 * P)]]


def attention(core):
    nc, tb = core.nc, core.tables
    layer_norm(core)
    h_t, x = core.ht, core.x
    with ExitStack() as stage:
        y = core.sbuf("y", [P, NT, D], ctx=stage)
        with core.stage() as ctx:
            hb = core.sbuf("hb", [P, T], ctx=ctx)
            turned = core.sbuf("turned", [P, 2, 2, T], ctx=ctx)
            roped = core.sbuf("roped", [P, 2, T], ctx=ctx)
            part_hi = core.sbuf("part_hi", [P, 2, T], F16, ctx=ctx)
            part_lo = core.sbuf("part_lo", [P, 2, T], F16, ctx=ctx)
            spread = core.sbuf("spread", [P, 2, GROUPS, T], F16, ctx=ctx)
            v_hi = core.sbuf("v_hi", [P, QT, D], F16, ctx=ctx)
            v_lo = core.sbuf("v_lo", [P, QT, D], F16, ctx=ctx)
            top = core.sbuf("top", [P, 2, 2], ctx=ctx)
            shift = core.sbuf("shift", [P, 2, 2], ctx=ctx)
            total = core.sbuf("total", [P, 4, 2], ctx=ctx)
            inverse = core.sbuf("inverse", [P, 2, 2], ctx=ctx)
            prob = core.sbuf("prob", [P, 2, 512], ctx=ctx)
            pt_hi = core.sbuf("pt_hi", [P, 2, 512], F16, ctx=ctx)
            pt_lo = core.sbuf("pt_lo", [P, 2, 512], F16, ctx=ctx)
            ps_score = core.psum("ps_score", [P, 3, 512], ctx)
            ps_turn = core.psum("ps_turn", [P, 3, 512], ctx)
            ps_y = core.psum("ps_y", [P, 2, 512], ctx)

            hb_ready = core.sem("hb_ready", ctx)
            projected = core.sem("projected", ctx)
            turned_ready = core.sem("turned_ready", ctx)
            rope_chain = core.sem("rope_chain", ctx)
            parts_ready = core.sem("parts_ready", ctx)
            spread_done = core.sem("spread_done", ctx)
            spread_ready = core.sem("spread_ready", ctx)
            v_done = core.sem("v_done", ctx)
            v_chain = core.sem("v_chain", ctx)
            scored = core.sem("scored", ctx)
            topped = core.sem("topped", ctx)
            shifted = core.sem("shifted", ctx)
            exped = core.sem("exped", ctx)
            prob_turned = core.sem("prob_turned", ctx)
            hi_ready = core.sem("hi_ready", ctx)
            lo_ready = core.sem("lo_ready", ctx)
            inverted = core.sem("inverted", ctx)
            summed = core.sem("summed", ctx)
            y_ready = core.sem("y_ready", ctx)

            PAIRS = HEADS // 2
            NU = PAIRS * len(UNITS)
            KIND = ("q", "k")

            blocks_through = np.cumsum([len(UNITS[n % len(UNITS)]) for n in range(NU)]).tolist()
            yb = y[:].rearrange("p t d -> p (t d)")

            def unit(n):
                pair, i = divmod(n, len(UNITS))
                return [(pair // 4 * 8 + pair % 4 + 4 * a, qt, col) for a, qt, col in UNITS[i]]

            with nc.Block() as block:

                def bank(i):
                    return ps_score[:, i, :] if i < 3 else ps_turn[:, 0, :]

                @block.tensor
                def _(pe):
                    def project(b):
                        pe.wait_ge(hb_ready, b + 1)
                        for i, name in enumerate(("att_q", "att_q_partner", "att_k", "att_k_partner")):
                            pe.matmul(bank(i), tb[name][:], hb[:], start=True, stop=True).then_inc(projected, 1)
                        for t in range(QT):
                            out = ps_turn[:, 1, t * P:(t + 1) * P]
                            pe.matmul(out, tb["ones_row"][:], tb["att_bv"][:], start=True, stop=False)
                            mm = pe.matmul(out, hb[:, t * P:(t + 1) * P], tb["att_v"][:], start=False, stop=True)
                        mm.then_inc(v_done, 1)
                        n = 0
                        for i in range(2):
                            pe.wait_ge(parts_ready, (2 * b + i + 1))
                            for g in range(GROUPS):
                                if n >= 2:
                                    pe.wait_ge(spread_ready, 2 * GROUPS * b + n - 1)
                                out = ps_y[:, n % 2, :]
                                pe.matmul(out, tb[f"spread_{KIND[i]}_hi"][:, g * P:(g + 1) * P], part_hi[:, i, :],
                                          start=True, stop=False)
                                pe.matmul(out, tb[f"spread_{KIND[i]}_lo"][:, g * P:(g + 1) * P], part_lo[:, i, :],
                                          start=False, stop=True).then_inc(spread_done, 1)
                                n += 1

                    def scores(b, n):
                        if n >= 3:
                            pe.wait_ge(exped, NU * b + n - 2)
                        for head, qt, col in unit(n):
                            g, row = head // 4, head % 4 * 32
                            width = (qt + 1) * P
                            pe.matmul(ps_score[:, n % 3, col:col + width],
                                      spread[row:row + 32, 0, g, qt * P:(qt + 1) * P],
                                      spread[row:row + 32, 1, g, 0:width], start=True, stop=False,
                                      skip_group_check=True)
                            mm = pe.matmul(ps_score[:, n % 3, col + qt * P:col + width], tb["ident_bf16"][:],
                                           tb["causal"][:], start=False, stop=True, skip_group_check=True)
                        mm.then_inc(scored, 1)

                    def turn(b, n):
                        pe.wait_ge(exped, NU * b + n + 1)
                        if n >= 3:
                            pe.wait_ge(lo_ready, NU * b + n - 2)
                        for c in range(4):
                            mm = pe.transpose(ps_turn[:, n % 3, c * P:(c + 1) * P], prob[:, n % 2, c * P:(c + 1) * P],
                                              core.ident[:])
                        mm.then_inc(prob_turned, 1)

                    def values(b, n):
                        pe.wait_ge(lo_ready, NU * b + n + 1)
                        if n >= 2:
                            pe.wait_ge(y_ready, NU * b + n - 1)
                        for i, (head, qt, col) in enumerate(unit(n)):
                            out = ps_y[:, n % 2, i * HD:(i + 1) * HD]
                            own = slice(head * HD, (head + 1) * HD)
                            for kt in range(qt + 1):
                                at = slice(col + kt * P, col + (kt + 1) * P)
                                pe.matmul(out, pt_hi[:, n % 2, at], v_hi[:, kt, own], start=(kt == 0), stop=False)
                                pe.matmul(out, pt_hi[:, n % 2, at], v_lo[:, kt, own], start=False, stop=False)
                                mm = pe.matmul(out, pt_lo[:, n % 2, at], v_hi[:, kt, own], start=False, stop=(kt == qt))
                        mm.then_inc(summed, 1)

                    with pe.Fori(0, B) as b:
                        project(b)
                        pe.wait_ge(spread_ready, 2 * GROUPS * (b + 1))
                        scores(b, 0)
                        scores(b, 1)
                        for n in range(NU):
                            if n + 2 < NU:
                                scores(b, n + 2)
                            turn(b, n)
                            if n == 1:
                                pe.wait_ge(v_chain, 2 * (b + 1))
                            if n >= 1:
                                values(b, n - 1)
                        values(b, NU - 1)
                        pe.wait_ge(y_ready, NU * (b + 1))

                @block.scalar
                def _(act):
                    nc.scalar.preload_act_table_set("exp_and_others")
                    with act.Fori(0, B) as b:
                        nc.scalar.activation(hb[:], h_t[:, bass.ds(b * T, T)], ACT.Copy).then_inc(hb_ready, 1)
                        act.wait_ge(v_done, b + 1)
                        nc.scalar.activation(v_hi[:].rearrange("p t d -> p (t d)"), ps_turn[:, 1, :],
                                             ACT.Copy).then_inc(v_chain, 1)
                        for n in range(2 * GROUPS):
                            act.wait_ge(spread_done, 2 * GROUPS * b + n + 1)
                            nc.scalar.activation(spread[:, n // GROUPS, n % GROUPS, :], ps_y[:, n % 2, :],
                                                 ACT.Copy).then_inc(spread_ready, 1)

                        def exps(n):
                            act.wait_ge(shifted, NU * b + n + 1)
                            if n >= 2:
                                act.wait_ge(prob_turned, NU * b + n - 1)
                            if n >= 4:
                                act.wait_ge(inverted, NU * b + n - 3)
                            for i, (head, qt, col) in enumerate(unit(n)):
                                last = nc.scalar.activation(prob[:, n % 2, col:col + (qt + 1) * P],
                                                            ps_score[:, n % 3, col:col + (qt + 1) * P], ACT.Exp,
                                                            bias=shift[:, n % 2, i:i + 1], scale=ATT_SCALE,
                                                            accum_out=total[:, n % 4, i:i + 1])
                            last.then_inc(exped, 1)

                        def his(n):
                            act.wait_ge(prob_turned, NU * b + n + 1)
                            if n >= 2:
                                act.wait_ge(summed, NU * b + n - 1)
                            nc.scalar.activation(pt_hi[:, n % 2, :], ps_turn[:, n % 3, :], ACT.Copy).then_inc(hi_ready, 1)

                        for n in range(NU):
                            exps(n)
                            if n >= 1:
                                his(n - 1)
                        his(NU - 1)

                @block.vector
                def _(dve):
                    with dve.Fori(0, B) as b:
                        for i in range(2):
                            for j in range(2):
                                dve.wait_ge(projected, 4 * b + 2 * i + j + 1)
                                nc.vector.scalar_tensor_tensor(
                                    out=turned[:, i, j, :], in0=bank(2 * i + j), scalar=tb["att_bias"][:, 2 * i + j:2 * i + j + 1],
                                    in1=tb[("rope_cos", "rope_sin")[j]][:], op0=ALU.add, op1=ALU.mult
                                ).then_inc(rope_chain, 1)
                        for i in range(2):
                            dve.wait_ge(rope_chain, 8 * b + 4 + 2 * i)
                            nc.vector.tensor_tensor(roped[:, i, :], turned[:, i, 0, :], turned[:, i, 1, :],
                                                    ALU.add).then_inc(rope_chain, 1)
                            dve.wait_ge(rope_chain, 8 * b + 5 + 2 * i)
                            nc.vector.tensor_copy(part_hi[:, i, :], roped[:, i, :]).then_inc(rope_chain, 1)
                            dve.wait_ge(rope_chain, 8 * b + 6 + 2 * i)
                            nc.vector.tensor_tensor(part_lo[:, i, :], roped[:, i, :], part_hi[:, i, :],
                                                    ALU.subtract).then_inc(parts_ready, 1)
                            dve.wait_ge(parts_ready, 2 * b + i + 1)
                        dve.wait_ge(v_chain, 2 * b + 1)
                        nc.vector.tensor_tensor(v_lo[:].rearrange("p t d -> p (t d)"), ps_turn[:, 1, :],
                                                v_hi[:].rearrange("p t d -> p (t d)"), ALU.subtract).then_inc(v_chain, 1)

                        def tops(n):
                            dve.wait_ge(scored, NU * b + n + 1)
                            if n >= 2:
                                dve.wait_ge(exped, NU * b + n - 1)
                            for i, (head, qt, col) in enumerate(unit(n)):
                                nc.vector.tensor_reduce(top[:, n % 2, i:i + 1], ps_score[:, n % 3, col:col + (qt + 1) * P],
                                                        AX.X, ALU.max).then_inc(topped, 1)
                            dve.wait_ge(topped, HEADS * QT * b + blocks_through[n])
                            k = len(unit(n))
                            nc.vector.tensor_scalar(shift[:, n % 2, 0:k], top[:, n % 2, 0:k], -ATT_SCALE, None,
                                                    ALU.mult).then_inc(shifted, 1)

                        def los(n):
                            dve.wait_ge(hi_ready, NU * b + n + 1)
                            nc.vector.tensor_tensor(pt_lo[:, n % 2, :], ps_turn[:, n % 3, :], pt_hi[:, n % 2, :],
                                                    ALU.subtract).then_inc(lo_ready, 1)
                            k = len(unit(n))
                            if n >= 2:
                                dve.wait_ge(y_ready, NU * b + n - 1)
                            nc.vector.reciprocal(inverse[:, n % 2, 0:k], total[:, n % 4, 0:k]).then_inc(inverted, 1)

                        def outs(n):
                            dve.wait_ge(summed, NU * b + n + 1)
                            dve.wait_ge(inverted, NU * b + n + 1)
                            for i, (head, qt, col) in enumerate(unit(n)):
                                last = nc.vector.tensor_scalar(
                                    yb[:, bass.ds(b * QT * D + qt * D + head * HD, HD)], ps_y[:, n % 2, i * HD:(i + 1) * HD],
                                    inverse[:, n % 2, i:i + 1], None, ALU.mult)
                            last.then_inc(y_ready, 1)

                        tops(0)
                        for n in range(NU):
                            if n + 1 < NU:
                                tops(n + 1)
                            if n >= 1:
                                los(n - 1)
                            if n >= 2:
                                outs(n - 2)
                        los(NU - 1)
                        outs(NU - 2)
                        outs(NU - 1)

        with core.stage() as ctx:
            yt = core.sbuf("yt", [P, NT, P], ctx=ctx)
            ps_yt = core.psum("ps_yt", [P, 4, 4, P], ctx)
            ps_out = core.psum("ps_out", [P, 4, 4, P], ctx)
            y_turned = core.sem("y_turned", ctx)
            yt_ready = core.sem("yt_ready", ctx)
            out_done = core.sem("out_done", ctx)
            with nc.Block() as block:

                @block.tensor
                def _(pe):
                    for g in range(4):
                        for t in range(4):
                            mm = pe.transpose(ps_yt[:, g, t, :], y[:, 4 * g + t, :], core.ident[:])
                        mm.then_inc(y_turned, 1)
                    for g in range(4):
                        pe.wait_ge(yt_ready, g + 1)
                        for t in range(4):
                            pe.matmul(ps_out[:, g, t, :], tb["ones_row"][:], tb["att_bo"][:], start=True, stop=False)
                            mm = pe.matmul(ps_out[:, g, t, :], yt[:, 4 * g + t, :], tb["att_o"][:], start=False, stop=True)
                        mm.then_inc(out_done, 1)

                @block.scalar
                def _(act):
                    for g in range(4):
                        act.wait_ge(y_turned, g + 1)
                        nc.scalar.activation(yt[:, 4 * g:4 * g + 4, :], ps_yt[:, g], ACT.Copy).then_inc(yt_ready, 1)

                @block.vector
                def _(dve):
                    for g in range(4):
                        dve.wait_ge(out_done, g + 1)
                        nc.vector.tensor_tensor(x[:, 4 * g:4 * g + 4, :], x[:, 4 * g:4 * g + 4, :], ps_out[:, g], ALU.add)
def host_constants():
    p = np.arange(P)
    block = p // SEG
    same = block[:, None] == block[None, :]
    c = {
        "ident": np.eye(P, dtype=np.float32),
        "ident16": np.eye(P, dtype=np.float16),
        "same_block": same.astype(np.float16),
        "earlier_segment": (same & (p[:, None] < p[None, :])).astype(np.float16),
        "earlier_token": (p[:, None] < p[None, :]).astype(np.float16),
        "ones16": np.ones((P, P), np.float16),
        "slot_numbers": np.tile(np.arange(1, CAP + 1, dtype=np.float16), (P, 1)),
        "token_ids": (p[:, None] + P * np.arange(NT)[None, :]).astype(np.float16),
        "bit_masks": np.tile((1 << np.arange(SCORE_BITS - 1, -1, -1)).astype(np.uint32), (P, 1)),
        "bit_values": np.tile((2.0 ** np.arange(SCORE_BITS - 1, -1, -1)).astype(np.float32), (P, 1)),
        "ones_row": np.ones((1, P), np.float32),
        "expert_ranks": np.broadcast_to(np.arange(E1, 0, -1, dtype=np.float32), (P, NT, E1)),
        "same_expert": np.broadcast_to((np.arange(NT * E1) % NT > 0).astype(np.float32), (P, NT * E1)),
        "ones8": np.ones((P, E1), np.float32),
        "tile_numbers": np.broadcast_to(np.arange(ETILES, dtype=np.float32)[:, None], (P, ETILES, E1)),
        "partition": p.astype(np.float32)[:, None],
    }
    theta = (1.0 / np.float32(10000.0) ** (np.arange(0, HD, 2, dtype=np.float32) / np.float32(HD))).astype(np.float32)
    angle = np.arange(1, T + 1, dtype=np.float32)[None, :] * theta[p % (HD // 2)][:, None]
    sign = np.where(p % HD < HD // 2, -1.0, 1.0).astype(np.float32)[:, None]
    c["rope_cos"] = np.cos(angle)
    c["rope_sin"] = sign * np.sin(angle)
    bf16 = mybir.dt.np(BF16)
    c["ident_bf16"] = np.eye(P).astype(bf16)
    c["causal"] = np.where(p[:, None] >= p[None, :], 0.0, -1e30).astype(bf16)
    for kind, part, places in (("q", "hi", (0, 1)), ("q", "lo", (2,)), ("k", "hi", (0, 2)), ("k", "lo", (1,))):
        s = np.zeros((P, GROUPS, P), np.float16)
        for head in range(HEADS):
            for i in range(HD):
                for place in places:
                    s[head * HD + i, head // 4, head % 4 * 32 + place * HD + i] = 1
        c[f"spread_{kind}_{part}"] = s.reshape(P, GROUPS * P)
    return c


def lay_out(i):
    def columns(a, parts):
        return a.reshape(-1, parts, P).transpose(2, 0, 1).reshape(P, -1)

    def rows(a):
        return a.reshape(-1, P, a.shape[-1]).transpose(1, 0, 2)

    a = {
        "x": i["L0_attn_x"].reshape(N, D),
        "l0_gate": i["L0_ffn_gate_w"].T,
        "l0_up": i["L0_ffn_up_w"].transpose(0, 2, 1),
        "l0_gate_proj": i["L0_ffn_gw"].transpose(0, 2, 1),
        "l0_down": i["L0_ffn_down_w"].transpose(0, 2, 1).reshape(E0, F0T, P, D).transpose(0, 2, 1, 3).reshape(E0, P, F0T * D),
        "l0_up_bias": columns(i["L0_ffn_up_b"], F0T),
        "l0_gate_bias": columns(i["L0_ffn_gb"], F0T),
        "l0_down_bias": i["L0_ffn_down_b"].reshape(1, E0 * D),
        "l0_sh_gate": i["L0_ffn_sh_gate_w"].T,
        "l0_sh_up": i["L0_ffn_sh_up_w"].T,
        "l0_sh_down": rows(i["L0_ffn_sh_down_w"].T),
        "lru_wi": i["L0_attn_lWi"].transpose(2, 0, 1),
        "lru_wif": i["L0_attn_lWif"].transpose(2, 0, 1),
        "lru_whf": i["L0_attn_lWhf"].transpose(2, 0, 1),
        "cell_wi": i["L0_attn_gWi"].T,
        "cell_wif": i["L0_attn_gWif"].T,
        "cell_whf": i["L0_attn_gWhf"].T,
        "lru_bhf": i["L0_attn_lbhf"].reshape(1, 2 * P),
        "cell_bhf": i["L0_attn_gbhf"].reshape(P, 1),
        "lru_gamma": i["L0_attn_gamma"].reshape(P, 1),
        "l1_gate": i["L1_ffn_gate_w"],
        "l1_sh_gate": i["L1_ffn_sh_gate"],
        "l1_sh_up": i["L1_ffn_sh_up"],
        "l1_sh_down": rows(i["L1_ffn_sh_down"]),
        "l1_experts": np.concatenate([i["L1_ffn_rt_gate"], i["L1_ffn_rt_up"],
                                      i["L1_ffn_rt_down"].reshape(E1, F1T, P, D).transpose(0, 2, 1, 3).reshape(E1, P, F1T * D)],
                                     axis=2).reshape(E1 * P, WROW),
        "lru_init": np.broadcast_to(i["L0_attn_l_init_hidden"].T[:, :, None], (D, 2, B)).reshape(P, 2 * B),
    }
    partner = (np.arange(P) // HD) * HD + (np.arange(P) + HD // 2) % HD
    a["att_q"], a["att_q_partner"] = i["L1_attn_Wq"].T, i["L1_attn_Wq"][partner].T
    a["att_k"], a["att_k_partner"] = i["L1_attn_Wk"].T, i["L1_attn_Wk"][partner].T
    a["att_v"], a["att_o"] = i["L1_attn_Wv"].T, i["L1_attn_Wo"].T
    a["att_bias"] = np.stack([i["L1_attn_bq"], i["L1_attn_bq"][partner],
                              i["L1_attn_bk"], i["L1_attn_bk"][partner]], axis=1)
    a["att_bv"], a["att_bo"] = i["L1_attn_bv"].reshape(1, D), i["L1_attn_bo"].reshape(1, D)
    return a


def scratch(nc, dram):
    dram["rows"] = nc.dram_tensor("rows", [N, HROW], F32, kind="Internal").ap()
    dram["sorted"] = nc.dram_tensor("sorted", [ETILES * P, D], F32, kind="Internal").ap()
    dram["expert_out"] = nc.dram_tensor("expert_out", [ETILES * P, D], F32, kind="Internal").ap()
    dram["sum"] = nc.dram_tensor("sum", [N, D], F32, kind="Internal").ap()


def store(core, out):
    with core.stage() as ctx:
        stored = core.sem("out_stored", ctx)
        with core.nc.Block() as block:

            @block.sync
            def _(sp):
                sp.dma_start(out.rearrange("(t p) d -> p t d", p=P), core.x[:]).then_inc(stored, 16)
                sp.wait_ge(stored, 16)


def program(nc, dram, out):
    scratch(nc, dram)
    core = Core(nc, dram)
    setup(core)
    moe0(core)
    lru(core)
    moe0(core)
    moe1(core)
    attention(core)
    moe1(core)
    store(core, out)


def kernel(**inputs):
    import concourse.bacc as bacc
    from concourse.bass_utils import run_bass_kernel_spmd

    arrays = {name: np.ascontiguousarray(a) for name, a in
              {**lay_out({name: np.asarray(a) for name, a in inputs.items()}), **host_constants()}.items()}
    nc = bacc.Bacc("TRN2", target_bir_lowering=False, num_devices=1)
    dram = {name: nc.dram_tensor(name, a.shape, mybir.dt.from_np(a.dtype), kind="ExternalInput").ap()
            for name, a in arrays.items()}
    out = nc.dram_tensor("out", [N, D], F32, kind="ExternalOutput").ap()
    program(nc, dram, out)
    result = run_bass_kernel_spmd(nc, [arrays], core_ids=[0])
    return result.results[0]["out"].reshape(B, T, D)
```

```python
from contextlib import ExitStack, contextmanager

import numpy as np

import concourse.bass as bass
from concourse import mybir

ALU = mybir.AluOpType
ACT = mybir.ActivationFunctionType
AX = mybir.AxisListType
F32 = mybir.dt.float32
F16 = mybir.dt.float16
U32 = mybir.dt.uint32

P = 128
D = 128
B, T = 4, 512
N = B * T
NT = N // P
LN_EPS = 1e-5

E0, F0, SH0 = 16, 512, 256
CAP = N // E0 * 2
SEG = P // E0
SEGLEN = N // SEG
F0T = F0 // P
HROW = D + E0
SCORE_BITS = 30


class Serial:

    def __init__(self, engine, sem):
        self.engine, self.sem, self.done = engine, sem, 0

    def step(self, instruction):
        instruction.then_inc(self.sem, 1)
        self.done += 1
        self.engine.wait_ge(self.sem, self.done)

    def mark(self, instruction):
        instruction.then_inc(self.sem, 1)
        self.done += 1

    def settle(self, all_but=0):
        self.engine.wait_ge(self.sem, self.done - all_but)


def pass_waits(core, pool):
    pool.sem_inc(core.waits_passed, 1)


class Core:

    def __init__(self, nc, dram):
        self.nc, self.dram, self.keep = nc, dram, ExitStack()
        self.made = 0
        self.to_clear = []

    def sbuf(self, name, shape, dtype=F32, ctx=None):
        self.made += 1
        return (ctx or self.keep).enter_context(self.nc.sbuf_tensor(f"{name}_{self.made}", shape, dtype))

    def psum(self, name, shape, ctx, dtype=F32):
        self.made += 1
        return ctx.enter_context(self.nc.psum_tensor(f"{name}_{self.made}", shape, dtype))

    def sem(self, name, ctx=None):
        self.made += 1
        sem = (ctx or self.keep).enter_context(self.nc.semaphore(f"{name}_{self.made}"))
        if ctx is not None:
            self.to_clear.append(sem.num)
        return sem

    @contextmanager
    def stage(self):
        outer, self.to_clear = self.to_clear, []
        with ExitStack() as ctx:
            yield ctx
            numbers = sorted(self.to_clear)
            runs = []
            for n in numbers:
                if runs and runs[-1].stop == n:
                    runs[-1] = range(runs[-1].start, n + 1)
                else:
                    runs.append(range(n, n + 1))
            if runs:
                with self.nc.Block() as block:

                    @block.gpsimd
                    def _(pool):
                        for run in runs:
                            pool.sem_clear(run)

        self.to_clear = outer


def setup(core):
    nc, dram = core.nc, core.dram
    core.x = core.sbuf("x", [P, NT, D])
    core.h = core.sbuf("h", [P, NT, D])
    core.ht = core.sbuf("ht", [P, N])
    core.ident = core.sbuf("ident", [P, P])
    core.x_loaded = core.sem("x_loaded")
    core.first_tables_loaded = core.sem("first_tables_loaded")
    core.tables_loaded = core.sem("tables_loaded")
    core.gate_loaded = core.sem("gate_loaded")
    core.cleared = core.sem("cleared")
    core.waits_passed = core.sem("waits_passed")

    small = {}

    def table(name, shape, dtype=F32):
        small[name] = core.sbuf(name, shape, dtype)

    table("same_block", [P, P], F16)
    table("earlier_segment", [P, P], F16)
    table("earlier_token", [P, P], F16)
    table("ones16", [P, P], F16)
    table("slot_numbers", [P, CAP], F16)
    table("token_ids", [P, NT], F16)
    table("bit_masks", [P, SCORE_BITS], U32)
    table("bit_values", [P, SCORE_BITS])
    table("ones_row", [1, P])
    table("l0_sh_gate", [P, SH0])
    table("l0_sh_up", [P, SH0])
    table("l0_sh_down", [P, SH0 // P, D])
    table("l0_gate_bias", [P, E0 * F0T])
    table("l0_up_bias", [P, E0 * F0T])
    table("l0_down_bias", [1, E0 * D])
    first = len(small)
    for name in ("lru_wi", "lru_wif", "lru_whf"):
        table(name, [P, 2, P])
    for name in ("cell_wi", "cell_wif", "cell_whf"):
        table(name, [P, P])
    table("lru_bhf", [1, 2 * P])
    table("cell_bhf", [P, 1])
    table("lru_gamma", [P, 1])
    table("lru_init", [P, 2 * B])
    table("l1_gate", [P, E1])
    table("l1_sh_gate", [P, F1])
    table("l1_sh_up", [P, F1])
    table("l1_sh_down", [P, F1T, D])
    table("expert_ranks", [P, NT, E1])
    table("same_expert", [P, E1 * NT])
    table("ones8", [P, E1])
    table("tile_numbers", [P, ETILES, E1])
    table("partition", [P, 1])
    for name in ("att_q", "att_q_partner", "att_k", "att_k_partner", "att_v", "att_o"):
        table(name, [P, P])
    table("att_bias", [P, 4])
    table("att_bv", [D, P])
    table("att_bo", [P, D])
    for name in ("rope_cos_q", "rope_sin_q", "rope_cos_k", "rope_sin_k"):
        table(name, [P, T])
    table("ident_bf16", [P, P], BF16)
    table("causal", [P, P], BF16)
    for kind in ("q", "k"):
        for part in ("hi", "lo"):
            table(f"spread_{kind}_{part}", [P, GROUPS * P], F16)
    core.tables = small
    core.first_tables, core.later_tables = list(small)[:first], list(small)[first:]
    core.gate_spread = core.sbuf("gate_spread", [P, SEG, P])

    core.zeros = core.sbuf("zeros", [P, ETILES * D])
    with core.stage() as ctx:
        gate = core.sbuf("gate", [P, E0], ctx=ctx)
        gate_zeroed = core.sem("gate_zeroed", ctx)
        spread = core.sem("spread", ctx)
        x_tiled = dram["x"].rearrange("(t p) d -> p t d", p=P)
        with nc.Block() as block:

            @block.sync
            def _(sp):
                sp.dma_start(core.x[:], x_tiled).then_inc(core.x_loaded, 16)
                sp.dma_start(gate[:], dram["l0_gate"]).then_inc(core.gate_loaded, 16)
                sp.dma_start(core.ident[:], dram["ident"]).then_inc(core.x_loaded, 16)
                sp.wait_ge(core.x_loaded, 32)

            @block.gpsimd
            def _(pool):
                nc.gpsimd.memset(core.gate_spread[:], 0.0).then_inc(gate_zeroed, 1)

            @block.vector
            def _(dve):
                dve.wait_ge(gate_zeroed, 1)
                dve.wait_ge(core.gate_loaded, 16)
                for s in range(SEG):
                    nc.vector.tensor_copy(core.gate_spread[:, s, s:P:SEG], gate[:]).then_inc(spread, 1)


def load_tables(core, sp, names, loaded):
    for name in names:
        sp.dma_start(core.tables[name][:], core.dram[name]).then_inc(loaded, 16)


def first_tables_ready(core):
    with core.nc.Block() as block:

        @block.sync
        def _(sp):
            sp.wait_ge(core.first_tables_loaded, 16 * len(core.first_tables))


def tables_ready(core):
    with core.nc.Block() as block:

        @block.sync
        def _(sp):
            sp.wait_ge(core.tables_loaded, 16 * len(core.later_tables))

        @block.gpsimd
        def _(pool):
            pool.wait_ge(core.cleared, 16)


def layer_norm(core, first=False):
    nc, dram, x, h, ht = core.nc, core.dram, core.x, core.h, core.ht
    with core.stage() as ctx:
        stats = core.sbuf("stats", [P, NT, 6], ctx=ctx)
        mean_var = core.sbuf("mean_var", [P, NT, 2], ctx=ctx)
        var = core.sbuf("var", [P, NT], ctx=ctx)
        std = core.sbuf("std", [P, NT], ctx=ctx)
        rstd = core.sbuf("rstd", [P, NT], ctx=ctx)
        shift = core.sbuf("shift", [P, NT], ctx=ctx)
        turned = core.psum("turned", [P, 4, 512], ctx)
        dve_chain = core.sem("ln_chain", ctx)
        var_ready = core.sem("var_ready", ctx)
        std_ready = core.sem("std_ready", ctx)
        factors_ready = core.sem("factors_ready", ctx)
        zeroed = core.sem("zeroed", ctx)
        h_by_dve = core.sem("h_by_dve", ctx)
        h_by_act = core.sem("h_by_act", ctx)
        turned_ready = core.sem("turned_ready", ctx)
        halves = (range(0, NT // 2), range(NT // 2, NT))
        order = (1, 0, 2, 3)

        def normalise_by_act(act, half):
            act.wait_ge(factors_ready, half + 1)
            for t in halves[half][4:]:
                nc.scalar.activation(h[:, t, :], x[:, t, :], ACT.Identity, bias=shift[:, t:t + 1],
                                     scale=rstd[:, t:t + 1]).then_inc(h_by_act, 1)

        with nc.Block() as block:

            if first:
                @block.sync
                def _(sp):
                    load_tables(core, sp, core.first_tables, core.first_tables_loaded)

                @block.gpsimd
                def _(pool):
                    nc.gpsimd.memset(core.zeros[:], 0.0).then_inc(zeroed, 1)
                    pool.wait_ge(zeroed, 1)
                    pool.dma_start(dram["sorted"].rearrange("(p t) d -> p (t d)", p=P), core.zeros[:]
                                   ).then_inc(core.cleared, 16)

            @block.vector
            def _(dve):
                chain = Serial(dve, dve_chain)

                def spreads(half):
                    for t in halves[half]:
                        chain.mark(nc.vector.bn_stats(stats[:, t, :], x[:, t, :]))

                def variances(half):
                    for t in halves[half]:
                        chain.mark(nc.vector.bn_aggr(mean_var[:, t, :], stats[:, t, :]))
                    chain.settle()
                    part = slice(halves[half].start, halves[half].stop)
                    nc.vector.tensor_scalar(var[:, part], mean_var[:, part, 1], LN_EPS, None,
                                            ALU.add).then_inc(var_ready, 1)

                def factors(half):
                    part = slice(halves[half].start, halves[half].stop)
                    dve.wait_ge(std_ready, half + 1)
                    chain.step(nc.vector.reciprocal(rstd[:, part], std[:, part]))
                    nc.vector.scalar_tensor_tensor(out=shift[:, part], in0=mean_var[:, part, 0], scalar=-1.0,
                                                   in1=rstd[:, part], op0=ALU.mult, op1=ALU.mult).then_inc(factors_ready, 1)

                def normalise(half):
                    for t in halves[half][:4]:
                        nc.vector.tensor_scalar(h[:, t, :], x[:, t, :], mean_var[:, t, 0:1], rstd[:, t:t + 1],
                                                ALU.subtract, ALU.mult).then_inc(h_by_dve, 1)

                spreads(0)
                chain.settle()
                variances(0)
                spreads(1)
                factors(0)
                chain.settle()
                variances(1)
                normalise(0)
                factors(1)
                normalise(1)
                for g in (0, 2):
                    dve.wait_ge(turned_ready, 4 * order.index(g) + 4)
                    nc.vector.tensor_copy(ht[:, 512 * g:512 * (g + 1)], turned[:, g, :])

            @block.tensor
            def _(pe):
                for t in (4 * g + i for g in order for i in range(4)):
                    by = (h_by_dve, h_by_act)[t // 4 % 2]
                    pe.wait_ge(by, t // 8 * 4 + t % 4 + 1)
                    pe.transpose(turned[:, t // 4, t % 4 * P:(t % 4 + 1) * P], h[:, t, :],
                                 core.ident[:]).then_inc(turned_ready, 1)

            @block.scalar
            def _(act):
                for half in range(2):
                    act.wait_ge(var_ready, half + 1)
                    part = slice(halves[half].start, halves[half].stop)
                    nc.scalar.activation(std[:, part], var[:, part], ACT.Sqrt).then_inc(std_ready, 1)
                    if half == 0:
                        normalise_by_act(act, 0)
                normalise_by_act(act, 1)
                for g in (1, 3):
                    act.wait_ge(turned_ready, 4 * order.index(g) + 4)
                    nc.scalar.activation(ht[:, 512 * g:512 * (g + 1)], turned[:, g, :], ACT.Copy)


class Routed:

    def __init__(self, core, ctx):
        self.select = core.sbuf("select", [P, 2, P], ctx=ctx)
        self.ones_row = core.sbuf("ones_row16", [1, P], F16, ctx=ctx)
        self.bias_parts = core.sbuf("bias_parts", [1, 2, E0 * D], F16, ctx=ctx)
        self.half_score = core.sbuf("half_score", [P, NT, E0], ctx=ctx)
        self.x_next = core.sbuf("x_next", [P, NT, D], ctx=ctx)
        self.stored = core.sem("stored", ctx)


def route_and_shared0(core, routed, first):
    nc, dram, tb = core.nc, core.dram, core.tables
    select, half_score, x_next, stored = routed.select, routed.half_score, routed.x_next, routed.stored
    ones_row16, bias_parts = routed.ones_row, routed.bias_parts
    K = SH0 // P
    BLK = 4
    with core.stage() as ctx:
        score = core.sbuf("score", [P, SEGLEN], ctx=ctx)
        over = core.sbuf("over", [P, SEGLEN], ctx=ctx)
        equal = core.sbuf("equal", [P, SEGLEN], ctx=ctx)
        count_eq = core.sbuf("count_eq", [P, SEGLEN], ctx=ctx)
        fits = core.sbuf("fits", [P, SEGLEN], ctx=ctx)
        taken_eq = core.sbuf("taken_eq", [P, SEGLEN], ctx=ctx)
        taken = core.sbuf("taken", [P, SEGLEN], ctx=ctx)
        count_taken = core.sbuf("count_taken", [P, SEGLEN], ctx=ctx)
        slot = core.sbuf("slot", [P, SEGLEN], ctx=ctx)
        ones = core.sbuf("ones", [P, SEGLEN], ctx=ctx)
        cand = core.sbuf("cand", [P, 2], U32, ctx=ctx)
        least = core.sbuf("least", [P, 2], U32, ctx=ctx)
        kept_bit = core.sbuf("kept_bit", [P, 1], U32, ctx=ctx)
        part_count = core.sbuf("part_count", [P, 1], F16, ctx=ctx)
        part_sum = core.sbuf("part_sum", [P, 2], F16, ctx=ctx)
        need = core.sbuf("need", [P, 1], ctx=ctx)
        offset = core.sbuf("offset", [P, 2], ctx=ctx)
        silu = core.sbuf("silu", [P, 2, 512], ctx=ctx)
        act = core.sbuf("act", [P, 2, K, 512], ctx=ctx)

        ps_score = core.psum("ps_score", [P, 512], ctx)
        ps_count = core.psum("ps_count", [P, 512], ctx)
        ps_turn = core.psum("ps_turn", [P, 4, P], ctx)
        ps_gu = core.psum("ps_gu", [P, 2, 2, 512], ctx)
        ps_down = core.psum("ps_down", [P, 4, P], ctx)

        scores_summed = core.sem("scores_summed", ctx)
        score_ready = core.sem("score_ready", ctx)
        chain_sem = core.sem("route_chain", ctx)
        counted = core.sem("counted", ctx)
        totalled = core.sem("totalled", ctx)
        turned = core.sem("turned", ctx)
        table_ready = core.sem("table_ready", ctx)
        gate_done = core.sem("gate_done", ctx)
        up_done = core.sem("up_done", ctx)
        silu_done = core.sem("silu_done", ctx)
        act_done = core.sem("act_done", ctx)
        down_done = core.sem("down_done", ctx)
        next_ready = core.sem("next_ready", ctx)
        bias_split = core.sem("bias_split", ctx)

        rounds = []
        for blk in range(BLK):
            for k in range(K):
                rounds += [("gate", blk, k), ("up", blk, k)]
                if k == 0 and blk:
                    rounds.append(("down", blk - 1, 0))
        rounds.append(("down", BLK - 1, 0))
        assert len(rounds) <= SCORE_BITS

        with nc.Block() as block:

            @block.tensor
            def _(pe):
                for s in range(SEG):
                    mm = pe.matmul(ps_score[:, 0:SEGLEN], core.gate_spread[:, s, :],
                                   core.ht[:, s * SEGLEN:(s + 1) * SEGLEN], start=(s == 0), stop=(s == SEG - 1))
                mm.then_inc(scores_summed, 1)

                def shared(what, blk, k):
                    n = blk * K + k
                    if what == "gate":
                        if n >= 2:
                            pe.wait_ge(act_done, n - 1)
                        pe.matmul(ps_gu[:, n % 2, 0, :], tb["l0_sh_gate"][:, k * P:(k + 1) * P],
                                  core.ht[:, blk * 512:(blk + 1) * 512], start=True, stop=True).then_inc(gate_done, 1)
                    elif what == "up":
                        pe.matmul(ps_gu[:, n % 2, 1, :], tb["l0_sh_up"][:, k * P:(k + 1) * P],
                                  core.ht[:, blk * 512:(blk + 1) * 512], start=True, stop=True).then_inc(up_done, 1)
                    else:
                        pe.wait_ge(act_done, K * (blk + 1))
                        if blk:
                            pe.wait_ge(next_ready, blk)
                        for t in range(4):
                            for j in range(K):
                                mm = pe.matmul(ps_down[:, t, :], act[:, blk % 2, j, t * P:(t + 1) * P],
                                               tb["l0_sh_down"][:, j, :], start=(j == 0), stop=(j == K - 1))
                        mm.then_inc(down_done, 1)

                for r in range(SCORE_BITS):
                    pe.wait_ge(counted, r + 1)
                    pe.matmul(ps_count[:, 0:1], tb["same_block"][:], part_count[:], start=True,
                              stop=True).then_inc(totalled, 1)
                    if r < len(rounds):
                        shared(*rounds[r])
                pe.wait_ge(counted, SCORE_BITS + 1)
                pe.matmul(ps_count[:, 0:1], tb["same_block"][:], part_count[:], start=True,
                          stop=True).then_inc(totalled, 1)
                for j in range(2):
                    pe.wait_ge(counted, SCORE_BITS + 2 + j)
                    pe.matmul(ps_count[:, 1 + j:2 + j], tb["earlier_segment"][:], part_sum[:, j:j + 1],
                              start=True, stop=True).then_inc(totalled, 1)
                for j in range(2):
                    pe.transpose(ps_turn[:, 2 + j, :], score[:, j * P:(j + 1) * P], core.ident[:])
                pe.wait_ge(counted, SCORE_BITS + 4)
                for j in range(2):
                    mm = pe.transpose(ps_turn[:, j, :], slot[:, j * P:(j + 1) * P], core.ident[:])
                mm.then_inc(turned, 1)

            @block.scalar
            def _(act_e):
                nc.scalar.preload_act_table_set("sigmoid_and_others")
                act_e.wait_ge(scores_summed, 1)
                nc.scalar.activation(score[:], ps_score[:, 0:SEGLEN], ACT.Sigmoid).then_inc(score_ready, 1)
                nc.scalar.preload_act_table_set("silu_and_others")
                for n in range(BLK * K):
                    act_e.wait_ge(gate_done, n + 1)
                    if n >= 2:
                        act_e.wait_ge(act_done, n - 1)
                    nc.scalar.activation(silu[:, n % 2, :], ps_gu[:, n % 2, 0, :], ACT.Silu).then_inc(silu_done, 1)

            @block.vector
            def _(dve):
                chain = Serial(dve, chain_sem)
                chain.mark(nc.vector.memset(ones[:], 1.0))
                chain.mark(nc.vector.memset(least[:], 0))
                chain.mark(nc.vector.tensor_copy(cand[:, 0:1], tb["bit_masks"][:, 0:1]))
                chain.settle()
                dve.wait_ge(score_ready, 1)

                def shared(what, blk, k):
                    n = blk * K + k
                    if what == "up":
                        dve.wait_ge(silu_done, n + 1)
                        dve.wait_ge(up_done, n + 1)
                        if blk >= 2:
                            dve.wait_ge(down_done, blk - 1)
                        nc.vector.tensor_tensor(act[:, blk % 2, k, :], silu[:, n % 2, :], ps_gu[:, n % 2, 1, :],
                                                ALU.mult).then_inc(act_done, 1)
                    elif what == "down":
                        dve.wait_ge(down_done, blk + 1)
                        nc.vector.scalar_tensor_tensor(
                            out=x_next[:, 4 * blk:4 * blk + 4, :], in0=ps_down[:], scalar=0.5,
                            in1=core.x[:, 4 * blk:4 * blk + 4, :], op0=ALU.mult, op1=ALU.add).then_inc(next_ready, 1)

                for r in range(SCORE_BITS):
                    now, nxt = r % 2, (r + 1) % 2
                    nc.vector.tensor_scalar(over[:], score[:], cand[:, now:now + 1].bitcast(F32), None, ALU.is_ge,
                                            ALU.add, accum_out=part_count[:]).then_inc(counted, 1)
                    if 1 <= r <= len(rounds):
                        shared(*rounds[r - 1])
                    dve.wait_ge(totalled, r + 1)
                    chain.step(nc.vector.tensor_scalar(kept_bit[:], ps_count[:, 0:1], float(CAP),
                                                       tb["bit_values"][:, r:r + 1], ALU.is_ge, ALU.mult))
                    if r + 1 < SCORE_BITS:
                        chain.mark(nc.vector.scalar_tensor_tensor(
                            out=cand[:, nxt:nxt + 1], in0=kept_bit[:], scalar=tb["bit_masks"][:, r + 1:r + 2],
                            in1=least[:, now:now + 1], op0=ALU.bitwise_or, op1=ALU.bitwise_or))
                    chain.mark(nc.vector.tensor_tensor(least[:, nxt:nxt + 1], least[:, now:now + 1], kept_bit[:],
                                                       ALU.bitwise_or))
                    chain.settle(all_but=1 if r + 1 < SCORE_BITS else 0)
                bound = least[:, SCORE_BITS % 2:SCORE_BITS % 2 + 1].bitcast(F32)

                nc.vector.tensor_scalar(over[:], score[:], bound, None, ALU.is_gt, ALU.add,
                                        accum_out=part_count[:]).then_inc(counted, 1)
                chain.step(nc.vector.tensor_scalar(equal[:], score[:], bound, None, ALU.is_equal))
                chain.step(nc.vector.tensor_tensor_scan(count_eq[:], ones[:], equal[:], 0.0, ALU.mult, ALU.add))
                nc.vector.tensor_copy(part_sum[:, 0:1], count_eq[:, SEGLEN - 1:SEGLEN]).then_inc(counted, 1)
                dve.wait_ge(totalled, SCORE_BITS + 2)
                chain.mark(nc.vector.tensor_scalar(need[:], ps_count[:, 0:1], -1.0, float(CAP), ALU.mult, ALU.add))
                chain.mark(nc.vector.tensor_copy(offset[:, 0:1], ps_count[:, 1:2]))
                chain.settle()
                chain.step(nc.vector.tensor_scalar(fits[:], count_eq[:], offset[:, 0:1], need[:], ALU.add, ALU.is_le))
                chain.step(nc.vector.tensor_tensor(taken_eq[:], equal[:], fits[:], ALU.mult))
                dve.wait_ge(counted, SCORE_BITS + 1)
                chain.step(nc.vector.tensor_tensor(taken[:], taken_eq[:], over[:], ALU.add))
                chain.step(nc.vector.tensor_tensor_scan(count_taken[:], ones[:], taken[:], 0.0, ALU.mult, ALU.add))
                nc.vector.tensor_copy(part_sum[:, 1:2], count_taken[:, SEGLEN - 1:SEGLEN]).then_inc(counted, 1)
                dve.wait_ge(totalled, SCORE_BITS + 3)
                chain.step(nc.vector.tensor_copy(offset[:, 1:2], ps_count[:, 2:3]))
                nc.vector.scalar_tensor_tensor(out=slot[:], in0=count_taken[:], scalar=offset[:, 1:2], in1=taken[:],
                                               op0=ALU.add, op1=ALU.mult).then_inc(counted, 1)
                dve.wait_ge(turned, 1)
                nc.vector.tensor_copy(select[:], ps_turn[:, 0:2, :]).then_inc(chain_sem, 1)
                for j in range(2):
                    nc.vector.tensor_scalar(
                        half_score[:, j:NT:2, :].rearrange("p s e -> p e s"),
                        ps_turn[:, 2 + j, :].rearrange("p (e s) -> p e s", s=SEG),
                        0.5, None, ALU.mult).then_inc(table_ready, 1)

            @block.gpsimd
            def _(pool):
                nc.gpsimd.memset(ones_row16[:], 1.0)
                nc.gpsimd.tensor_copy(bias_parts[:, 0, :], tb["l0_down_bias"][:]).then_inc(bias_split, 1)
                pool.wait_ge(bias_split, 1)
                nc.gpsimd.tensor_tensor(bias_parts[:, 1, :], tb["l0_down_bias"][:], bias_parts[:, 0, :], ALU.subtract)

            @block.sync
            def _(sp):
                rows = dram["rows"].rearrange("(t p) r -> p t r", p=P)
                sp.dma_start(rows[:, :, 0:D], core.h[:]).then_inc(stored, 16)
                if first:
                    load_tables(core, sp, core.later_tables, core.tables_loaded)
                sp.wait_ge(next_ready, BLK)
                sp.dma_start(dram["sum"].rearrange("(t p) d -> p t d", p=P), x_next[:]).then_inc(stored, 16)
                sp.wait_ge(table_ready, 2)
                sp.dma_start(rows[:, :, D:HROW], half_score[:]).then_inc(stored, 16)

DEPTH = 4


def experts0(core, routed):
    nc, dram, tb = core.nc, core.dram, core.tables
    select, ones_row16, bias_parts = routed.select, routed.ones_row, routed.bias_parts
    CH = CAP // P
    with core.stage() as ctx:
        onehot = core.sbuf("onehot", [P, 2, NT, CAP], F16, ctx=ctx)
        ids = core.sbuf("ids", [P, DEPTH, CH], U32, ctx=ctx)
        rows = core.sbuf("rows", [P, DEPTH, CH, HROW], ctx=ctx)
        xt = core.sbuf("xt", [P, 2, CAP], ctx=ctx)
        w_up = core.sbuf("w_up", [P, DEPTH, F0], ctx=ctx)
        w_gate = core.sbuf("w_gate", [P, DEPTH, F0], ctx=ctx)
        w_down = core.sbuf("w_down", [P, DEPTH, F0T, D], ctx=ctx)
        silu = core.sbuf("silu", [P, 2, CAP], ctx=ctx)
        hidden = core.sbuf("hidden", [P, 2, F0T, CAP], ctx=ctx)
        result = core.sbuf("result", [P, DEPTH, CH, D], ctx=ctx)
        ps_ids = core.psum("ps_ids", [P, 512], ctx)
        ps_xt = core.psum("ps_xt", [P, 512], ctx)
        ps_gu = core.psum("ps_gu", [P, 2, 2, 512], ctx)
        ps_down = core.psum("ps_down", [P, 2, 4, P], ctx)

        onehot_ready = core.sem("onehot_ready", ctx)
        ids_summed = core.sem("ids_summed", ctx)
        ids_ready = core.sem("ids_ready", ctx)
        gathered = [core.sem("gathered") for _ in range(DEPTH)]
        scattered = [core.sem("scattered") for _ in range(DEPTH)]
        weights_loaded = [core.sem("weights_loaded", ctx) for _ in range(DEPTH)]
        xt_turned = core.sem("xt_turned", ctx)
        xt_ready = core.sem("xt_ready", ctx)
        gate_done = core.sem("gate_done", ctx)
        up_done = core.sem("up_done", ctx)
        silu_done = core.sem("silu_done", ctx)
        hidden_done = core.sem("hidden_done", ctx)
        down_done = core.sem("down_done", ctx)
        result_done = core.sem("result_done", ctx)
        x_loaded = core.sem("x_loaded", ctx)

        QUADS = E0 // DEPTH

        def later(i):
            return not isinstance(i, int) or i > 0

        def each_expert(engine, body):
            for j in range(DEPTH):
                body(0, j)
            with engine.Fori(1, QUADS - 1) as quad:
                for j in range(DEPTH):
                    body(quad, j)
            for j in range(DEPTH):
                body(QUADS - 1, j)

        def number(quad, j):
            return DEPTH * quad + j, quad + j // DEPTH, j % DEPTH

        def exists(quad, j):
            return not isinstance(quad, int) or DEPTH * quad + j < E0

        def span(at, size=1):
            return slice(at, at + size) if isinstance(at, int) else bass.ds(at, size)

        with nc.Block() as block:

            @block.sync
            def _(sp):
                def load(e, k):
                    for dst, name in ((w_gate[:, k, :], "l0_gate_proj"), (w_up[:, k, :], "l0_up"),
                                      (w_down[:, k].rearrange("p f d -> p (f d)"), "l0_down")):
                        sp.dma_start(dst, dram[name][span(e)].rearrange("o p f -> (o p) f")
                                     ).then_inc(weights_loaded[k], 16)

                for k in range(DEPTH):
                    load(k, k)
                with sp.Fori(1, QUADS) as quad:
                    for k in range(DEPTH):
                        sp.wait_ge(down_done, DEPTH * quad + k - DEPTH + 1)
                        load(DEPTH * quad + k, k)
                for k in range(DEPTH):
                    sp.wait_ge(scattered[k], 32 * QUADS)
                sp.dma_start(core.x[:], dram["sum"].rearrange("(t p) d -> p t d", p=P)).then_inc(x_loaded, 16)
                sp.wait_ge(x_loaded, 16)

            @block.vector
            def _(dve):
                def onehots(quad, j, tiles):
                    e, _, _ = number(quad, j)
                    if tiles[0] == 0:
                        dve.wait_ge(ids_summed, e + 1)
                    for t in tiles:
                        last = nc.vector.tensor_scalar(onehot[:, j % 2, t, :], tb["slot_numbers"][:],
                                                       select_flat[:, span(e * SEG + t % 2 * P + t // 2)],
                                                       None, ALU.is_equal)
                    if tiles[-1] == NT - 1:
                        last.then_inc(onehot_ready, 1)

                def take_ids(quad, j):
                    e, quad, k = number(quad, j)
                    dve.wait_ge(ids_summed, e + 3)
                    if later(quad):
                        dve.wait_ge(scattered[k], 32 * quad)
                    nc.vector.tensor_copy(ids[:, k, :], ps_ids[:, 0:CH]).then_inc(ids_ready, 1)

                select_flat = select[:].rearrange("p j c -> p (j c)")
                dve.sem_inc(hidden_done, 2)
                onehots(0, 0, range(NT))
                onehots(0, 1, range(0, 6))
                take_ids(0, 0)
                onehots(0, 1, range(6, NT))
                onehots(0, 2, range(NT))
                take_ids(0, 1)

                portions = [range(0, 0), range(0, 5), range(5, 7), range(7, NT)]

                def expert(quad, j):
                    e, _, k = number(quad, j)
                    for f in range(F0T):
                        dve.wait_ge(silu_done, e * F0T + f + 1)
                        dve.wait_ge(up_done, e * F0T + f + 1)
                        nc.vector.scalar_tensor_tensor(
                            out=hidden[:, k % 2, f, :], in0=ps_gu[:, f % 2, 1, 0:CAP],
                            scalar=tb["l0_up_bias"][:, span(e * F0T + f)],
                            in1=silu[:, f % 2, :], op0=ALU.add, op1=ALU.mult).then_inc(hidden_done, 1)
                        if f == 1 and exists(quad, j + 2):
                            take_ids(quad, j + 2)
                        if exists(quad, j + 3) and len(portions[f]):
                            onehots(quad, j + 3, portions[f])

                each_expert(dve, expert)

            @block.tensor
            def _(pe):
                def sum_ids(quad, j):
                    e, _, _ = number(quad, j)
                    pe.wait_ge(onehot_ready, e + 1)
                    if j > 0 or later(quad):
                        pe.wait_ge(ids_ready, e)
                    for c in range(CH):
                        for t in range(NT):
                            mm = pe.matmul(ps_ids[:, c:c + 1], onehot[:, j % 2, t, c * P:(c + 1) * P],
                                           tb["token_ids"][:, t:t + 1], start=(t == 0), stop=(t == NT - 1))
                    mm.then_inc(ids_summed, 1)

                def turn(quad, j):
                    e, quad_of, k = number(quad, j)
                    pe.wait_ge(gathered[k], 32 * (quad_of + 1))
                    if j > 0 or later(quad):
                        pe.wait_ge(xt_ready, e)
                    for c in range(CH):
                        mm = pe.transpose(ps_xt[:, c * P:(c + 1) * P], rows[:, k, c, 0:D], core.ident[:])
                    mm.then_inc(xt_turned, 1)

                pe.sem_inc(ids_summed, 2)
                sum_ids(0, 0)
                sum_ids(0, 1)
                turn(0, 0)

                def expert(quad, j):
                    e, _, k = number(quad, j)
                    pe.wait_ge(xt_ready, e + 1)
                    pe.wait_ge(weights_loaded[k], 48 * (quad + 1))
                    for f in range(F0T):
                        pe.wait_ge(hidden_done, e * F0T + f + 1)
                        pe.matmul(ps_gu[:, f % 2, 0, 0:CAP], w_gate[:, k, f * P:(f + 1) * P], xt[:, k % 2, :],
                                  start=True, stop=True).then_inc(gate_done, 1)
                        pe.matmul(ps_gu[:, f % 2, 1, 0:CAP], w_up[:, k, f * P:(f + 1) * P], xt[:, k % 2, :],
                                  start=True, stop=True).then_inc(up_done, 1)
                        if f == 1 and exists(quad, j + 2):
                            sum_ids(quad, j + 2)
                    if exists(quad, j + 1):
                        turn(quad, j + 1)
                    pe.wait_ge(result_done, e + 1)
                    for c in range(CH):
                        for part in range(2):
                            pe.matmul(ps_down[:, k % 2, c, :], ones_row16[:], bias_parts[:, part, span(e * D, D)],
                                      start=(c == 0 and part == 0), stop=False, skip_group_check=True)
                    for f in range(F0T):
                        pe.wait_ge(hidden_done, e * F0T + f + 3)
                        for c in range(CH):
                            mm = pe.matmul(ps_down[:, k % 2, c, :], hidden[:, k % 2, f, c * P:(c + 1) * P],
                                           w_down[:, k, f, :], start=False, stop=(f == F0T - 1),
                                           skip_group_check=True)
                    mm.then_inc(down_done, 1)

                each_expert(pe, expert)

            @block.scalar
            def _(act):
                nc.scalar.preload_act_table_set("silu_and_others")
                act.sem_inc(result_done, 2)

                def take_xt(quad, j):
                    e, _, k = number(quad, j)
                    act.wait_ge(xt_turned, e + 1)
                    nc.scalar.activation(xt[:, k % 2, :], ps_xt[:, 0:CAP], ACT.Copy).then_inc(xt_ready, 1)

                take_xt(0, 0)

                def expert(quad, j):
                    e, _, k = number(quad, j)
                    for f in range(F0T):
                        act.wait_ge(gate_done, e * F0T + f + 1)
                        act.wait_ge(hidden_done, e * F0T + f + 1)
                        nc.scalar.activation(silu[:, f % 2, :], ps_gu[:, f % 2, 0, 0:CAP], ACT.Silu,
                                             bias=tb["l0_gate_bias"][:, span(e * F0T + f)]).then_inc(silu_done, 1)
                    if exists(quad, j + 1):
                        take_xt(quad, j + 1)
                    act.wait_ge(down_done, e + 1)
                    if later(quad):
                        act.wait_ge(scattered[k], 32 * quad)
                    for c in range(CH):
                        last = nc.scalar.activation(result[:, k, c, :], ps_down[:, k % 2, c, :], ACT.Copy,
                                                    scale=rows[:, k, c, span(e + D)])
                    last.then_inc(result_done, 1)

                each_expert(act, expert)

            @block.gpsimd
            def _(pool):
                def gather(quad, j):
                    e, quad, k = number(quad, j)
                    pool.wait_ge(ids_ready, e + 1)
                    if later(quad):
                        pool.wait_ge(result_done, e - 1)
                    pass_waits(core, pool)
                    for c in range(CH):
                        pool.indirect_dma_start(rows[:, k, c, :], None, dram["rows"],
                                                bass.IndirectOffsetOnAxis(ap=ids[:, k, c:c + 1], axis=0)
                                                ).then_inc(gathered[k], 16)

                pool.wait_ge(routed.stored, 48)
                gather(0, 0)
                gather(0, 1)

                def expert(quad, j):
                    e, _, k = number(quad, j)
                    if exists(quad, j + 2):
                        gather(quad, j + 2)
                    pool.wait_ge(result_done, e + 3)
                    if j > 0:
                        pool.wait_ge(scattered[j - 1], 32 * (quad + 1))
                    elif later(quad):
                        pool.wait_ge(scattered[DEPTH - 1], 32 * quad)
                    pass_waits(core, pool)
                    for c in range(CH):
                        pool.indirect_dma_start(dram["sum"], bass.IndirectOffsetOnAxis(ap=ids[:, k, c:c + 1], axis=0),
                                                result[:, k, c, :], None, compute_op=ALU.add
                                                ).then_inc(scattered[k], 16)

                each_expert(pool, expert)


def moe0(core, first=False):
    with core.stage() as ctx:
        routed = Routed(core, ctx)
        layer_norm(core, first)
        if first:
            first_tables_ready(core)
        route_and_shared0(core, routed, first)
        experts0(core, routed)


C = 8
CHUNKS = T // C
W = C * B
LAYERS = 2
L2 = LAYERS * B
SHARE = 5
LAG = 2


LRU_WEIGHTS = ("lru_wi", "lru_wif", "lru_whf", "cell_wi", "cell_wif", "cell_whf", "lru_bhf")


def rms_norm(core, xnt, xnt_hi, xnt_lo, w_hi, w_lo):
    nc, h, tb = core.nc, core.h, core.tables
    with core.stage() as ctx:
        xn = core.sbuf("xn", [P, NT, D], ctx=ctx)
        square = core.sbuf("square", [P, NT, D], ctx=ctx)
        norm2 = core.sbuf("norm2", [P, NT], ctx=ctx)
        norm = core.sbuf("norm", [P, NT], ctx=ctx)
        bounded = core.sbuf("bounded", [P, NT], ctx=ctx)
        inverse = core.sbuf("inverse", [P, NT], ctx=ctx)
        factor = core.sbuf("factor", [P, NT], ctx=ctx)
        gamma1 = core.sbuf("gamma1", [P, 1], ctx=ctx)
        ps_turn = core.psum("ps_turn", [P, 4, 512], ctx)
        HALF = NT // 2
        squared = core.sem("squared", ctx)
        summed = core.sem("summed", ctx)
        norm_ready = core.sem("norm_ready", ctx)
        dve_chain = core.sem("rms_chain", ctx)
        gamma_ready = core.sem("gamma_ready", ctx)
        xn_ready = core.sem("xn_ready", ctx)
        turned = core.sem("turned", ctx)
        w_hi_ready = core.sem("w_hi_ready", ctx)
        xnt_ready = core.sem("xnt_ready", ctx)
        with nc.Block() as block:

            @block.gpsimd
            def _(pool):
                nc.gpsimd.tensor_tensor(square[:, 0:HALF, :], h[:, 0:HALF, :], h[:, 0:HALF, :],
                                        ALU.mult).then_inc(squared, 1)
                for i, name in enumerate(LRU_WEIGHTS):
                    pool.wait_ge(w_hi_ready, i + 1)
                    nc.gpsimd.tensor_tensor(w_lo[name][:], tb[name][:], w_hi[name][:], ALU.subtract)

            @block.scalar
            def _(act):
                for t in range(HALF, NT):
                    nc.scalar.activation(square[:, t, :], h[:, t, :], ACT.Square,
                                         accum_out=norm2[:, t:t + 1]).then_inc(summed, 1)
                for name in LRU_WEIGHTS:
                    nc.scalar.activation(w_hi[name][:], tb[name][:], ACT.Copy).then_inc(w_hi_ready, 1)
                act.wait_ge(summed, 1 + NT - HALF)
                nc.scalar.activation(norm[:], norm2[:], ACT.Sqrt).then_inc(norm_ready, 1)
                act.wait_ge(gamma_ready, 1)
                for g in range(4):
                    act.wait_ge(turned, 4 * g + 4)
                    nc.scalar.activation(xnt[:, g, :], ps_turn[:, g, :], ACT.Copy, scale=gamma1[:]).then_inc(xnt_ready, 1)
                    nc.scalar.activation(xnt_hi[:, g, :], ps_turn[:, g, :], ACT.Copy,
                                         scale=gamma1[:]).then_inc(xnt_ready, 1)

            @block.vector
            def _(dve):
                chain = Serial(dve, dve_chain)
                nc.vector.tensor_scalar(gamma1[:], tb["lru_gamma"][:], 1.0, None, ALU.add).then_inc(gamma_ready, 1)
                dve.wait_ge(squared, 1)
                nc.vector.tensor_reduce(norm2[:, 0:HALF], square[:, 0:HALF, :], AX.X, ALU.add).then_inc(summed, 1)
                dve.wait_ge(norm_ready, 1)
                chain.step(nc.vector.tensor_scalar(bounded[:], norm[:], 1e-12, None, ALU.max))
                chain.step(nc.vector.reciprocal(inverse[:], bounded[:]))
                chain.step(nc.vector.tensor_scalar(factor[:], inverse[:], float(np.sqrt(np.float32(D))), None, ALU.mult))
                for t in range(NT):
                    nc.vector.tensor_scalar(xn[:, t, :], h[:, t, :], factor[:, t:t + 1], None,
                                            ALU.mult).then_inc(xn_ready, 1)
                for g in range(4):
                    dve.wait_ge(xnt_ready, 2 * g + 2)
                    nc.vector.tensor_tensor(xnt_lo[:, g, :], xnt[:, g, :], xnt_hi[:, g, :], ALU.subtract)

            @block.tensor
            def _(pe):
                for t in range(NT):
                    pe.wait_ge(xn_ready, t + 1)
                    pe.transpose(ps_turn[:, t // 4, t % 4 * P:(t % 4 + 1) * P], xn[:, t, :],
                                 core.ident[:]).then_inc(turned, 1)


def recurrence(core, xnt, xnt_hi, xnt_lo, w_hi, w_lo, zt):
    nc, tb = core.nc, core.tables
    with core.stage() as ctx:
        whf_hi, whf_lo = w_hi["lru_whf"], w_lo["lru_whf"]
        ones = core.sbuf("ones", [1, W], F16, ctx=ctx)
        gate = core.sbuf("gate", [P, L2], ctx=ctx)
        u = core.sbuf("u", [P, L2], ctx=ctx)
        u_hi = core.sbuf("u_hi", [P, L2], F16, ctx=ctx)
        u_lo = core.sbuf("u_lo", [P, L2], F16, ctx=ctx)
        gap = core.sbuf("gap", [P, L2], ctx=ctx)
        h_hi = core.sbuf("h_hi", [P, 2, C, L2], F16, ctx=ctx)
        h_lo = core.sbuf("h_lo", [P, 2, C, L2], F16, ctx=ctx)
        states = core.sbuf("states", [P, 2, C, L2], ctx=ctx)
        towards = core.sbuf("towards", [P, 2, C, L2], ctx=ctx)
        tanh_once = core.sbuf("tanh_once", [P, LAYERS, C, B], ctx=ctx)
        cell_once = core.sbuf("cell_once", [P, C, B], ctx=ctx)
        cell_n = core.sbuf("cell_n", [P, C, B], ctx=ctx)
        cell_g = core.sbuf("cell_g", [P, C, B], ctx=ctx)
        cell_gap = core.sbuf("cell_gap", [P, C, B], ctx=ctx)
        cell_u = core.sbuf("cell_u", [P, C, B], ctx=ctx)
        ps_gate = core.psum("ps_gate", [P, 2, 2, 512], ctx)
        ps_n = core.psum("ps_n", [P, LAYERS, 512], ctx)
        ps_cell_n = core.psum("ps_cell_n", [P, 512], ctx)
        ps_cell_g = core.psum("ps_cell_g", [P, 512], ctx)

        begun = core.sem("begun", ctx)
        split_chain = core.sem("split_chain", ctx)
        input_ready = core.sem("input_ready", ctx)
        gate_done = core.sem("gate_done", ctx)
        u_hi_done = core.sem("u_hi_done", ctx)
        u_done = core.sem("u_done", ctx)
        u_lo_done = core.sem("u_lo_done", ctx)
        state_done = core.sem("state_done", ctx)
        gap_done = core.sem("gap_done", ctx)
        h_hi_done = core.sem("h_hi_done", ctx)
        h_lo_done = core.sem("h_lo_done", ctx)
        towards_ready = core.sem("towards_ready", ctx)
        n_done = [core.sem("n_done", ctx) for _ in range(LAYERS)]
        n_read = [core.sem("n_read", ctx) for _ in range(LAYERS)]
        cell_n_done = core.sem("cell_n_done", ctx)
        cell_g_done = core.sem("cell_g_done", ctx)
        cell_n_read = core.sem("cell_n_read", ctx)
        cell_inputs = core.sem("cell_inputs", ctx)
        cell_chain = core.sem("cell_chain", ctx)

        def each_chunk(engine, body):
            def peeled(c):
                runs = [l for l in range(LAYERS) if 0 <= c - l * LAG < CHUNKS]
                nexts = [l for l in range(LAYERS) if 0 <= c + 1 - l * LAG < CHUNKS]
                body(c, c % 2, runs, nexts, c >= LAG + 1)

            both = list(range(LAYERS))
            for c in range(4):
                peeled(c)
            with engine.Fori(1, CHUNKS // 4 - 1) as quad:
                for k in range(4):
                    body(4 * quad + k, k % 2, both, both, True)
            for c in range(CHUNKS - 4, CHUNKS + LAG):
                peeled(c)

        def chunks_begun(c):
            if isinstance(c, int):
                return sum(max(0, min(c + 1 - l * LAG, CHUNKS)) for l in range(LAYERS))
            return LAYERS * c + sum(1 - l * LAG for l in range(LAYERS))

        def columns(layers):
            return slice(layers[0] * B, (layers[-1] + 1) * B)

        with nc.Block() as block:

            @block.tensor
            def _(pe):
                def three(out, name, at, rhs_hi, rhs_lo, start=False, stop=False, done=None):
                    terms = ((w_hi[name], rhs_hi), (w_lo[name], rhs_hi), (w_hi[name], rhs_lo))

                    def term(i):
                        weights, rhs = terms[i]
                        mm = pe.matmul(out, weights[:, at, :] if at is not None else weights[:], rhs,
                                       start=start and i == 0, stop=stop and i == 2, skip_group_check=True)
                        if done is not None and i == 2:
                            mm.then_inc(done, 1)
                    return [lambda i=i: term(i) for i in range(3)]

                def after(wait_for, value, products):
                    if isinstance(value, int) and value == 0:
                        return products
                    return [lambda: (pe.wait_ge(wait_for, value), products[0]())] + products[1:]

                def inputs(l, c, k, half=None):
                    if l == 0:
                        at = (c + 1) * C + (half or 0)
                        if half is None:
                            at = slice(at, at + C) if isinstance(at, int) else bass.ds(at, C)
                        else:
                            at = slice(at, at + C - 1, 2) if isinstance(at, int) else bass.ds(at, C // 2, step=2)
                        return [x[:, :, at].rearrange("p b t -> p t b") for x in (xnt_hi, xnt_lo)]
                    steps = slice(0, C) if half is None else slice(half, C, 2)
                    return [x[:, 1 - k, steps, 0:B] for x in (h_hi, h_lo)]

                def project_n(l, c, k):
                    m = c + 1 - l * LAG
                    return after(n_read[l], m, three(ps_n[:, l, 0:W], "lru_wi", l, *inputs(l, c, k), start=True,
                                                     stop=True, done=n_done[l]))

                def project_gate(l, c, k, half, first):
                    out = ps_gate[:, 1 - k, half, 0:C // 2 * L2].rearrange("p (t c) -> p t c", c=L2)
                    out = out[:, :, l * B:(l + 1) * B]

                    def bias(part):
                        pe.matmul(out, part["lru_bhf"][:, l * P:(l + 1) * P], ones[:, 0:W // 2],
                                  start=False, stop=False, skip_group_check=True)
                    return three(out, "lru_wif", l, *inputs(l, c, k, half), start=first) + [
                        lambda: bias(w_hi), lambda: bias(w_lo)]

                def fillers(c, k, nexts, cell):
                    work = []
                    for l in nexts:
                        work += project_n(l, c, k)
                    if cell:
                        m = c - LAG - 1
                        x_at = m * C
                        x_at = slice(x_at, x_at + C) if isinstance(x_at, int) else bass.ds(x_at, C)
                        seen = [x[:, 1 - k, :, B:L2] for x in (h_hi, h_lo)]
                        before = [x[:, :, x_at].rearrange("p b t -> p t b") for x in (xnt_hi, xnt_lo)]
                        work += after(cell_n_read, m, three(ps_cell_n[:, 0:W], "cell_wi", None, *seen, start=True,
                                                            stop=True, done=cell_n_done))
                        work += after(cell_inputs, m, three(ps_cell_g[:, 0:W], "cell_wif", None, *seen, start=True))
                        work += three(ps_cell_g[:, 0:W], "cell_whf", None, *before, stop=True, done=cell_g_done)
                    for half in range(2):
                        for l in nexts:
                            work += project_gate(l, c, k, half, l == nexts[0])
                    return work

                def before_products(k, s, layers):
                    at = (k, s - 2) if s >= 2 else (1 - k, C + s - 2)
                    for l in layers:
                        out = ps_gate[:, k, s % 2, s // 2 * L2 + l * B:s // 2 * L2 + (l + 1) * B]
                        part = slice(l * B, (l + 1) * B)
                        pe.matmul(out, whf_hi[:, l, :], h_hi[:, at[0], at[1], part], start=False, stop=False, skip_group_check=True)
                        pe.matmul(out, whf_lo[:, l, :], h_hi[:, at[0], at[1], part], start=False, stop=False, skip_group_check=True)
                        pe.matmul(out, whf_hi[:, l, :], h_lo[:, at[0], at[1], part], start=False, stop=False, skip_group_check=True)

                def iteration(c, k, runs, nexts, cell):
                    work = fillers(c, k, nexts, cell)
                    assert len(work) <= SHARE * (C - 1)
                    for s in range(C):
                        at = c * C + s
                        start_of_all = isinstance(at, int) and at == 0
                        out = [ps_gate[:, k, s % 2, s // 2 * L2 + l * B:s // 2 * L2 + (l + 1) * B] for l in range(LAYERS)]
                        if not start_of_all:
                            pe.wait_ge(u_hi_done, at)
                        for l in runs:
                            part = slice(l * B, (l + 1) * B)
                            pe.matmul(out[l], whf_hi[:, l, :], u_hi[:, part], start=False, stop=False, skip_group_check=True)
                            pe.matmul(out[l], whf_lo[:, l, :], u_hi[:, part], start=False, stop=False, skip_group_check=True)
                        if not start_of_all:
                            pe.wait_ge(u_lo_done, at)
                        for l in runs:
                            part = slice(l * B, (l + 1) * B)
                            mm = pe.matmul(out[l], whf_hi[:, l, :], u_lo[:, part], start=False, stop=True, skip_group_check=True)
                        mm.then_inc(input_ready, 1)
                        if s + 1 < C:
                            if not start_of_all:
                                pe.wait_ge(h_lo_done, at)
                            before_products(k, s + 1, runs)
                            for product in work[s * SHARE:(s + 1) * SHARE]:
                                product()
                        elif nexts:
                            pe.wait_ge(h_lo_done, at)
                            before_products(1 - k, 0, nexts)

                pe.wait_ge(begun, 1)
                for product in project_n(0, -1, 1):
                    product()
                for half in range(2):
                    for product in project_gate(0, -1, 1, half, True):
                        product()
                before_products(0, 0, [0])
                each_chunk(pe, iteration)
                pe.wait_ge(h_lo_done, (CHUNKS + LAG) * C)
                for filler in fillers(CHUNKS + LAG, 0, [], True):
                    filler()

            @block.scalar
            def _(act):
                nc.scalar.preload_act_table_set("sigmoid_and_others")

                def double_tanh(l, m, k_to):
                    def first():
                        act.wait_ge(n_done[l], m + 1)
                        nc.scalar.activation(tanh_once[:, l], ps_n[:, l, 0:W].rearrange("p (t b) -> p t b", b=B),
                                             ACT.Tanh).then_inc(n_read[l], 1)

                    def second():
                        act.wait_ge(n_read[l], m + 1)
                        nc.scalar.activation(towards[:, k_to, :, l * B:(l + 1) * B], tanh_once[:, l],
                                             ACT.Tanh).then_inc(towards_ready, 1)
                    return [first, second]

                def cell_work(m):
                    def first():
                        act.wait_ge(cell_n_done, m + 1)
                        if not (isinstance(m, int) and m == 0):
                            act.wait_ge(cell_chain, 3 * m)
                        nc.scalar.activation(cell_once[:], ps_cell_n[:, 0:W].rearrange("p (t b) -> p t b", b=B),
                                             ACT.Tanh).then_inc(cell_n_read, 1)

                    def second():
                        act.wait_ge(cell_n_read, m + 1)
                        nc.scalar.activation(cell_n[:], cell_once[:], ACT.Tanh)

                    def third():
                        act.wait_ge(cell_g_done, m + 1)
                        nc.scalar.activation(cell_g[:], ps_cell_g[:, 0:W].rearrange("p (t b) -> p t b", b=B),
                                             ACT.Sigmoid, bias=tb["cell_bhf"][:]).then_inc(cell_inputs, 1)
                    return [first, second, third]

                def iteration(c, k, runs, nexts, cell):
                    work = [None]
                    for l in nexts:
                        work += double_tanh(l, c + 1 - l * LAG, 1 - k)
                    if cell:
                        work += cell_work(c - LAG - 1)
                    assert len(work) <= C
                    sl = columns(runs)
                    for s in range(C):
                        act.wait_ge(input_ready, c * C + s + 1)
                        nc.scalar.activation(gate[:, sl], ps_gate[:, k, s % 2, s // 2 * L2 + sl.start:s // 2 * L2 + sl.stop],
                                             ACT.Sigmoid).then_inc(gate_done, 1)
                        if s < len(work) and work[s]:
                            work[s]()

                for step in double_tanh(0, 0, 0):
                    step()
                each_chunk(act, iteration)
                for step in cell_work(CHUNKS - 1):
                    step()

            @block.vector
            def _(dve):
                chain = Serial(dve, split_chain)
                chain.mark(nc.vector.memset(ones[:], 1.0))
                chain.mark(nc.vector.memset(u_hi[:], 0.0))
                chain.mark(nc.vector.memset(u_lo[:], 0.0))
                chain.mark(nc.vector.tensor_copy(states[:, 1, C - 1, :], tb["lru_init"][:]))
                for s in (C - 2, C - 1):
                    chain.mark(nc.vector.tensor_copy(h_hi[:, 1, s, :], tb["lru_init"][:]))
                chain.settle()
                for s in (C - 2, C - 1):
                    chain.mark(nc.vector.tensor_tensor(h_lo[:, 1, s, :], tb["lru_init"][:], h_hi[:, 1, s, :],
                                                       ALU.subtract))
                nc.vector.memset(u[:], 0.0).then_inc(begun, 1)
                dve.wait_ge(begun, 1)
                chain.settle()
                dve.wait_ge(towards_ready, 1)
                chain.step(nc.vector.tensor_tensor(gap[:, 0:B], towards[:, 0, 0, 0:B], states[:, 1, C - 1, 0:B],
                                                   ALU.subtract))

                def iteration(c, k, runs, nexts, cell):
                    sl = columns(runs)
                    for s in range(C):
                        at = c * C + s
                        before = states[:, k, s - 1, sl] if s else states[:, 1 - k, C - 1, sl]
                        now = states[:, k, s, sl]
                        if s + 1 == C and nexts:
                            dve.wait_ge(towards_ready, chunks_begun(c + 1))
                        dve.wait_ge(gate_done, at + 1)
                        nc.vector.tensor_tensor(u_hi[:, sl], gate[:, sl], gap[:, sl], ALU.mult).then_inc(u_hi_done, 1)
                        nc.vector.tensor_tensor(u[:, sl], gate[:, sl], gap[:, sl], ALU.mult).then_inc(u_done, 1)
                        dve.wait_ge(u_done, at + 1)
                        nc.vector.tensor_tensor(u_lo[:, sl], u[:, sl], u_hi[:, sl], ALU.subtract).then_inc(u_lo_done, 1)
                        nc.vector.tensor_tensor(now, before, u[:, sl], ALU.add).then_inc(state_done, 1)
                        dve.wait_ge(state_done, at + 1)
                        if s + 1 < C:
                            nc.vector.tensor_tensor(gap[:, sl], towards[:, k, s + 1, sl], now,
                                                    ALU.subtract).then_inc(gap_done, 1)
                        elif nexts:
                            nx = columns(nexts)
                            nc.vector.tensor_tensor(gap[:, nx], towards[:, 1 - k, 0, nx], states[:, k, s, nx],
                                                    ALU.subtract).then_inc(gap_done, 1)
                        else:
                            nc.vector.memset(gap[:, sl], 0.0).then_inc(gap_done, 1)
                        nc.vector.tensor_copy(h_hi[:, k, s, sl], now).then_inc(h_hi_done, 1)
                        dve.wait_ge(h_hi_done, at + 1)
                        nc.vector.tensor_tensor(h_lo[:, k, s, sl], now, h_hi[:, k, s, sl],
                                                ALU.subtract).then_inc(h_lo_done, 1)
                        dve.wait_ge(gap_done, at + 1)

                each_chunk(dve, iteration)

            @block.gpsimd
            def _(pool):
                nc.gpsimd.tensor_tensor(core.x[:], core.x[:], core.h[:], ALU.add)

                def cell(m):
                    at = m * C
                    at = slice(at, at + C) if isinstance(at, int) else bass.ds(at, C)
                    xn_now = xnt[:, :, at].rearrange("p b t -> p t b")
                    pool.wait_ge(cell_inputs, m + 1)
                    nc.gpsimd.tensor_tensor(cell_gap[:], cell_n[:], xn_now, ALU.subtract).then_inc(cell_chain, 1)
                    pool.wait_ge(cell_chain, 3 * m + 1)
                    nc.gpsimd.tensor_tensor(cell_u[:], cell_g[:], cell_gap[:], ALU.mult).then_inc(cell_chain, 1)
                    pool.wait_ge(cell_chain, 3 * m + 2)
                    nc.gpsimd.tensor_tensor(zt[:, :, at].rearrange("p b t -> p t b"), cell_u[:], xn_now,
                                            ALU.add).then_inc(cell_chain, 1)
                    pool.wait_ge(cell_chain, 3 * m + 3)

                with pool.Fori(0, CHUNKS) as m:
                    cell(m)


def turn_and_add(core, zt):
    nc = core.nc
    with core.stage() as ctx:
        ps_turn = core.psum("ps_turn", [P, 4, 4, P], ctx)
        turned = core.sem("turned", ctx)
        with nc.Block() as block:

            @block.tensor
            def _(pe):
                for t in range(NT):
                    pe.transpose(ps_turn[:, t // 4, t % 4, :], zt[:, t // 4, t % 4 * P:(t % 4 + 1) * P],
                                 core.ident[:]).then_inc(turned, 1)

            @block.vector
            def _(dve):
                for g in range(4):
                    dve.wait_ge(turned, 4 * g + 4)
                    nc.vector.tensor_tensor(core.x[:, 4 * g:4 * g + 4, :], ps_turn[:, g], core.x[:, 4 * g:4 * g + 4, :],
                                            ALU.add)


def lru(core):
    with core.stage() as ctx:
        xnt = core.sbuf("xnt", [P, B, T], ctx=ctx)
        zt = core.sbuf("zt", [P, B, T], ctx=ctx)
        xnt_hi = core.sbuf("xnt_hi", [P, B, T], F16, ctx=ctx)
        xnt_lo = core.sbuf("xnt_lo", [P, B, T], F16, ctx=ctx)
        w_hi, w_lo = ({name: core.sbuf(f"{name}_{part}", list(core.tables[name].shape), F16, ctx=ctx)
                       for name in LRU_WEIGHTS} for part in ("hi", "lo"))
        layer_norm(core)
        rms_norm(core, xnt, xnt_hi, xnt_lo, w_hi, w_lo)
        recurrence(core, xnt, xnt_hi, xnt_lo, w_hi, w_lo, zt)
        turn_and_add(core, zt)


E1, F1 = 8, 256
F1T = F1 // P
ETILES = NT + E1
WROW = 3 * F1


def moe1(core, out=None):
    nc, dram, tb = core.nc, core.dram, core.tables
    layer_norm(core)
    x, h, ht = core.x, core.h, core.ht
    K = F1T
    BLK = 4
    TE = NT * E1
    with ExitStack() as stage:
        position = core.sbuf("position", [P, NT], U32, ctx=stage)
        weight_rows = core.sbuf("weight_rows", [P, ETILES], U32, ctx=stage)
        with core.stage() as ctx:
            top = core.sbuf("top", [P, NT], ctx=ctx)
            score = core.sbuf("score", [P, NT], ctx=ctx)
            best = core.sbuf("best", [P, NT, E1], ctx=ctx)
            rank = core.sbuf("rank", [P, NT, E1], ctx=ctx)
            top_rank = core.sbuf("top_rank", [P, NT], ctx=ctx)
            chosen = core.sbuf("chosen", [P, NT, E1], F16, ctx=ctx)
            totals = core.sbuf("totals", [P, E1, NT], ctx=ctx)
            upto = core.sbuf("upto", [P, E1, NT], ctx=ctx)
            before = core.sbuf("before", [P, E1, NT], ctx=ctx)
            tiles_int = core.sbuf("tiles_int", [P, 2, E1], U32, ctx=ctx)
            tiles = core.sbuf("tiles", [P, E1], ctx=ctx)
            ends = core.sbuf("ends", [P, E1], ctx=ctx)
            starts = core.sbuf("starts", [P, E1], ctx=ctx)
            base = core.sbuf("base", [P, E1, NT], ctx=ctx)
            spots = core.sbuf("spots", [P, NT, E1], ctx=ctx)
            own_spot = core.sbuf("own_spot", [P, NT, E1], ctx=ctx)
            ended = core.sbuf("ended", [P, ETILES, E1], ctx=ctx)
            owner = core.sbuf("owner", [P, ETILES], ctx=ctx)
            owner_base = core.sbuf("owner_base", [P, ETILES], ctx=ctx)
            scaled = core.sbuf("scaled", [P, NT, D], ctx=ctx)
            silu = core.sbuf("silu", [P, 2, 512], ctx=ctx)
            act = core.sbuf("act", [P, 2, K, 512], ctx=ctx)
            ps_gu = core.psum("ps_gu", [P, 2, 2, 512], ctx)
            ps_down = core.psum("ps_down", [P, 4, P], ctx)
            ps_logit = core.psum("ps_logit", [P, 512], ctx)
            ps_rank = core.psum("ps_rank", [P, 2, TE], ctx)

            logits_done = core.sem("logits_done", ctx)
            chain_sem = core.sem("chain", ctx)
            top_ready = core.sem("top_ready", ctx)
            score_ready = core.sem("score_ready", ctx)
            chosen_ready = core.sem("chosen_ready", ctx)
            ranked = core.sem("ranked", ctx)
            scaled_ready = core.sem("scaled_ready", ctx)
            position_ready = core.sem("position_ready", ctx)
            sorted_out = core.sem("sorted_out")
            gate_done = core.sem("gate_done", ctx)
            up_done = core.sem("up_done", ctx)
            silu_done = core.sem("silu_done", ctx)
            act_done = core.sem("act_done", ctx)
            down_done = core.sem("down_done", ctx)
            x_updated = core.sem("x_updated", ctx)
            with nc.Block() as block:

                @block.tensor
                def _(pe):
                    for t in range(NT):
                        mm = pe.matmul(ps_logit[:, t * E1:(t + 1) * E1], ht[:, t * P:(t + 1) * P], tb["l1_gate"][:],
                                       start=True, stop=True)
                    mm.then_inc(logits_done, 1)

                    def products(n):
                        blk, k = n // K, n % K
                        if n >= 2:
                            pe.wait_ge(act_done, n - 1)
                        for i, (name, done) in enumerate((("l1_sh_gate", gate_done), ("l1_sh_up", up_done))):
                            pe.matmul(ps_gu[:, n % 2, i, :], tb[name][:, k * P:(k + 1) * P],
                                      ht[:, blk * 512:(blk + 1) * 512], start=True, stop=True).then_inc(done, 1)

                    products(0)
                    pe.wait_ge(chosen_ready, 1)
                    flat = chosen[:].rearrange("p t e -> p (t e)")
                    pe.matmul(ps_rank[:, 0, :], tb["earlier_token"][:], flat, start=True, stop=True)
                    pe.matmul(ps_rank[:, 1, :], tb["ones16"][:], flat, start=True, stop=True).then_inc(ranked, 1)
                    for n in range(1, BLK * K + 1):
                        if n < BLK * K:
                            products(n)
                        if n % K == 0:
                            blk = n // K - 1
                            pe.wait_ge(act_done, K * (blk + 1))
                            if blk:
                                pe.wait_ge(x_updated, blk)
                            for t in range(4):
                                for j in range(K):
                                    mm = pe.matmul(ps_down[:, t, :], act[:, blk % 2, j, t * P:(t + 1) * P],
                                                   tb["l1_sh_down"][:, j, :], start=(j == 0), stop=(j == K - 1))
                            mm.then_inc(down_done, 1)

                @block.scalar
                def _(act_e):
                    nc.scalar.preload_act_table_set("sigmoid_and_others")
                    act_e.wait_ge(top_ready, 1)
                    nc.scalar.activation(score[:], top[:], ACT.Sigmoid).then_inc(score_ready, 1)
                    nc.scalar.preload_act_table_set("silu_and_others")
                    for n in range(BLK * K):
                        act_e.wait_ge(gate_done, n + 1)
                        if n >= 2:
                            act_e.wait_ge(act_done, n - 1)
                        nc.scalar.activation(silu[:, n % 2, :], ps_gu[:, n % 2, 0, :], ACT.Silu).then_inc(silu_done, 1)
                        if n == 0:
                            act_e.wait_ge(score_ready, 1)
                            for t in range(NT):
                                nc.scalar.activation(scaled[:, t, :], h[:, t, :], ACT.Copy,
                                                     scale=score[:, t:t + 1]).then_inc(scaled_ready, 1)

                @block.vector
                def _(dve):
                    chain = Serial(dve, chain_sem)
                    logits = ps_logit[:, 0:TE].rearrange("p (t e) -> p t e", e=E1)

                    def over_experts(a):
                        return a.rearrange("p (t o) -> p t o", o=1).to_broadcast([P, NT, E1])

                    def gated(n):
                        blk, k = n // K, n % K
                        dve.wait_ge(silu_done, n + 1)
                        dve.wait_ge(up_done, n + 1)
                        if blk >= 2:
                            dve.wait_ge(down_done, blk - 1)
                        nc.vector.tensor_tensor(act[:, blk % 2, k, :], silu[:, n % 2, :], ps_gu[:, n % 2, 1, :],
                                                ALU.mult).then_inc(act_done, 1)
                        if k == K - 1:
                            dve.wait_ge(down_done, blk + 1)
                            nc.vector.scalar_tensor_tensor(
                                out=x[:, 4 * blk:4 * blk + 4, :], in0=ps_down[:], scalar=0.5,
                                in1=x[:, 4 * blk:4 * blk + 4, :], op0=ALU.mult, op1=ALU.add).then_inc(x_updated, 1)

                    dve.wait_ge(logits_done, 1)
                    nc.vector.tensor_reduce(top[:], logits, AX.X, ALU.max).then_inc(top_ready, 1)
                    dve.wait_ge(top_ready, 1)
                    chain.step(nc.vector.tensor_tensor(best[:], logits, over_experts(top[:]), ALU.is_equal))
                    chain.step(nc.vector.tensor_tensor(rank[:], best[:], tb["expert_ranks"][:], ALU.mult))
                    chain.step(nc.vector.tensor_reduce(top_rank[:], rank[:], AX.X, ALU.max))
                    nc.vector.tensor_tensor(chosen[:], rank[:], over_experts(top_rank[:]),
                                            ALU.is_equal).then_inc(chosen_ready, 1)
                    gated(0)
                    dve.wait_ge(ranked, 1)
                    by_expert = ps_rank[:, 1, :].rearrange("p (t e) -> p e t", e=E1)
                    chain.step(nc.vector.tensor_copy(totals[:], by_expert))
                    chain.step(nc.vector.tensor_tensor_scan(
                        upto[:].rearrange("p e t -> p (e t)"), tb["same_expert"][:],
                        totals[:].rearrange("p e t -> p (e t)"), 0.0, ALU.mult, ALU.add))
                    chain.mark(nc.vector.tensor_tensor(before[:], upto[:], totals[:], ALU.subtract))
                    chain.step(nc.vector.tensor_scalar(tiles_int[:, 0, :], upto[:, :, NT - 1], float(P - 1), None, ALU.add))
                    chain.step(nc.vector.tensor_scalar(tiles_int[:, 1, :], tiles_int[:, 0, :], 7, None,
                                                       ALU.logical_shift_right))
                    chain.step(nc.vector.tensor_copy(tiles[:], tiles_int[:, 1, :]))
                    chain.step(nc.vector.tensor_tensor_scan(ends[:], tb["ones8"][:], tiles[:], 0.0, ALU.mult, ALU.add))
                    chain.step(nc.vector.tensor_tensor(starts[:], ends[:], tiles[:], ALU.subtract))
                    chain.step(nc.vector.scalar_tensor_tensor(
                        out=base[:], in0=starts[:].rearrange("p (e o) -> p e o", o=1).to_broadcast([P, E1, NT]),
                        scalar=float(P), in1=before[:], op0=ALU.mult, op1=ALU.add))
                    chain.step(nc.vector.tensor_tensor(spots[:], ps_rank[:, 0, :].rearrange("p (t e) -> p t e", e=E1),
                                                       base[:].rearrange("p e t -> p t e"), ALU.add))
                    dve.wait_ge(chosen_ready, 1)
                    chain.step(nc.vector.tensor_tensor(own_spot[:], spots[:], chosen[:], ALU.mult))
                    chain.mark(nc.vector.tensor_reduce(top_rank[:], own_spot[:], AX.X, ALU.add))
                    chain.step(nc.vector.tensor_tensor(
                        ended[:], ends[:].rearrange("p (o e) -> p o e", o=1).to_broadcast([P, ETILES, E1]),
                        tb["tile_numbers"][:], ALU.is_le))
                    nc.vector.tensor_copy(position[:], top_rank[:]).then_inc(position_ready, 1)
                    chain.step(nc.vector.tensor_reduce(owner[:], ended[:], AX.X, ALU.add))
                    chain.step(nc.vector.tensor_scalar(owner_base[:], owner[:], float(E1 - 1), float(P), ALU.min, ALU.mult))
                    nc.vector.tensor_scalar(weight_rows[:], owner_base[:], tb["partition"][:], None, ALU.add)
                    for n in range(1, BLK * K):
                        gated(n)

                @block.gpsimd
                def _(pool):
                    pool.wait_ge(position_ready, 1)
                    for t in range(NT):
                        pool.wait_ge(scaled_ready, t + 1)
                        pool.indirect_dma_start(dram["sorted"], bass.IndirectOffsetOnAxis(ap=position[:, t:t + 1], axis=0),
                                                scaled[:, t, :], None).then_inc(sorted_out, 16)
                    pool.wait_ge(sorted_out, 16 * NT)

        with core.stage() as ctx:
            rows = core.sbuf("rows", [P, DEPTH, D], ctx=ctx)
            w = core.sbuf("w", [P, DEPTH, WROW], ctx=ctx)
            w_index = core.sbuf("w_index", [P, DEPTH], U32, ctx=ctx)
            xt = core.sbuf("xt", [P, 2, P], ctx=ctx)
            silu = core.sbuf("silu", [P, 2, F1T, P], ctx=ctx)
            hidden = core.sbuf("hidden", [P, 2, F1T, P], ctx=ctx)
            y = core.sbuf("y", [P, DEPTH, D], ctx=ctx)
            ps_xt = core.psum("ps_xt", [P, 2, 512], ctx)
            ps_gu = core.psum("ps_gu", [P, 2, 2, 512], ctx)
            ps_y = core.psum("ps_y", [P, 2, 512], ctx)
            rows_loaded = [core.sem("rows_loaded", ctx) for _ in range(DEPTH)]
            w_loaded = [core.sem("w_loaded") for _ in range(DEPTH)]
            y_stored = [core.sem("y_stored", ctx) for _ in range(DEPTH)]
            index_ready = core.sem("index_ready", ctx)
            xt_turned = core.sem("xt_turned", ctx)
            xt_ready = core.sem("xt_ready", ctx)
            gate_done = core.sem("gate_done", ctx)
            up_done = core.sem("up_done", ctx)
            silu_done = core.sem("silu_done", ctx)
            hidden_done = core.sem("hidden_done", ctx)
            down_done = core.sem("down_done", ctx)
            y_ready = core.sem("y_ready", ctx)

            QUADS = ETILES // DEPTH

            def each_tile(engine, body):
                for quad in range(2):
                    for i in range(DEPTH):
                        body(quad, i)
                with engine.Fori(2, QUADS - 1) as quad:
                    for i in range(DEPTH):
                        body(quad, i)
                for i in range(DEPTH):
                    body(QUADS - 1, i)

            def number(quad, i):
                return DEPTH * quad + i, quad + i // DEPTH, i % DEPTH

            def exists(quad, i):
                return not isinstance(quad, int) or 0 <= DEPTH * quad + i < ETILES

            def span(at, size=1):
                return slice(at, at + size) if isinstance(at, int) else bass.ds(at, size)

            with nc.Block() as block:

                @block.sync
                def _(sp):
                    def tile(quad, i):
                        j, _, k = number(quad, i)
                        if exists(quad, i - DEPTH):
                            sp.wait_ge(xt_turned, j - 3)
                        sp.dma_start(rows[:, k, :], dram["sorted"][span(j * P, P), :]).then_inc(rows_loaded[k], 16)

                    each_tile(sp, tile)
                    for k in range(DEPTH):
                        sp.wait_ge(y_stored[k], 16 * QUADS)

                @block.gpsimd
                def _(pool):
                    def tile(quad, i):
                        j, _, k = number(quad, i)
                        pool.wait_ge(index_ready, j + 1)
                        if exists(quad, i - DEPTH):
                            pool.wait_ge(down_done, j - 3)
                        pass_waits(core, pool)
                        pool.indirect_dma_start(w[:, k, :], None, dram["l1_experts"],
                                                bass.IndirectOffsetOnAxis(ap=w_index[:, k:k + 1], axis=0)
                                                ).then_inc(w_loaded[k], 16)

                    each_tile(pool, tile)

                @block.vector
                def _(dve):
                    def index(quad, i):
                        j, quad, k = number(quad, i)
                        if exists(quad, i % DEPTH - DEPTH):
                            dve.wait_ge(w_loaded[k], 16 * quad)
                        nc.vector.tensor_copy(w_index[:, k:k + 1], weight_rows[:, span(j)]).then_inc(index_ready, 1)

                    def take_xt(quad, i):
                        j, _, _ = number(quad, i)
                        dve.wait_ge(xt_turned, j + 1)
                        if exists(quad, i - 2):
                            dve.wait_ge(up_done, j - 1)
                        nc.vector.tensor_copy(xt[:, i % 2, :], ps_xt[:, i % 2, 0:P]).then_inc(xt_ready, 1)

                    def tile(quad, i):
                        j, _, _ = number(quad, i)
                        if exists(quad, i + 1):
                            take_xt(quad, i + 1)
                        if exists(quad, i + 3) and exists(quad, i - 1):
                            index(quad, i + 3)
                        dve.wait_ge(silu_done, j + 1)
                        dve.wait_ge(up_done, j + 1)
                        if exists(quad, i - 2):
                            dve.wait_ge(down_done, j - 1)
                        nc.vector.tensor_tensor(hidden[:, i % 2], silu[:, i % 2],
                                                ps_gu[:, i % 2, 1, 0:F1].rearrange("p (f t) -> p f t", f=F1T),
                                                ALU.mult).then_inc(hidden_done, 1)

                    for i in range(DEPTH):
                        index(0, i)
                    take_xt(0, 0)
                    each_tile(dve, tile)

                @block.tensor
                def _(pe):
                    def turn(quad, i):
                        j, quad_of, k = number(quad, i)
                        pe.wait_ge(rows_loaded[k], 16 * (quad_of + 1))
                        if exists(quad, i - 2):
                            pe.wait_ge(xt_ready, j - 1)
                        pe.transpose(ps_xt[:, i % 2, 0:P], rows[:, k, :], core.ident[:]).then_inc(xt_turned, 1)

                    def down(quad, i):
                        j, _, k = number(quad, i)
                        pe.wait_ge(hidden_done, j + 1)
                        if exists(quad, i - 2):
                            pe.wait_ge(y_ready, j - 1)
                        for f in range(F1T):
                            mm = pe.matmul(ps_y[:, i % 2, 0:D], hidden[:, i % 2, f, :],
                                           w[:, k, 2 * F1 + f * P:2 * F1 + (f + 1) * P],
                                           start=(f == 0), stop=(f == F1T - 1))
                        mm.then_inc(down_done, 1)

                    def tile(quad, i):
                        j, _, k = number(quad, i)
                        pe.wait_ge(xt_ready, j + 1)
                        pe.wait_ge(w_loaded[k], 16 * (quad + 1))
                        if exists(quad, i - 2):
                            pe.wait_ge(hidden_done, j - 1)
                        for part, done in enumerate((gate_done, up_done)):
                            for f in range(F1T):
                                mm = pe.matmul(ps_gu[:, i % 2, part, f * P:(f + 1) * P],
                                               w[:, k, part * F1 + f * P:part * F1 + (f + 1) * P], xt[:, i % 2, :],
                                               start=True, stop=True)
                            mm.then_inc(done, 1)
                        if exists(quad, i + 1):
                            turn(quad, i + 1)
                        if exists(quad, i - 1):
                            down(quad, i - 1)

                    turn(0, 0)
                    each_tile(pe, tile)
                    down(QUADS - 1, DEPTH - 1)

                @block.scalar
                def _(act):
                    nc.scalar.preload_act_table_set("silu_and_others")

                    def give(quad, i):
                        j, quad_of, k = number(quad, i)
                        act.wait_ge(down_done, j + 1)
                        if exists(quad, i - DEPTH):
                            act.wait_ge(y_stored[k], 16 * quad_of)
                        nc.scalar.activation(y[:, k, :], ps_y[:, i % 2, 0:D], ACT.Copy, scale=0.5).then_inc(y_ready, 1)
                        act.wait_ge(y_ready, j + 1)
                        act.dma_start(dram["expert_out"][span(j * P, P), :], y[:, k, :]).then_inc(y_stored[k], 16)

                    def tile(quad, i):
                        j, _, _ = number(quad, i)
                        act.wait_ge(gate_done, j + 1)
                        if exists(quad, i - 2):
                            act.wait_ge(hidden_done, j - 1)
                        nc.scalar.activation(silu[:, i % 2], ps_gu[:, i % 2, 0, 0:F1].rearrange("p (f t) -> p f t", f=F1T),
                                             ACT.Silu).then_inc(silu_done, 1)
                        if exists(quad, i - 1):
                            give(quad, i - 1)

                    each_tile(act, tile)
                    give(QUADS - 1, DEPTH - 1)

        with core.stage() as ctx:
            back = core.sbuf("back", [P, NT, D], ctx=ctx)
            fetched = [core.sem("fetched") for _ in range(4)]
            x_ready = core.sem("x_ready", ctx)
            stored = core.sem("stored", ctx)
            with nc.Block() as block:

                if out is not None:
                    @block.sync
                    def _(sp):
                        for g in range(4):
                            sp.wait_ge(x_ready, g + 1)
                            sp.dma_start(out[512 * g:512 * (g + 1), :].rearrange("(t p) d -> p t d", p=P),
                                         x[:, 4 * g:4 * g + 4, :]).then_inc(stored, 16)
                        sp.wait_ge(stored, 64)

                @block.gpsimd
                def _(pool):
                    for t in range(NT):
                        pool.indirect_dma_start(back[:, t, :], None, dram["expert_out"],
                                                bass.IndirectOffsetOnAxis(ap=position[:, t:t + 1], axis=0)
                                                ).then_inc(fetched[t // 4], 16)

                @block.vector
                def _(dve):
                    for g in range(4):
                        dve.wait_ge(fetched[g], 64)
                        part = slice(4 * g, 4 * g + 4)
                        nc.vector.tensor_tensor(x[:, part, :], x[:, part, :], back[:, part, :],
                                                ALU.add).then_inc(x_ready, 1)


HEADS, HD = 16, 8
GROUPS = 4
QT = T // P
BF16 = mybir.dt.bfloat16
ATT_SCALE = float(HD) ** -0.5
UNITS = [[(0, 3, 0)], [(0, 0, 0), (0, 2, P)], [(1, 3, 0)], [(1, 0, 0), (1, 2, P)], [(0, 1, 0), (1, 1, 2 * P)]]


def project(core, part_hi, part_lo, v_parts, out_bias):
    nc, tb, h_t = core.nc, core.tables, core.ht
    with core.stage() as ctx:
        hb = core.sbuf("hb", [P, T], ctx=ctx)
        turned = core.sbuf("turned", [P, 2, 2, T], ctx=ctx)
        roped = core.sbuf("roped", [P, 2, T], ctx=ctx)
        ps_qk = core.psum("ps_qk", [P, 4, 512], ctx)
        ps_v = core.psum("ps_v", [P, 512], ctx)
        ps_bias = core.psum("ps_bias", [P, 512], ctx)
        bias_done = core.sem("bias_done", ctx)
        hb_ready = core.sem("hb_ready", ctx)
        projected = core.sem("projected", ctx)
        rotated = core.sem("rotated", ctx)
        roped_ready = core.sem("roped_ready", ctx)
        lo_ready = core.sem("lo_ready", ctx)
        v_done = core.sem("v_done", ctx)
        v_split = core.sem("v_split", ctx)
        hi_ready = core.sem("hi_ready", ctx)
        v_hi_ready = core.sem("v_hi_ready", ctx)

        def v_part(b, part):
            one = v_parts[:, bass.ds(b, 1), :, :, part, :]
            return one.rearrange("p o t h c -> p (o t) h c")

        def v_sum():
            return ps_v[:].rearrange("p (t h c) -> p t h c", t=QT, h=HEADS)

        def flat(a):
            return a.rearrange("p o t -> p (o t)")

        with nc.Block() as block:

            @block.tensor
            def _(pe):
                pe.matmul(ps_bias[:, 0:D], tb["att_bv"][:], tb["att_o"][:], start=True, stop=True).then_inc(bias_done, 1)
                pe.sem_inc(v_done, 1)
                with pe.Fori(0, B) as b:
                    for i, name in enumerate(("att_q", "att_q_partner", "att_k", "att_k_partner")):
                        pe.wait_ge(rotated, 4 * b + i + 1)
                        pe.matmul(ps_qk[:, i, :], tb[name][:], h_t[:, bass.ds(b * T, T)], start=True,
                                  stop=True).then_inc(projected, 1)
                    pe.wait_ge(hb_ready, b + 1)
                    pe.wait_ge(v_split, b + 1)
                    for t in range(QT):
                        out = ps_v[:, t * P:(t + 1) * P]
                        mm = pe.matmul(out, hb[:, t * P:(t + 1) * P], tb["att_v"][:], start=True, stop=True)
                    mm.then_inc(v_done, 1)

            @block.scalar
            def _(act):
                with act.Fori(0, B) as b:
                    act.wait_ge(v_done, b + 1)
                    nc.scalar.activation(hb[:], h_t[:, bass.ds(b * T, T)], ACT.Copy).then_inc(hb_ready, 1)
                    for i in range(2):
                        act.wait_ge(roped_ready, 2 * b + i + 3)
                        nc.scalar.activation(flat(part_hi[:, bass.ds(b, 1), i, :]), roped[:, i, :],
                                             ACT.Copy).then_inc(hi_ready, 1)
                        if i == 0:
                            act.wait_ge(v_done, b + 2)
                            nc.scalar.activation(v_part(b, 0), v_sum(), ACT.Copy).then_inc(v_hi_ready, 1)

            @block.vector
            def _(dve):
                dve.wait_ge(bias_done, 1)
                nc.vector.tensor_tensor(out_bias[:], ps_bias[:, 0:D], tb["att_bo"][:], ALU.add)
                dve.sem_inc(rotated, 4)
                dve.sem_inc(v_split, 1)
                dve.sem_inc(lo_ready, 2)
                with dve.Fori(0, B) as b:
                    for i in range(2):
                        dve.wait_ge(roped_ready, 2 * b + i + 1)
                        for j in range(2):
                            dve.wait_ge(projected, 4 * b + 2 * i + j + 1)
                            nc.vector.scalar_tensor_tensor(
                                out=turned[:, i, j, :], in0=ps_qk[:, 2 * i + j, :],
                                scalar=tb["att_bias"][:, 2 * i + j:2 * i + j + 1],
                                in1=tb[f"rope_{('cos', 'sin')[j]}_{'qk'[i]}"][:], op0=ALU.add, op1=ALU.mult).then_inc(rotated, 1)
                    for i in range(2):
                        dve.wait_ge(hi_ready, 2 * b + i + 1)
                        nc.vector.tensor_tensor(flat(part_lo[:, bass.ds(b, 1), i, :]), roped[:, i, :],
                                                flat(part_hi[:, bass.ds(b, 1), i, :]), ALU.subtract).then_inc(lo_ready, 1)
                        if i == 0:
                            dve.wait_ge(v_hi_ready, b + 1)
                            nc.vector.tensor_tensor(v_part(b, 1), v_sum(), v_part(b, 0),
                                                    ALU.subtract).then_inc(v_split, 1)

            @block.gpsimd
            def _(pool):
                pool.sem_inc(roped_ready, 2)
                with pool.Fori(0, B) as b:
                    for i in range(2):
                        pool.wait_ge(rotated, 4 * b + 2 * i + 6)
                        pool.wait_ge(lo_ready, 2 * b + i + 1)
                        nc.gpsimd.tensor_tensor(roped[:, i, :], turned[:, i, 0, :], turned[:, i, 1, :],
                                                ALU.add).then_inc(roped_ready, 1)


def heads(core, part_hi, part_lo, v_parts, out_bias, y):
    nc, tb = core.nc, core.tables
    with core.stage() as ctx:
        spread = core.sbuf("spread", [P, 2, GROUPS, T], F16, ctx=ctx)
        least = core.sbuf("least", [P, 3, 2], ctx=ctx)
        total = core.sbuf("total", [P, QT, HEADS], ctx=ctx)
        v_now = core.sbuf("v_now", [P, QT, HEADS, 2, HD], F16, ctx=ctx)
        y_sum = core.sbuf("y_sum", [P, QT * HEADS, HD], ctx=ctx)
        y_both = core.sbuf("y_both", [P, QT * HEADS, HD], ctx=ctx)
        inverse = core.sbuf("inverse", [P, QT, HEADS], ctx=ctx)
        prob = core.sbuf("prob", [P, 3, 512], ctx=ctx)
        pt_hi = core.sbuf("pt_hi", [P, 3, 512], F16, ctx=ctx)
        pt_lo = core.sbuf("pt_lo", [P, 3, 512], F16, ctx=ctx)
        ps_score = core.psum("ps_score", [P, 3, 512], ctx)
        ps_turn = core.psum("ps_turn", [P, 3, 512], ctx)
        ps_y = core.psum("ps_y", [P, 2, 512], ctx)

        spread_done = core.sem("spread_done", ctx)
        spread_ready = [core.sem("spread_ready", ctx) for _ in range(2)]
        scored = core.sem("scored", ctx)
        least_ready = core.sem("least_ready", ctx)
        exped = core.sem("exped", ctx)
        prob_turned = core.sem("prob_turned", ctx)
        hi_ready = core.sem("hi_ready", ctx)
        lo_ready = core.sem("lo_ready", ctx)
        inverted = core.sem("inverted", ctx)
        summed = core.sem("summed", ctx)
        v_ready = core.sem("v_ready", ctx)
        y_half = core.sem("y_half", ctx)
        y_added = core.sem("y_added", ctx)
        y_ready = core.sem("y_ready", ctx)

        PAIRS = HEADS // 2
        NU = PAIRS * len(UNITS)
        SPREADS = 2 * GROUPS
        LATE = 2
        KIND = ("q", "k")

        yb = y[:].rearrange("p t d -> p (t d)")

        def unit(n):
            pair, i = divmod(n, len(UNITS))
            return [(pair // 4 * 8 + pair % 4 + 4 * a, qt, col) for a, qt, col in UNITS[i]]

        def later(b):
            return not isinstance(b, int) or b > 0

        y_products = ps_y[:].rearrange("p k c -> p (k c)").rearrange("p (n e c) -> p n e c", e=2, c=HD)

        def each_sequence(engine, body):
            with engine.Fori(0, B - 1) as b:
                body(b, True)
            body(B - 1, False)

        with nc.Block() as block:

            def spread_taken(engine, b, n):
                engine.wait_ge(spread_ready[n % 2], SPREADS // 2 * b + n // 2 + 1)

            def take_spread(engine, copy, b, parity):
                for n in range(parity, SPREADS, 2):
                    engine.wait_ge(spread_done, SPREADS * b + n + 1)
                    copy(spread[:, n // GROUPS, n % GROUPS, :], ps_score[:, n % 3, :]).then_inc(spread_ready[parity], 1)

            @block.tensor
            def _(pe):
                def spread_heads(b):
                    for n in range(SPREADS):
                        i, g = divmod(n, GROUPS)
                        if n >= 3:
                            spread_taken(pe, b, n - 3)
                        out = ps_score[:, n % 3, :]
                        for part, source in (("hi", part_hi), ("lo", part_lo)):
                            mm = pe.matmul(out, tb[f"spread_{KIND[i]}_{part}"][:, g * P:(g + 1) * P],
                                           source[:, bass.ds(b, 1), i, :].rearrange("p o t -> p (o t)"),
                                           start=(part == "hi"), stop=(part == "lo"))
                        mm.then_inc(spread_done, 1)

                def scores(b, n):
                    if n >= 3:
                        pe.wait_ge(exped, NU * b + n - 2)
                    for head, qt, col in unit(n):
                        g, row = head // 4, head % 4 * 32
                        width = (qt + 1) * P
                        pe.matmul(ps_score[:, n % 3, col:col + width],
                                  spread[row:row + 32, 0, g, qt * P:(qt + 1) * P],
                                  spread[row:row + 32, 1, g, 0:width], start=True, stop=False,
                                  skip_group_check=True)
                        mm = pe.matmul(ps_score[:, n % 3, col + qt * P:col + width], tb["ident_bf16"][:],
                                       tb["causal"][:], start=False, stop=True, skip_group_check=True)
                    mm.then_inc(scored, 1)

                def turn(b, n):
                    pe.wait_ge(exped, NU * b + n + 1)
                    if n >= 3:
                        pe.wait_ge(lo_ready, NU * b + n - 2)
                    for c in range(4):
                        mm = pe.transpose(ps_turn[:, n % 3, c * P:(c + 1) * P], prob[:, n % 3, c * P:(c + 1) * P],
                                          core.ident[:])
                    mm.then_inc(prob_turned, 1)

                def values(b, n):
                    pe.wait_ge(lo_ready, NU * b + n + 1)
                    for head, qt, col in unit(n):
                        at = (qt % 2 * HEADS + head) * 2 * HD
                        out = ps_y[:, qt // 2, at:at + 2 * HD]
                        for kt in range(qt + 1):
                            at = slice(col + kt * P, col + (kt + 1) * P)
                            v = v_now[:, kt, head].rearrange("p k c -> p (k c)")
                            pe.matmul(out, pt_hi[:, n % 3, at], v, start=(kt == 0), stop=False)
                            mm = pe.matmul(out, pt_lo[:, n % 3, at], v, start=False, stop=(kt == qt))
                    mm.then_inc(summed, 1)

                def sequence(b, has_next):
                    for n in range(SPREADS - 3, SPREADS):
                        spread_taken(pe, b, n)
                    scores(b, 0)
                    scores(b, 1)
                    for n in range(NU):
                        if n + 2 < NU:
                            scores(b, n + 2)
                        turn(b, n)
                        if n == LATE:
                            pe.wait_ge(v_ready, b + 1)
                            pe.wait_ge(y_added, b + 1)
                        if n >= LATE:
                            values(b, n - LATE)
                    for n in range(NU - LATE, NU - 1):
                        values(b, n)
                    if has_next:
                        spread_heads(b + 1)
                    values(b, NU - 1)

                spread_heads(0)
                each_sequence(pe, sequence)

            @block.gpsimd
            def _(pool):
                pool.sem_inc(y_ready, 1)
                with pool.Fori(0, B) as b:
                    pool.wait_ge(inverted, b + 1)
                    pool.wait_ge(y_added, b + 2)
                    nc.gpsimd.tensor_tensor(
                        yb[:, bass.ds(b * QT * D, QT * D)].rearrange("p (n c) -> p n c", c=HD), y_both[:],
                        inverse[:].rearrange("p t (h o) -> p (t h) o", o=1).to_broadcast([P, QT * HEADS, HD]),
                        ALU.mult).then_inc(y_ready, 1)
                nc.gpsimd.tensor_tensor(core.x[:], core.x[:],
                                        out_bias[:].rearrange("p (o d) -> p o d", o=1).to_broadcast([P, NT, D]),
                                        ALU.add)

            @block.scalar
            def _(act):
                nc.scalar.preload_act_table_set("exp_and_others")

                def take_even(b):
                    take_spread(act, lambda out, bank: nc.scalar.activation(out, bank, ACT.Copy), b, 0)

                def sequence(b, has_next):
                    def exps(n):
                        act.wait_ge(least_ready, NU * b + n + 1)
                        if n >= 3:
                            act.wait_ge(prob_turned, NU * b + n - 2)
                        for i, (head, qt, col) in enumerate(unit(n)):
                            last = nc.scalar.activation(prob[:, n % 3, col:col + (qt + 1) * P],
                                                        ps_score[:, n % 3, col:col + (qt + 1) * P], ACT.Exp,
                                                        bias=least[:, n % 3, i:i + 1], scale=-1.0,
                                                        accum_out=total[:, qt, head:head + 1])
                        last.then_inc(exped, 1)

                    def his(n):
                        act.wait_ge(prob_turned, NU * b + n + 1)
                        if n >= 3:
                            act.wait_ge(summed, NU * b + n - 2)
                        nc.scalar.activation(pt_hi[:, n % 3, :], ps_turn[:, n % 3, :], ACT.Copy).then_inc(hi_ready, 1)

                    for n in range(NU):
                        exps(n)
                        if n >= 1:
                            his(n - 1)
                    his(NU - 1)
                    if has_next:
                        take_even(b + 1)
                    act.wait_ge(summed, NU * (b + 1))
                    act.wait_ge(y_added, b + 1)
                    nc.scalar.activation(y_sum[:], y_products[:, :, 0, :], ACT.Copy).then_inc(y_half, 1)

                take_even(0)
                each_sequence(act, sequence)

            @block.vector
            def _(dve):
                dve.sem_inc(y_added, 1)
                def leasts(b, n):
                    dve.wait_ge(scored, NU * b + n + 1)
                    if n >= 3:
                        dve.wait_ge(exped, NU * b + n - 2)
                    for i, (head, qt, col) in enumerate(unit(n)):
                        last = nc.vector.tensor_reduce(least[:, n % 3, i:i + 1],
                                                       ps_score[:, n % 3, col:col + (qt + 1) * P], AX.X, ALU.min)
                    last.then_inc(least_ready, 1)

                def begin(b):
                    take_spread(dve, nc.vector.tensor_copy, b, 1)
                    if later(b):
                        dve.wait_ge(summed, NU * b)
                    one = v_parts[:, bass.ds(b, 1)]
                    nc.vector.tensor_copy(v_now[:].rearrange("p t h k c -> p (t h k c)"),
                                          one.rearrange("p o t h k c -> p (o t h k c)")).then_inc(v_ready, 1)
                    for n in range(2):
                        leasts(b, n)

                def sequence(b, has_next):
                    def los(n):
                        dve.wait_ge(hi_ready, NU * b + n + 1)
                        nc.vector.tensor_tensor(pt_lo[:, n % 3, :], ps_turn[:, n % 3, :], pt_hi[:, n % 3, :],
                                                ALU.subtract).then_inc(lo_ready, 1)

                    for n in range(NU):
                        if n + 2 < NU:
                            leasts(b, n + 2)
                        if n >= 1:
                            los(n - 1)
                    los(NU - 1)
                    dve.wait_ge(exped, NU * (b + 1))
                    dve.wait_ge(y_ready, b + 1)
                    nc.vector.reciprocal(inverse[:], total[:]).then_inc(inverted, 1)
                    if has_next:
                        begin(b + 1)
                    dve.wait_ge(y_half, b + 1)
                    nc.vector.tensor_tensor(y_both[:], y_sum[:], y_products[:, :, 1, :], ALU.add).then_inc(y_added, 1)

                begin(0)
                each_sequence(dve, sequence)


def attention(core):
    nc, tb = core.nc, core.tables
    layer_norm(core)
    x = core.x
    with ExitStack() as stage:
        y = core.sbuf("y", [P, NT, D], ctx=stage)
        with core.stage() as parts:
            part_hi = core.sbuf("part_hi", [P, B, 2, T], F16, ctx=parts)
            part_lo = core.sbuf("part_lo", [P, B, 2, T], F16, ctx=parts)
            v_parts = core.sbuf("v_parts", [P, B, QT, HEADS, 2, HD], F16, ctx=parts)
            out_bias = core.sbuf("out_bias", [P, D], ctx=parts)
            project(core, part_hi, part_lo, v_parts, out_bias)
            heads(core, part_hi, part_lo, v_parts, out_bias, y)

        with core.stage() as ctx:
            yt = core.sbuf("yt", [P, NT, P], ctx=ctx)
            ps_yt = core.psum("ps_yt", [P, 4, 4, P], ctx)
            ps_out = core.psum("ps_out", [P, 4, 4, P], ctx)
            y_turned = core.sem("y_turned", ctx)
            yt_ready = core.sem("yt_ready", ctx)
            out_done = core.sem("out_done", ctx)
            with nc.Block() as block:

                @block.tensor
                def _(pe):
                    for g in range(4):
                        for t in range(4):
                            mm = pe.transpose(ps_yt[:, g, t, :], y[:, 4 * g + t, :], core.ident[:])
                        mm.then_inc(y_turned, 1)
                    for g in range(4):
                        pe.wait_ge(yt_ready, g + 1)
                        for t in range(4):
                            mm = pe.matmul(ps_out[:, g, t, :], yt[:, 4 * g + t, :], tb["att_o"][:], start=True, stop=True)
                        mm.then_inc(out_done, 1)

                @block.scalar
                def _(act):
                    for g in range(4):
                        act.wait_ge(y_turned, g + 1)
                        nc.scalar.activation(yt[:, 4 * g:4 * g + 4, :], ps_yt[:, g], ACT.Copy).then_inc(yt_ready, 1)

                @block.vector
                def _(dve):
                    for g in range(4):
                        dve.wait_ge(out_done, g + 1)
                        nc.vector.tensor_tensor(x[:, 4 * g:4 * g + 4, :], x[:, 4 * g:4 * g + 4, :], ps_out[:, g], ALU.add)
def host_constants():
    p = np.arange(P)
    block = p // SEG
    same = block[:, None] == block[None, :]
    c = {
        "ident": np.eye(P, dtype=np.float32),
        "same_block": same.astype(np.float16),
        "earlier_segment": (same & (p[:, None] < p[None, :])).astype(np.float16),
        "earlier_token": (p[:, None] < p[None, :]).astype(np.float16),
        "ones16": np.ones((P, P), np.float16),
        "slot_numbers": np.tile(np.arange(1, CAP + 1, dtype=np.float16), (P, 1)),
        "token_ids": (p[:, None] + P * np.arange(NT)[None, :]).astype(np.float16),
        "bit_masks": np.tile((1 << np.arange(SCORE_BITS - 1, -1, -1)).astype(np.uint32), (P, 1)),
        "bit_values": np.tile((2.0 ** np.arange(SCORE_BITS - 1, -1, -1)).astype(np.float32), (P, 1)),
        "ones_row": np.ones((1, P), np.float32),
        "expert_ranks": np.broadcast_to(np.arange(E1, 0, -1, dtype=np.float32), (P, NT, E1)),
        "same_expert": np.broadcast_to((np.arange(NT * E1) % NT > 0).astype(np.float32), (P, NT * E1)),
        "ones8": np.ones((P, E1), np.float32),
        "tile_numbers": np.broadcast_to(np.arange(ETILES, dtype=np.float32)[:, None], (P, ETILES, E1)),
        "partition": p.astype(np.float32)[:, None],
    }
    theta = (1.0 / np.float32(10000.0) ** (np.arange(0, HD, 2, dtype=np.float32) / np.float32(HD))).astype(np.float32)
    angle = np.arange(1, T + 1, dtype=np.float32)[None, :] * theta[p % (HD // 2)][:, None]
    sign = np.where(p % HD < HD // 2, -1.0, 1.0).astype(np.float32)[:, None]
    for kind, factor in (("q", -ATT_SCALE), ("k", 1.0)):
        c[f"rope_cos_{kind}"] = (np.float32(factor) * np.cos(angle)).astype(np.float32)
        c[f"rope_sin_{kind}"] = (np.float32(factor) * sign * np.sin(angle)).astype(np.float32)
    bf16 = mybir.dt.np(BF16)
    c["ident_bf16"] = np.eye(P).astype(bf16)
    c["causal"] = np.where(p[:, None] >= p[None, :], 0.0, 1e30).astype(bf16)
    for kind, part, places in (("q", "hi", (0, 1)), ("q", "lo", (2,)), ("k", "hi", (0, 2)), ("k", "lo", (1,))):
        s = np.zeros((P, GROUPS, P), np.float16)
        for head in range(HEADS):
            for i in range(HD):
                for place in places:
                    s[head * HD + i, head // 4, head % 4 * 32 + place * HD + i] = 1
        c[f"spread_{kind}_{part}"] = s.reshape(P, GROUPS * P)
    return c


def lay_out(i):
    def columns(a, parts):
        return a.reshape(-1, parts, P).transpose(2, 0, 1).reshape(P, -1)

    def rows(a):
        return a.reshape(-1, P, a.shape[-1]).transpose(1, 0, 2)

    a = {
        "x": i["L0_attn_x"].reshape(N, D),
        "l0_gate": i["L0_ffn_gate_w"].T,
        "l0_up": i["L0_ffn_up_w"].transpose(0, 2, 1),
        "l0_gate_proj": i["L0_ffn_gw"].transpose(0, 2, 1),
        "l0_down": i["L0_ffn_down_w"].transpose(0, 2, 1).reshape(E0, F0T, P, D).transpose(0, 2, 1, 3).reshape(E0, P, F0T * D),
        "l0_up_bias": columns(i["L0_ffn_up_b"], F0T),
        "l0_gate_bias": columns(i["L0_ffn_gb"], F0T),
        "l0_down_bias": i["L0_ffn_down_b"].reshape(1, E0 * D),
        "l0_sh_gate": i["L0_ffn_sh_gate_w"].T,
        "l0_sh_up": i["L0_ffn_sh_up_w"].T,
        "l0_sh_down": rows(i["L0_ffn_sh_down_w"].T),
        "lru_wi": i["L0_attn_lWi"].transpose(2, 0, 1),
        "lru_wif": i["L0_attn_lWif"].transpose(2, 0, 1),
        "lru_whf": i["L0_attn_lWhf"].transpose(2, 0, 1),
        "cell_wi": i["L0_attn_gWi"].T,
        "cell_wif": i["L0_attn_gWif"].T,
        "cell_whf": i["L0_attn_gWhf"].T,
        "lru_bhf": i["L0_attn_lbhf"].reshape(1, 2 * P),
        "cell_bhf": i["L0_attn_gbhf"].reshape(P, 1),
        "lru_gamma": i["L0_attn_gamma"].reshape(P, 1),
        "l1_gate": i["L1_ffn_gate_w"],
        "l1_sh_gate": i["L1_ffn_sh_gate"],
        "l1_sh_up": i["L1_ffn_sh_up"],
        "l1_sh_down": rows(i["L1_ffn_sh_down"]),
        "l1_experts": np.concatenate([i["L1_ffn_rt_gate"], i["L1_ffn_rt_up"],
                                      i["L1_ffn_rt_down"].reshape(E1, F1T, P, D).transpose(0, 2, 1, 3).reshape(E1, P, F1T * D)],
                                     axis=2).reshape(E1 * P, WROW),
        "lru_init": np.broadcast_to(i["L0_attn_l_init_hidden"].T[:, :, None], (D, 2, B)).reshape(P, 2 * B),
    }
    partner = (np.arange(P) // HD) * HD + (np.arange(P) + HD // 2) % HD
    a["att_q"], a["att_q_partner"] = i["L1_attn_Wq"].T, i["L1_attn_Wq"][partner].T
    a["att_k"], a["att_k_partner"] = i["L1_attn_Wk"].T, i["L1_attn_Wk"][partner].T
    a["att_v"], a["att_o"] = i["L1_attn_Wv"].T, i["L1_attn_Wo"].T
    a["att_bias"] = np.stack([i["L1_attn_bq"], i["L1_attn_bq"][partner],
                              i["L1_attn_bk"], i["L1_attn_bk"][partner]], axis=1)
    a["att_bv"] = np.broadcast_to(i["L1_attn_bv"][:, None], (D, P))
    a["att_bo"] = np.broadcast_to(i["L1_attn_bo"][None, :], (P, D))
    return a


def scratch(nc, dram):
    dram["rows"] = nc.dram_tensor("rows", [N, HROW], F32, kind="Internal").ap()
    dram["sorted"] = nc.dram_tensor("sorted", [ETILES * P, D], F32, kind="Internal").ap()
    dram["expert_out"] = nc.dram_tensor("expert_out", [ETILES * P, D], F32, kind="Internal").ap()
    dram["sum"] = nc.dram_tensor("sum", [N, D], F32, kind="Internal").ap()


def program(nc, dram, out):
    scratch(nc, dram)
    core = Core(nc, dram)
    setup(core)
    moe0(core, first=True)
    tables_ready(core)
    lru(core)
    moe0(core)
    moe1(core)
    attention(core)
    moe1(core, out)


def kernel(**inputs):
    import concourse.bacc as bacc
    from concourse.bass_utils import run_bass_kernel_spmd

    arrays = {name: np.ascontiguousarray(a) for name, a in
              {**lay_out({name: np.asarray(a) for name, a in inputs.items()}), **host_constants()}.items()}
    nc = bacc.Bacc("TRN2", target_bir_lowering=False, num_devices=1)
    dram = {name: nc.dram_tensor(name, a.shape, mybir.dt.from_np(a.dtype), kind="ExternalInput").ap()
            for name, a in arrays.items()}
    out = nc.dram_tensor("out", [N, D], F32, kind="ExternalOutput").ap()
    program(nc, dram, out)
    result = run_bass_kernel_spmd(nc, [arrays], core_ids=[0])
    return result.results[0]["out"].reshape(B, T, D)
```
